# Optimizing a Trainium2 kernel written in Bass

```python
import numpy as np
import jax
import jax.numpy as jnp

def _softmax(x, axis=-1):
    return jax.nn.softmax(x, axis=axis)

def _gelu(x):
    return jax.nn.gelu(x, approximate=True)

def _silu(x):
    return jax.nn.silu(x)

def _sigmoid(x):
    return jax.nn.sigmoid(x)

def _layernorm(x, axis=-1, eps=1e-05):
    m = jnp.mean(x, axis=axis, keepdims=True)
    v = jnp.var(x, axis=axis, keepdims=True)
    return (x - m) / jnp.sqrt(v + eps)

def _scatter_add(tgt, idx, src, axis=0):
    return tgt.at[idx].add(src)

def _segment_sum(src, seg, n):
    return jax.ops.segment_sum(src, seg, n)
kernel_name = 'mk_early_fusion_d2_tok_img768_r4_86d44f'

def setup_inputs(seed: int=0):
    np.random.seed(seed)
    _w = jnp.asarray

    def _rec_inputs():
        import jax
        import jax.numpy as jnp
        _rk = jax.random.key(seed)
        x = -0.000596345 + 1.00056 * jax.random.normal(jax.random.fold_in(_rk, 1), (2, 3, 64, 64), jnp.float32)
        txt = 0.00108355 + 1.41619 * jax.random.normal(jax.random.fold_in(_rk, 2), (2, 77, 192), jnp.float32)
        return (x, txt)
    x, txt = _rec_inputs()

    def _L0_tok_setup():
        import jax, jax.numpy as jnp
        import numpy as np
        P = 4
        key = jax.random.key(seed)
        k1, k2, k3, k4 = jax.random.split(key, 4)
        B, C, H, Wd = (16, 3, 64, 64)
        emb = 192
        num_patches = H // P * (Wd // P)
        in_dim = C * P * P
        x = jax.random.normal(k1, (B, C, H, Wd), dtype=jnp.float32)
        W = jax.random.normal(k2, (emb, in_dim), dtype=jnp.float32) * (1.0 / np.sqrt(in_dim))
        b = jax.random.normal(k3, (emb,), dtype=jnp.float32) * 0.01
        pos = jax.random.normal(k4, (num_patches, emb), dtype=jnp.float32)
        return {'x': x, 'W': W, 'b': b, 'pos': pos}
    _L0_tok_all = _L0_tok_setup()
    _L0_tok_in = {k: v for k, v in _L0_tok_all.items() if k in ('W', 'b', 'pos')}
    del _L0_tok_all

    def _L0_attn_setup():
        import jax, jax.numpy as jnp
        import numpy as np
        B, T, C = (4, 512, 192)
        H, D = (12, 64)
        R = 64
        ROPE_THETA = 10000.0

        def _rope_cos_sin(t, d, dtype):
            inv_freq = 1.0 / ROPE_THETA ** (jnp.arange(0, d, 2, dtype=jnp.float32) / d)
            ang = jnp.arange(t, dtype=jnp.float32)[:, None] * inv_freq[None, :]
            ang = jnp.concatenate([ang, ang], axis=-1)
            return (jnp.cos(ang).astype(dtype), jnp.sin(ang).astype(dtype))

        def _apply_rope(q, cos, sin):
            d2 = q.shape[-1] // 2
            rot = jnp.concatenate([-q[..., d2:], q[..., :d2]], axis=-1)
            return q * cos + rot * sin
        key = jax.random.key(seed)
        ks = jax.random.split(key, 8)
        s = lambda fan_in: 1.0 / np.sqrt(fan_in)
        return {'x': jax.random.normal(ks[0], (B, T, C), jnp.float32), 'Wq': jax.random.normal(ks[1], (C, H * D), jnp.float32) * s(C), 'Wdown': jax.random.normal(ks[2], (C, R), jnp.float32) * s(C), 'ln_g': jnp.ones((R,), jnp.float32), 'ln_b': jnp.zeros((R,), jnp.float32), 'Wup': jax.random.normal(ks[3], (R, 2 * H * D), jnp.float32) * s(R), 'Wo': jax.random.normal(ks[4], (H * D, C), jnp.float32) * s(H * D), 'bo': jnp.zeros((C,), jnp.float32)}
    _L0_attn_all = _L0_attn_setup()
    _L0_attn_in = {k: v for k, v in _L0_attn_all.items() if k in ('Wq', 'Wdown', 'ln_g', 'ln_b', 'Wup', 'Wo', 'bo')}
    del _L0_attn_all

    def _L0_ffn_setup():
        import math
        import jax, jax.numpy as jnp
        import numpy as np
        N_HEAD = 12
        N_EXP = 8
        TOP_K = 2
        TRAIN_CAPACITY = 1.25
        MIN_CAPACITY = 4
        LN_EPS = 1e-05
        NEG_INF = -1e+30

        def _layer_norm(x, w, b):
            mu = jnp.mean(x, axis=-1, keepdims=True)
            var = jnp.var(x, axis=-1, keepdims=True)
            return (x - mu) * jax.lax.rsqrt(var + LN_EPS) * w + b

        def _attention(x, qkv_w, qkv_b, proj_w, proj_b):
            B, T, C = x.shape
            H, D = (N_HEAD, C // N_HEAD)
            qkv = x @ qkv_w + qkv_b
            q, k, v = jnp.split(qkv, 3, axis=-1)
            q = q.reshape(B, T, H, D).transpose(0, 2, 1, 3)
            k = k.reshape(B, T, H, D).transpose(0, 2, 1, 3)
            v = v.reshape(B, T, H, D).transpose(0, 2, 1, 3)
            scores = jnp.einsum('bhqd,bhkd->bhqk', q, k) / math.sqrt(D)
            causal = jnp.tril(jnp.ones((T, T), bool))
            scores = jnp.where(causal, scores, NEG_INF)
            attn = jax.nn.softmax(scores, axis=-1)
            y = jnp.einsum('bhqk,bhkd->bhqd', attn, v)
            y = y.transpose(0, 2, 1, 3).reshape(B, T, C)
            return y @ proj_w + proj_b

        def _moe(x, w_g, fc_w, fc_b, pj_w, pj_b):
            B, T, C = x.shape
            N, E, K = (B * T, N_EXP, TOP_K)
            cap = int(math.floor(K * TRAIN_CAPACITY * N / E))
            cap += cap % 2
            cap = max(cap, MIN_CAPACITY)
            logits = (x @ w_g).reshape(N, E)
            _, topk_idx = jax.lax.top_k(logits, K)
            hot = jax.nn.one_hot(topk_idx, E, dtype=jnp.int32)
            sel = hot.sum(axis=1) > 0
            router_probs = jax.nn.softmax(jnp.where(sel, logits, NEG_INF), axis=-1)
            exp_mask = hot.transpose(1, 0, 2)
            exp_rank = jnp.cumsum(exp_mask.reshape(K * N, E), axis=0) - 1
            exp_rank = exp_rank.reshape(K, N, E)
            exp_mask = exp_mask * (exp_rank < cap).astype(jnp.int32)
            exp_rank = jnp.sum(exp_mask * exp_rank, axis=-1)
            exp_weights = exp_mask.astype(x.dtype) * router_probs[None]
            rank_sc = jax.nn.one_hot(exp_rank, cap, dtype=x.dtype)
            cb_weight = jnp.einsum('kne,knc->nec', exp_weights, rank_sc)
            sec_mask = (cb_weight != 0).astype(x.dtype)
            xf = x.reshape(N, C)
            xb = jnp.einsum('nec,nd->ecd', sec_mask, xf)
            h = jax.nn.gelu(jnp.einsum('ecd,edf->ecf', xb, fc_w) + fc_b, approximate=False)
            out = jnp.einsum('ecf,efd->ecd', h, pj_w) + pj_b
            y = jnp.einsum('nec,ecd->nd', cb_weight, out)
            return y.reshape(B, T, C)
        key = jax.random.key(seed)
        ks = jax.random.split(key, 12)
        B, T, C = (4, 256, 192)
        E, F = (N_EXP, 4 * C)
        s = 0.02
        return {'x': jax.random.normal(ks[0], (B, T, C), jnp.float32), 'ln1_w': jnp.ones((C,), jnp.float32), 'ln1_b': jnp.zeros((C,), jnp.float32), 'ln2_w': jnp.ones((C,), jnp.float32), 'ln2_b': jnp.zeros((C,), jnp.float32), 'attn_qkv_w': jax.random.normal(ks[1], (C, 3 * C), jnp.float32) * s, 'attn_qkv_b': jnp.zeros((3 * C,), jnp.float32), 'attn_proj_w': jax.random.normal(ks[2], (C, C), jnp.float32) * s, 'attn_proj_b': jnp.zeros((C,), jnp.float32), 'w_g': jax.random.normal(ks[3], (C, E), jnp.float32) * s, 'exp_fc_w': jax.random.normal(ks[4], (E, C, F), jnp.float32) * s, 'exp_fc_b': jnp.zeros((E, 1, F), jnp.float32), 'exp_proj_w': jax.random.normal(ks[5], (E, F, C), jnp.float32) * s, 'exp_proj_b': jnp.zeros((E, 1, C), jnp.float32)}
    _L0_ffn_all = _L0_ffn_setup()
    _L0_ffn_in = {k: v for k, v in _L0_ffn_all.items() if k in ('ln1_w', 'ln1_b', 'ln2_w', 'ln2_b', 'attn_qkv_w', 'attn_qkv_b', 'attn_proj_w', 'attn_proj_b', 'w_g', 'exp_fc_w', 'exp_fc_b', 'exp_proj_w', 'exp_proj_b')}
    del _L0_ffn_all

    def _L1_attn_setup():
        import jax, jax.numpy as jnp
        import numpy as np
        B, L, D, H = (4, 256, 192, 12)
        DH = D // H
        key = jax.random.key(seed)
        kx, kk, kq, kv = jax.random.split(key, 4)
        scale = 1.0 / D
        x = jax.random.normal(kx, (B, L, D), dtype=jnp.float32)
        k = jax.random.uniform(kk, (H, D, D), dtype=jnp.float32) * scale
        q = jax.random.uniform(kq, (H, D, D), dtype=jnp.float32) * scale
        v = jax.random.uniform(kv, (H, DH, D), dtype=jnp.float32) * scale
        return {'x': x, 'k': k, 'q': q, 'v': v}
    _L1_attn_all = _L1_attn_setup()
    _L1_attn_in = {k: v for k, v in _L1_attn_all.items() if k in ('k', 'q', 'v')}
    del _L1_attn_all

    def _L1_ffn_setup():
        import jax, jax.numpy as jnp
        import numpy as np
        HIDDEN = 192
        INNER = 128
        EPS = 1e-05
        key = jax.random.key(seed)
        ks = jax.random.split(key, 6)
        B, S = (8, 1024)
        x = jax.random.normal(ks[0], (B, S, HIDDEN), dtype=jnp.float32)
        W1 = jax.random.normal(ks[1], (INNER, HIDDEN), dtype=jnp.float32) * 0.02
        b1 = jnp.zeros((INNER,), dtype=jnp.float32)
        W2 = jax.random.normal(ks[2], (HIDDEN, INNER), dtype=jnp.float32) * 0.02
        b2 = jnp.zeros((HIDDEN,), dtype=jnp.float32)
        bound = 1.0 / np.sqrt(HIDDEN)
        Wo = jax.random.uniform(ks[3], (HIDDEN, HIDDEN), minval=-bound, maxval=bound, dtype=jnp.float32)
        bo = jax.random.uniform(ks[4], (HIDDEN,), minval=-bound, maxval=bound, dtype=jnp.float32)
        gamma = jnp.ones((HIDDEN,), dtype=jnp.float32)
        beta = jnp.zeros((HIDDEN,), dtype=jnp.float32)
        return {'x': x, 'W1': W1, 'b1': b1, 'W2': W2, 'b2': b2, 'Wo': Wo, 'bo': bo, 'gamma': gamma, 'beta': beta}
    _L1_ffn_all = _L1_ffn_setup()
    _L1_ffn_in = {k: v for k, v in _L1_ffn_all.items() if k in ('W1', 'b1', 'W2', 'b2', 'Wo', 'bo', 'gamma', 'beta')}
    del _L1_ffn_all
    return {'x': x, 'txt': txt, 'L0_tok_W': _L0_tok_in['W'], 'L0_tok_b': _L0_tok_in['b'], 'L0_tok_pos': _L0_tok_in['pos'], 'L0_attn_Wq': _L0_attn_in['Wq'], 'L0_attn_Wdown': _L0_attn_in['Wdown'], 'L0_attn_ln_g': _L0_attn_in['ln_g'], 'L0_attn_ln_b': _L0_attn_in['ln_b'], 'L0_attn_Wup': _L0_attn_in['Wup'], 'L0_attn_Wo': _L0_attn_in['Wo'], 'L0_attn_bo': _L0_attn_in['bo'], 'L0_ffn_ln1_w': _L0_ffn_in['ln1_w'], 'L0_ffn_ln1_b': _L0_ffn_in['ln1_b'], 'L0_ffn_ln2_w': _L0_ffn_in['ln2_w'], 'L0_ffn_ln2_b': _L0_ffn_in['ln2_b'], 'L0_ffn_attn_qkv_w': _L0_ffn_in['attn_qkv_w'], 'L0_ffn_attn_qkv_b': _L0_ffn_in['attn_qkv_b'], 'L0_ffn_attn_proj_w': _L0_ffn_in['attn_proj_w'], 'L0_ffn_attn_proj_b': _L0_ffn_in['attn_proj_b'], 'L0_ffn_w_g': _L0_ffn_in['w_g'], 'L0_ffn_exp_fc_w': _L0_ffn_in['exp_fc_w'], 'L0_ffn_exp_fc_b': _L0_ffn_in['exp_fc_b'], 'L0_ffn_exp_proj_w': _L0_ffn_in['exp_proj_w'], 'L0_ffn_exp_proj_b': _L0_ffn_in['exp_proj_b'], 'L1_attn_k': _L1_attn_in['k'], 'L1_attn_q': _L1_attn_in['q'], 'L1_attn_v': _L1_attn_in['v'], 'L1_ffn_W1': _L1_ffn_in['W1'], 'L1_ffn_b1': _L1_ffn_in['b1'], 'L1_ffn_W2': _L1_ffn_in['W2'], 'L1_ffn_b2': _L1_ffn_in['b2'], 'L1_ffn_Wo': _L1_ffn_in['Wo'], 'L1_ffn_bo': _L1_ffn_in['bo'], 'L1_ffn_gamma': _L1_ffn_in['gamma'], 'L1_ffn_beta': _L1_ffn_in['beta']}

def reference(x, txt, L0_tok_W, L0_tok_b, L0_tok_pos, L0_attn_Wq, L0_attn_Wdown, L0_attn_ln_g, L0_attn_ln_b, L0_attn_Wup, L0_attn_Wo, L0_attn_bo, L0_ffn_ln1_w, L0_ffn_ln1_b, L0_ffn_ln2_w, L0_ffn_ln2_b, L0_ffn_attn_qkv_w, L0_ffn_attn_qkv_b, L0_ffn_attn_proj_w, L0_ffn_attn_proj_b, L0_ffn_w_g, L0_ffn_exp_fc_w, L0_ffn_exp_fc_b, L0_ffn_exp_proj_w, L0_ffn_exp_proj_b, L1_attn_k, L1_attn_q, L1_attn_v, L1_ffn_W1, L1_ffn_b1, L1_ffn_W2, L1_ffn_b2, L1_ffn_Wo, L1_ffn_bo, L1_ffn_gamma, L1_ffn_beta):
    import jax
    import jax.numpy as jnp

    def _L0_tok_ref(x, W, b, pos):
        import jax, jax.numpy as jnp
        import numpy as np
        P = 4
        B, C, H, Wd = x.shape
        Hp, Wp = (H // P, Wd // P)
        patches = x.reshape(B, C, Hp, P, Wp, P).transpose(0, 1, 2, 4, 3, 5)
        patches = patches.reshape(B, -1, C * P * P)
        out = jnp.einsum('bnk,ek->bne', patches, W) + b
        out = out + pos[None, :, :]
        return out

    def _L0_attn_ref(x, Wq, Wdown, ln_g, ln_b, Wup, Wo, bo):
        import jax, jax.numpy as jnp
        import numpy as np
        B, T, C = (4, 512, 192)
        H, D = (12, 64)
        R = 64
        ROPE_THETA = 10000.0

        def _rope_cos_sin(t, d, dtype):
            inv_freq = 1.0 / ROPE_THETA ** (jnp.arange(0, d, 2, dtype=jnp.float32) / d)
            ang = jnp.arange(t, dtype=jnp.float32)[:, None] * inv_freq[None, :]
            ang = jnp.concatenate([ang, ang], axis=-1)
            return (jnp.cos(ang).astype(dtype), jnp.sin(ang).astype(dtype))

        def _apply_rope(q, cos, sin):
            d2 = q.shape[-1] // 2
            rot = jnp.concatenate([-q[..., d2:], q[..., :d2]], axis=-1)
            return q * cos + rot * sin
        b, t, c = x.shape
        q = (x @ Wq).reshape(b, t, H, D).transpose(0, 2, 1, 3)
        ckv = x @ Wdown
        mu = jnp.mean(ckv, axis=-1, keepdims=True)
        var = jnp.var(ckv, axis=-1, keepdims=True)
        ckv = (ckv - mu) * jax.lax.rsqrt(var + 1e-05) * ln_g + ln_b
        kv = (ckv @ Wup).reshape(b, t, 2, H, D)
        k = kv[:, :, 0].transpose(0, 2, 1, 3)
        v = kv[:, :, 1].transpose(0, 2, 1, 3)
        cos, sin = _rope_cos_sin(t, D, x.dtype)
        q = _apply_rope(q, cos, sin)
        k = _apply_rope(k, cos, sin)
        wei = jnp.einsum('bhqd,bhkd->bhqk', q, k) * D ** (-0.5)
        causal = jnp.tril(jnp.ones((t, t), bool))
        wei = jnp.where(causal, wei, -jnp.inf)
        wei = jax.nn.softmax(wei, axis=-1)
        out = jnp.einsum('bhqk,bhkd->bhqd', wei, v)
        out = out.transpose(0, 2, 1, 3).reshape(b, t, H * D)
        return out @ Wo + bo

    def _L0_ffn_ref(x, ln1_w, ln1_b, ln2_w, ln2_b, attn_qkv_w, attn_qkv_b, attn_proj_w, attn_proj_b, w_g, exp_fc_w, exp_fc_b, exp_proj_w, exp_proj_b):
        import math
        import jax, jax.numpy as jnp
        import numpy as np
        N_HEAD = 12
        N_EXP = 8
        TOP_K = 2
        TRAIN_CAPACITY = 1.25
        MIN_CAPACITY = 4
        LN_EPS = 1e-05
        NEG_INF = -1e+30

        def _layer_norm(x, w, b):
            mu = jnp.mean(x, axis=-1, keepdims=True)
            var = jnp.var(x, axis=-1, keepdims=True)
            return (x - mu) * jax.lax.rsqrt(var + LN_EPS) * w + b

        def _attention(x, qkv_w, qkv_b, proj_w, proj_b):
            B, T, C = x.shape
            H, D = (N_HEAD, C // N_HEAD)
            qkv = x @ qkv_w + qkv_b
            q, k, v = jnp.split(qkv, 3, axis=-1)
            q = q.reshape(B, T, H, D).transpose(0, 2, 1, 3)
            k = k.reshape(B, T, H, D).transpose(0, 2, 1, 3)
            v = v.reshape(B, T, H, D).transpose(0, 2, 1, 3)
            scores = jnp.einsum('bhqd,bhkd->bhqk', q, k) / math.sqrt(D)
            causal = jnp.tril(jnp.ones((T, T), bool))
            scores = jnp.where(causal, scores, NEG_INF)
            attn = jax.nn.softmax(scores, axis=-1)
            y = jnp.einsum('bhqk,bhkd->bhqd', attn, v)
            y = y.transpose(0, 2, 1, 3).reshape(B, T, C)
            return y @ proj_w + proj_b

        def _moe(x, w_g, fc_w, fc_b, pj_w, pj_b):
            B, T, C = x.shape
            N, E, K = (B * T, N_EXP, TOP_K)
            cap = int(math.floor(K * TRAIN_CAPACITY * N / E))
            cap += cap % 2
            cap = max(cap, MIN_CAPACITY)
            logits = (x @ w_g).reshape(N, E)
            _, topk_idx = jax.lax.top_k(logits, K)
            hot = jax.nn.one_hot(topk_idx, E, dtype=jnp.int32)
            sel = hot.sum(axis=1) > 0
            router_probs = jax.nn.softmax(jnp.where(sel, logits, NEG_INF), axis=-1)
            exp_mask = hot.transpose(1, 0, 2)
            exp_rank = jnp.cumsum(exp_mask.reshape(K * N, E), axis=0) - 1
            exp_rank = exp_rank.reshape(K, N, E)
            exp_mask = exp_mask * (exp_rank < cap).astype(jnp.int32)
            exp_rank = jnp.sum(exp_mask * exp_rank, axis=-1)
            exp_weights = exp_mask.astype(x.dtype) * router_probs[None]
            rank_sc = jax.nn.one_hot(exp_rank, cap, dtype=x.dtype)
            cb_weight = jnp.einsum('kne,knc->nec', exp_weights, rank_sc)
            sec_mask = (cb_weight != 0).astype(x.dtype)
            xf = x.reshape(N, C)
            xb = jnp.einsum('nec,nd->ecd', sec_mask, xf)
            h = jax.nn.gelu(jnp.einsum('ecd,edf->ecf', xb, fc_w) + fc_b, approximate=False)
            out = jnp.einsum('ecf,efd->ecd', h, pj_w) + pj_b
            y = jnp.einsum('nec,ecd->nd', cb_weight, out)
            return y.reshape(B, T, C)
        x = x + _attention(_layer_norm(x, ln1_w, ln1_b), attn_qkv_w, attn_qkv_b, attn_proj_w, attn_proj_b)
        x = x + _moe(_layer_norm(x, ln2_w, ln2_b), w_g, exp_fc_w, exp_fc_b, exp_proj_w, exp_proj_b)
        return x

    def _L1_attn_ref(x, k, q, v):
        import jax, jax.numpy as jnp
        import numpy as np
        B, L, D, H = (4, 256, 192, 12)
        DH = D // H
        K = jnp.einsum('bld,ncd->bncl', x, k)
        Q = jnp.einsum('bld,ncd->bncl', x, q)
        V = jnp.einsum('bld,ncd->bncl', x, v)
        scores = jnp.einsum('bndl,bndm->bnlm', Q, K)
        S = jax.nn.softmax(scores, axis=-1)
        R = jnp.einsum('bnkl,bndl->bndk', S, V)
        R = R.reshape(x.shape[0], D, -1)
        return jnp.transpose(R, (0, 2, 1))

    def _L1_ffn_ref(x, W1, b1, W2, b2, Wo, bo, gamma, beta):
        import jax, jax.numpy as jnp
        import numpy as np
        HIDDEN = 192
        INNER = 128
        EPS = 1e-05
        h = jax.nn.relu(jnp.einsum('bsd,id->bsi', x, W1) + b1)
        pred = jnp.einsum('bsi,di->bsd', h, W2) + b2
        out = jnp.einsum('bsd,ed->bse', pred, Wo) + bo
        mu = jnp.mean(out, axis=-1, keepdims=True)
        var = jnp.mean(jnp.square(out - mu), axis=-1, keepdims=True)
        out = (out - mu) * jax.lax.rsqrt(var + EPS) * gamma + beta
        return out
    h = _L0_tok_ref(x, L0_tok_W, L0_tok_b, L0_tok_pos)
    h = jnp.concatenate([h, txt], axis=1)
    h = h + _L0_attn_ref(_layernorm(h, axis=-1), L0_attn_Wq, L0_attn_Wdown, L0_attn_ln_g, L0_attn_ln_b, L0_attn_Wup, L0_attn_Wo, L0_attn_bo)
    h = h + _L0_ffn_ref(_layernorm(h, axis=-1), L0_ffn_ln1_w, L0_ffn_ln1_b, L0_ffn_ln2_w, L0_ffn_ln2_b, L0_ffn_attn_qkv_w, L0_ffn_attn_qkv_b, L0_ffn_attn_proj_w, L0_ffn_attn_proj_b, L0_ffn_w_g, L0_ffn_exp_fc_w, L0_ffn_exp_fc_b, L0_ffn_exp_proj_w, L0_ffn_exp_proj_b)
    h = h + _L1_attn_ref(_layernorm(h, axis=-1), L1_attn_k, L1_attn_q, L1_attn_v)
    h = h + _L1_ffn_ref(_layernorm(h, axis=-1), L1_ffn_W1, L1_ffn_b1, L1_ffn_W2, L1_ffn_b2, L1_ffn_Wo, L1_ffn_bo, L1_ffn_gamma, L1_ffn_beta)
    return h

_drawn_inputs = setup_inputs


def setup_inputs(seed=0):
    import zlib

    import numpy as np

    out = dict(_drawn_inputs(seed))
    spreads = {'L0_attn_ln_g': (1.0, 0.2),
     'L0_attn_ln_b': (0.0, 0.1),
     'L0_attn_bo': (0.0, 0.1),
     'L0_ffn_ln1_w': (1.0, 0.6),
     'L0_ffn_ln1_b': (0.0, 0.8),
     'L0_ffn_ln2_w': (1.0, 0.6),
     'L0_ffn_ln2_b': (0.0, 0.8),
     'L0_ffn_attn_qkv_b': (0.0, 0.621),
     'L0_ffn_attn_proj_b': (0.0, 0.313),
     'L0_ffn_exp_fc_b': (0.0, 0.8),
     'L0_ffn_exp_proj_b': (0.0, 0.303),
     'L1_ffn_b1': (0.0, 0.318),
     'L1_ffn_b2': (0.0, 0.1),
     'L1_ffn_gamma': (1.0, 0.2),
     'L1_ffn_beta': (0.0, 0.379)}
    factors = {'L0_tok_b': 6.975,
     'L0_ffn_attn_qkv_w': 6.644,
     'L0_ffn_attn_proj_w': 4.078,
     'L1_attn_k': 64.0,
     'L1_attn_q': 64.0,
     'L1_attn_v': 23.573}
    for name, (base, spread) in spreads.items():
        noise = np.random.default_rng([zlib.crc32(name.encode()), seed]).standard_normal(out[name].shape)
        drawn = base * np.exp(spread * noise) if base else spread * noise
        out[name] = jnp.asarray(drawn.astype(out[name].dtype))
    for name, factor in factors.items():
        out[name] = (out[name] * factor).astype(out[name].dtype)
    return out
```

```python
from contextlib import ExitStack

import concourse.bass as bass
from concourse import mybir

F32 = mybir.dt.float32
BF16 = mybir.dt.bfloat16
I32 = mybir.dt.int32
U32 = mybir.dt.uint32
ALU = mybir.AluOpType
ACT = mybir.ActivationFunctionType
AX = mybir.AxisListType

B, T, C = 2, 333, 192
N = B * T
P = 111
CI = T // P
NC_ = B * CI
FC = 96
KC = C // FC
HEADS = 12
PAIRS = HEADS // 2
SPH = B * CI
STEPS = HEADS * SPH
D0 = 64
D1 = 16
GROUPS = HEADS // 4
PATCH = 48
E, CAP = 8, 208
FF = 768
FK = FF // 128
SH = CAP // 2
SLOTS = E * CAP
INNER = 128
EPS = 1e-5

CONST_W = dict(ident=128, dup=128, cos_sin_q=T, cos_sin_k=T, before=P, ones=P, causal=P, expert=E,
               dump=2 * NC_, restart=E * 2 * NC_, eps=1)
COLS_W = dict(lng=1, lnb=1, ln1w=KC, ln1b=KC, qkb=2 * GROUPS, fb1=1, fb2=KC, fcb=E * FK)
ROWS_W = dict(bo0=C, projb=C, vb=C, ln2w=C, ln2b=C, bo1=C, gamma=C, beta=C, pjb=E * C)


def offsets(widths):
    at, out = 0, {}
    for name, w in widths.items():
        out[name] = (at, at + w)
        at += w
    return out, at


CONST_AT, CONST_N = offsets(CONST_W)
COLS_AT, COLS_N = offsets(COLS_W)
ROWS_AT, ROWS_N = offsets(ROWS_W)


def build(nc, a, out):
    ctx = ExitStack()
    with ctx:
        def sb(name, shape, dt=F32):
            return ctx.enter_context(nc.sbuf_tensor(name, shape, dt))

        def sem(name):
            return ctx.enter_context(nc.semaphore(name))

        bank = [ctx.enter_context(nc.psum_tensor(f"bank{i}", [128, 512], F32)) for i in range(8)]
        score_bank, pt_bank, o_bank, proj_bank = bank[0:3], bank[3:5], bank[5], bank[6:8]
        turn_bank = [pt_bank[0], pt_bank[1], proj_bank[0], proj_bank[1]]

        const = sb("consts", [128, CONST_N])
        cols = sb("cols", [128, COLS_N])
        rows = sb("rows", [P, ROWS_N])
        cst = {k: const[:, lo:hi] for k, (lo, hi) in CONST_AT.items()}
        col = {k: cols[:, lo:hi] for k, (lo, hi) in COLS_AT.items()}
        row = {k: rows[:, lo:hi] for k, (lo, hi) in ROWS_AT.items()}
        ident_bf = sb("ident_bf", [P, P], BF16)
        causal_bf = sb("causal_bf", [P, P], BF16)
        before_bf = sb("before_bf", [P, P], BF16)
        ones_bf = sb("ones_bf", [P, P], BF16)
        tok_x = sb("tok_x", [PATCH + 1, N])
        tok_w = sb("tok_w", [PATCH + 1, C])
        base = sb("base", [P, NC_, C])
        h_a = sb("h_a", [P, NC_, C])
        h_b = sb("h_b", [P, NC_, C])
        g_a = sb("g_a", [P, NC_, C])
        xn = sb("xn", [P, NC_, C])
        x_t = sb("x_t", [FC, KC, N])
        bn = sb("bn", [P, NC_, 6])
        mv = sb("mv", [P, NC_, 2])
        std = sb("std", [P, NC_])
        rstd = sb("rstd", [P, NC_])
        wdown = sb("wdown", [FC, KC, D0])
        wup_v = sb("wup_v", [D0, HEADS * D0])
        c_n = sb("c_n", [P, NC_, D0])
        c_t = sb("c_t", [D0, N])
        wq_h = sb("wq_h", [FC, 2, KC, 128])
        wk_h = sb("wk_h", [D0, 2, 128])
        q_t = sb("q_t", [128, 2, N])
        k_cs = sb("k_cs", [128, B, T])
        k_t = sb("k_t", [128, 2, N])
        wo0 = sb("wo0", [128, FK, C])
        wide_a = sb("wide_a", [128, FK * N + 612])
        wide_b = sb("wide_b", [128, FK * N + 612])
        v_0 = wide_a[0:P, 0:NC_ * FF].rearrange("p (c f) -> p c f", c=NC_)
        o_0t = wide_a[:, 0:FK * N].rearrange("p (k n) -> p k n", k=FK)
        o_0 = wide_b[0:P, 0:NC_ * FF].rearrange("p (c f) -> p c f", c=NC_)
        q_1t = wide_b[:, 0:GROUPS * N].rearrange("p (g n) -> p g n", g=GROUPS)
        k_1t = wide_b[:, GROUPS * N:2 * GROUPS * N].rearrange("p (g n) -> p g n", g=GROUPS)
        v_1 = sb("v_1", [P, NC_, C])
        o_1 = sb("o_1", [P, NC_, C])
        probs = sb("probs", [P, 3, T])
        probs_t = sb("probs_t", [P, 2, CI, P])
        nmax = sb("nmax", [P, SPH])
        rsum = sb("rsum", [P, 4 * CI])
        rinv = sb("rinv", [P, 2, CI])
        wqk1 = sb("wqk1", [FC, KC, 2 * GROUPS, 128])
        w1s = sb("w1s", [FC, KC, 2 * C + E])
        fc_w = sb("fc_w", [FC, 2, KC, FF])
        pj_w = sb("pj_w", [128, 2, FK, C])
        lg = sb("lg", [P, NC_, E])
        m8 = sb("m8", [P, NC_, 8])
        i8 = sb("i8", [P, NC_, 8], U32)
        i8f = sb("i8f", [P, 2, NC_])
        oh = sb("oh", [P, 2, NC_, E], BF16)
        tot = sb("tot", [P, E, 2 * NC_])
        run = sb("run", [P, E, 2 * NC_])
        rk = sb("rk", [P, 2 * NC_, E])
        small = {k: sb("r_" + k, [P, 2 * NC_]) for k in ("rank", "keep", "slot", "off", "w")}
        scat = sb("scat", [P, 2 * NC_], I32)
        gath = sb("gath", [P, 2 * NC_], I32)
        ediff = sb("ediff", [P, NC_])
        eexp = sb("eexp", [P, NC_])
        eden = sb("eden", [P, NC_])
        x_slot = sb("x_slot", [SH, 2, 2, C])
        x_slot_t = sb("x_slot_t", [FC, 2, KC, CAP])
        hid = sb("hid", [128, 2, FK, CAP])
        y_slot = sb("y_slot", [SH, 2, 2, C])
        y_tok = sb("y_tok", [P, 2 * NC_, C])
        zero = sb("zero", [SH, C])
        wqk2 = sb("wqk2", [FC, 2, 2, KC, C])
        wv2 = sb("wv2", [FC, KC, C])
        qk_2 = sb("qk_2", [FC, KC, C])
        z_t = wide_a[0:FC, 0:2 * KC * N].rearrange("p (s k n) -> p s k n", s=2, k=KC)
        fw1 = sb("fw1", [FC, KC, INNER])
        fw2 = sb("fw2", [INNER, C])
        fwo = sb("fwo", [FC, KC, C])
        f_h = wide_b[0:INNER, 0:N]
        f_p = x_t

        x_dram = nc.dram_tensor("slot_rows", [SLOTS + 2 * N, C], F32, kind="Internal").ap()
        y_dram = nc.dram_tensor("expert_rows", [SLOTS, C], F32, kind="Internal").ap()

        ld_tok, ld_base, ld_const, ld_cols, ld_rows = (sem(s) for s in (
            "ld_tok", "ld_base", "ld_const", "ld_cols", "ld_rows"))
        ld_w0, ld_wo0, ld_w1, ld_wv2, ld_wf = (sem(s) for s in (
            "ld_w0", "ld_wo0", "ld_w1", "ld_wv2", "ld_wf"))
        ld_head = [sem(f"ld_head{p}") for p in range(2)]
        ld_head2 = [sem(f"ld_head2{p}") for p in range(2)]
        ld_fc = [sem(f"ld_fc{p}") for p in range(2)]
        ld_pj = [sem(f"ld_pj{p}") for p in range(2)]
        cast_done = sem("cast_done")
        tok_mm = sem("tok_mm")
        h_ready = sem("h_ready")
        hb_ready = sem("hb_ready")
        var_ready = sem("var_ready")
        std_ready = sem("std_ready")
        norm_ready = sem("norm_ready")
        turn_mm = sem("turn_mm")
        turn_act = sem("turn_act")
        turn_dve = sem("turn_dve")
        lat_mm = sem("lat_mm")
        lat_ready = sem("lat_ready")
        lat_turn = sem("lat_turn")
        ct_ready = sem("ct_ready")
        v_mm = sem("v_mm")
        v_act = sem("v_act")
        v_dve = sem("v_dve")
        proj_mm = sem("proj_mm")
        proj_dve = sem("proj_dve")
        proj_act = sem("proj_act")
        scores_mm = sem("scores_mm")
        max_ready = sem("max_ready")
        probs_ready = sem("probs_ready")
        probs_turn = sem("probs_turn")
        pt_ready = sem("pt_ready")
        av_mm = sem("av_mm")
        rinv_ready = sem("rinv_ready")
        o_ready = sem("o_ready")
        qk1_mm = sem("qk1_mm")
        q1_ready = sem("q1_ready")
        k1_ready = sem("k1_ready")
        y_mm = sem("y_mm")
        gate_mm = sem("gate_mm")
        oh_ready = sem("oh_ready")
        rank_mm = sem("rank_mm")
        diff_ready = sem("diff_ready")
        exp_ready = sem("exp_ready")
        place_ready = sem("place_ready")
        zero_ready = sem("zero_ready")
        zeroed = sem("zeroed")
        scattered = sem("scattered")
        ld_slot = [sem(f"ld_slot{p}") for p in range(2)]
        slot_turn = sem("slot_turn")
        slot_t_ready = sem("slot_t_ready")
        hid_mm = sem("hid_mm")
        hid_ready = sem("hid_ready")
        out_mm = sem("out_mm")
        ys_ready = sem("ys_ready")
        st_slot = [sem(f"st_slot{p}") for p in range(2)]
        gathered = sem("gathered")
        qk2_done = sem("qk2_done")
        fh_mm = sem("fh_mm")
        fh_ready = sem("fh_ready")
        fp_mm = sem("fp_mm")
        fp_ready = sem("fp_ready")
        dve_step = sem("dve_step")
        stored = sem("stored")

        block = ctx.enter_context(nc.Block())

        def flat(x):
            return x.rearrange("p a b -> p (a b)")

        def width(causal, i):
            return P * (i + 1) if causal else T

        def tok(b, i):
            return slice(b * T + i * P, b * T + (i + 1) * P)

        @block.sync
        def _(sp):
            sp.dma_start(tok_x[:], a["tok_x"]).then_inc(ld_tok, 16)
            sp.dma_start(tok_w[:], a["tok_w"]).then_inc(ld_tok, 16)
            sp.dma_start(base[:], a["base"]).then_inc(ld_base, 16)
            sp.dma_start(const[:], a["const"]).then_inc(ld_const, 16)
            sp.dma_start(wdown[:], a["wdown"]).then_inc(ld_w0, 16)
            sp.dma_start(cols[:], a["cols"]).then_inc(ld_cols, 16)
            sp.dma_start(wup_v[:], a["wup_v"]).then_inc(ld_w0, 16)
            for p in range(2):
                sp.dma_start(wq_h[:, p], a["wq_h"][p]).then_inc(ld_head[p], 16)
                sp.dma_start(wk_h[:, p], a["wk_h"][p]).then_inc(ld_head[p], 16)
            sp.dma_start(rows[:], a["rows"].partition_broadcast(P)).then_inc(ld_rows, 16)
            sp.dma_start(wo0[:], a["wo0"]).then_inc(ld_wo0, 16)
            sp.dma_start(wqk1[:], a["wqk1"]).then_inc(ld_w1, 16)
            sp.dma_start(w1s[:], a["w1s"]).then_inc(ld_w1, 16)
            for p in range(2):
                sp.dma_start(fc_w[:, p], a["fc_w"][p]).then_inc(ld_fc[p], 16)
                sp.dma_start(pj_w[:, p], a["pj_w"][p]).then_inc(ld_pj[p], 16)
                sp.dma_start(wqk2[:, p], a["wqk2"][p]).then_inc(ld_head2[p], 16)
            sp.dma_start(wv2[:], a["wv2"]).then_inc(ld_wv2, 16)
            sp.dma_start(fw1[:], a["fw1"]).then_inc(ld_wf, 16)
            sp.dma_start(fw2[:], a["fw2"]).then_inc(ld_wf, 16)
            sp.dma_start(fwo[:], a["fwo"]).then_inc(ld_wf, 16)
            sp.wait_ge(zero_ready, 1)
            sp.dma_start(x_dram[0:SLOTS, :].rearrange("(s p) c -> p s c", p=SH),
                         zero[:].unsqueeze(1).to_broadcast([SH, 2 * E, C])).then_inc(zeroed, 16)
            with nc.sync.Fori(1, PAIRS) as pair:
                for p in range(2):
                    h = pair * 2 + p
                    sp.wait_ge(proj_mm, h * 6 - 6)
                    sp.dma_start(wq_h[:, p], a["wq_h"][bass.ds(h, 1)].rearrange("o p k n -> (o p) k n")).then_inc(ld_head[p], 16)
                    sp.dma_start(wk_h[:, p], a["wk_h"][bass.ds(h, 1)].rearrange("o p n -> (o p) n")).then_inc(ld_head[p], 16)
            sp.wait_ge(scattered, 16 * 2 * NC_)
            x_rows = x_dram[0:SLOTS, :].rearrange("(e s p) c -> e p s c", e=E, s=2)
            y_rows = y_dram.rearrange("(e s p) c -> e p s c", e=E, s=2)
            for e in range(2):
                sp.dma_start(x_slot[:, e], x_rows[e]).then_inc(ld_slot[e], 16)
            for e in range(E):
                p = e % 2
                if e + 2 < E:
                    sp.wait_ge(hid_mm, FK * (e + 1))
                    sp.dma_start(x_slot[:, p], x_rows[e + 2]).then_inc(ld_slot[p], 16)
                    sp.dma_start(fc_w[:, p], a["fc_w"][e + 2]).then_inc(ld_fc[p], 16)
                    sp.wait_ge(out_mm, 2 * (e + 1))
                    sp.dma_start(pj_w[:, p], a["pj_w"][e + 2]).then_inc(ld_pj[p], 16)
                sp.wait_ge(ys_ready, 2 * (e + 1))
                sp.dma_start(y_rows[e], y_slot[:, p]).then_inc(st_slot[p], 16)
            with nc.sync.Fori(1, PAIRS) as pair:
                for p in range(2):
                    h = pair * 2 + p
                    sp.wait_ge(proj_mm, h * 5 - 5 + 6 * HEADS)
                    sp.dma_start(wqk2[:, p], a["wqk2"][bass.ds(h, 1)].rearrange("o p s k n -> (o p) s k n")).then_inc(ld_head2[p], 16)
            out_v = out.rearrange("b (i p) c -> p (b i) c", p=P)
            for ci in range(NC_):
                sp.wait_ge(h_ready, HR_OUT + ci + 1)
                sp.dma_start(out_v[:, ci], h_b[:, ci]).then_inc(stored, 16)
            sp.wait_ge(stored, 16 * NC_)

        @block.tensor
        def _(pe):
            mm = nc.tensor.matmul
            ident = cst["ident"]
            turned = [0]

            def turn(src, width_, dst_parts, groups, ready):
                for g, (fs, b) in enumerate(groups):
                    if ready is not None:
                        pe.wait_ge(norm_ready, ready + CI * (b + 1))
                    n = turned[0]
                    if g >= 4:
                        pe.wait_ge(turn_dve if n % 2 else turn_act, (n - 4) // 2 + 1)
                    for i in range(CI):
                        last = nc.tensor.transpose(turn_bank[n % 4][0:dst_parts, i * P:(i + 1) * P],
                                                   src[:, b * CI + i, fs], ident[0:P, 0:P])
                    last.then_inc(turn_mm, 1)
                    turned[0] += 1

            def wait_turned():
                pe.wait_ge(turn_act, turned[0] // 2)
                pe.wait_ge(turn_dve, turned[0] // 2)

            def turn_xn(ready):
                turn(xn, FC, FC, [(slice(k * FC, (k + 1) * FC), b) for b in range(B) for k in range(KC)], ready)
                wait_turned()

            def v_banks(lhs, w, per):
                for ci in range(NC_):
                    for k in range(KC):
                        last = mm(score_bank[ci // 2][0:P, (ci % 2) * C:(ci % 2 + 1) * C],
                                  lhs[:, k, ci * P:(ci + 1) * P], w(k), start=(k == 0), stop=(k == KC - 1))
                    if ci % 2:
                        last.then_inc(v_mm, 1)

            def transposes(n, s, causal, wait_n):
                i = s % CI
                pe.wait_ge(probs_ready, wait_n + 1)
                for j in range(width(causal, i) // P):
                    last = nc.tensor.transpose(pt_bank[s % 2][0:P, j * P:(j + 1) * P],
                                               probs[:, s % 3, j * P:(j + 1) * P], ident[0:P, 0:P])
                last.then_inc(probs_turn, 1)

            def av(n, u, s, causal, v, hd, d):
                b, i = divmod(s, CI)
                pe.wait_ge(pt_ready, n + 1)
                if i == 0:
                    pe.wait_ge(o_ready, u + 1)
                cnt = width(causal, i) // P
                for j in range(cnt):
                    last = mm(o_bank[0:P, i * d:(i + 1) * d], probs_t[:, s % 2, j, :],
                              v[:, b * CI + j, hd], start=(j == 0), stop=(j == cnt - 1))
                last.then_inc(av_mm, 1)


            pe.wait_ge(ld_tok, 32)
            for ci in range(NC_):
                mm(score_bank[ci // 2][0:P, (ci % 2) * C:(ci % 2 + 1) * C], tok_x[:, ci * P:(ci + 1) * P],
                   tok_w[:], start=True, stop=True).then_inc(tok_mm, 1)

            pe.wait_ge(ld_const, 16)
            pe.wait_ge(ld_w0, 32)
            turn_xn(0)
            for ci in range(NC_):
                for k in range(KC):
                    last = mm(o_bank[0:P, ci * D0:(ci + 1) * D0], x_t[:, k, ci * P:(ci + 1) * P], wdown[:, k],
                              start=(k == 0), stop=(k == KC - 1))
            last.then_inc(lat_mm, 1)

            def proj0(h, p, piece):
                kind, b = (("q", 0), ("k", 0), ("q", 1), ("d", 0), ("k", 1), ("d", 1))[piece]
                dst = proj_bank[piece % 2][:, 0:T]
                first = isinstance(h, int) and h == 0
                if piece == 0:
                    pe.wait_ge(ld_head[p], head_loads(h, p))
                    if not first:
                        pe.wait_ge(proj_dve, 4 * h)
                elif piece == 1:
                    if not first:
                        pe.wait_ge(proj_act, 2 * h)
                elif piece == 2:
                    pe.wait_ge(proj_dve, 4 * h + 1)
                elif piece == 3:
                    pe.wait_ge(proj_dve, 4 * h + 2)
                elif piece == 4:
                    pe.wait_ge(proj_dve, 4 * h + 3)
                else:
                    pe.wait_ge(proj_dve, 4 * h + 4)
                    pe.wait_ge(proj_act, 2 * h + 1)
                xs = slice(b * T, (b + 1) * T)
                if kind == "q":
                    for k in range(KC):
                        last = mm(dst, wq_h[:, p, k], x_t[:, k, xs], start=(k == 0), stop=(k == KC - 1))
                elif kind == "k":
                    last = mm(dst, wk_h[:, p], c_t[:, xs], start=True, stop=True)
                else:
                    last = mm(dst, cst["dup"], k_cs[:, b], start=True, stop=True)
                last.then_inc(proj_mm, 1)

            def scores0(h, n, p, s):
                b, i = divmod(s, CI)
                if i == 0:
                    pe.wait_ge(proj_dve, 4 * h + (2 if b == 0 else 4))
                    pe.wait_ge(proj_act, 2 * h + b + 1)
                w = P * (i + 1)
                dst = score_bank[s % 3]
                mm(dst[0:P, 0:w], q_t[:, p, tok(b, i)], k_t[:, p, b * T:b * T + w], start=True, stop=False)
                mm(dst[0:P, i * P:w], ident_bf[:], causal_bf[:], start=False, stop=True).then_inc(scores_mm, 1)

            for b in range(B):
                pe.wait_ge(lat_ready, CI * (b + 1))
                for i in range(CI):
                    last = nc.tensor.transpose(pt_bank[b][0:D0, i * P:(i + 1) * P], c_n[:, b * CI + i, :], ident[0:P, 0:P])
                last.then_inc(lat_turn, 1)
            pe.wait_ge(ct_ready, B)
            for m in range(2 * NC_):
                ci, half = divmod(m, 2)
                if m >= 3:
                    pe.wait_ge(v_act if (m - 3) % 2 else v_dve, (m - 3) // 2 + 1)
                mm(score_bank[m % 3][0:P, 0:384], c_t[:, ci * P:(ci + 1) * P], wup_v[:, half * 384:(half + 1) * 384],
                   start=True, stop=True).then_inc(v_mm, 1)
            for piece in range(6):
                proj0(0, 0, piece)
            pe.wait_ge(cast_done, 1)
            pe.wait_ge(v_act, NC_)
            pe.wait_ge(v_dve, NC_)
            for s in range(2):
                scores0(0, s, 0, s)
            pieces = {0: (0, 1), 1: (2, 3), 2: (4,), 3: (5,)}

            def body0(pair, final):
                for p in range(2):
                    h = pair * 2 + p
                    for s in range(SPH):
                        n = h * SPH + s
                        transposes(n, s, True, n)
                        more = not (final and p == 1)
                        if more:
                            for piece in pieces.get(s, ()):
                                proj0(h + 1, 1 - p, piece)
                        if s + 2 < SPH:
                            scores0(h, n + 2, p, s + 2)
                        elif more:
                            scores0(h + 1, n + 2, 1 - p, s + 2 - SPH)
                        av(n, h * B + s // CI, s, True, v_0, head_cols(h, D0), D0)

            with nc.tensor.Fori(0, PAIRS - 1) as pair:
                body0(pair, False)
            body0(PAIRS - 1, True)

            pe.wait_ge(o_ready, 1 + STEPS // CI)
            pe.wait_ge(ld_wo0, 16)
            turn(o_0, 128, 128, [(slice(k * 128, (k + 1) * 128), b) for b in range(B) for k in range(FK)], None)
            wait_turned()
            for ci in range(NC_):
                for k in range(FK):
                    last = mm(score_bank[ci // 2][0:P, (ci % 2) * C:(ci % 2 + 1) * C],
                              o_0t[:, k, ci * P:(ci + 1) * P], wo0[:, k], start=(k == 0), stop=(k == FK - 1))
                last.then_inc(y_mm, 1)

            pe.wait_ge(ld_w1, 32)
            turn_xn(NC_)
            for m in range(2 * 2 * GROUPS):
                blk, b = divmod(m, 2)
                if m >= 4:
                    if m - 4 < 2 * GROUPS:
                        pe.wait_ge(q1_ready, m - 3)
                    else:
                        pe.wait_ge(k1_ready, m - 3 - 2 * GROUPS)
                for k in range(KC):
                    last = mm(turn_bank[m % 4][:, 0:T], wqk1[:, k, blk], x_t[:, k, b * T:(b + 1) * T],
                              start=(k == 0), stop=(k == KC - 1))
                last.then_inc(qk1_mm, 1)
            v_banks(x_t, lambda k: w1s[:, k, 0:C], C)
            pe.wait_ge(q1_ready, 2 * GROUPS)
            pe.wait_ge(k1_ready, 2 * GROUPS)
            pe.wait_ge(v_dve, NC_ + 3)

            def scores1(m):
                h, s = divmod(m, SPH)
                b, i = divmod(s, CI)
                g, at = h // 4, 32 * (h % 4)
                w = P * (i + 1)
                dst = score_bank[s % 3]
                mm(dst[0:P, 0:w], q_1t[at:at + D1, g, tok(b, i)], k_1t[at:at + D1, g, b * T:b * T + w],
                   start=True, stop=False)
                mm(dst[0:P, i * P:w], ident_bf[:], causal_bf[:], start=False, stop=True).then_inc(scores_mm, 1)

            scores1(0)
            scores1(1)
            for m in range(STEPS):
                h, s = divmod(m, SPH)
                transposes(STEPS + m, s, True, STEPS + m)
                if m + 2 < STEPS:
                    scores1(m + 2)
                av(STEPS + m, (STEPS + m) // CI, s, True, v_1, slice(h * D1, (h + 1) * D1), D1)
            pe.wait_ge(o_ready, 1 + 2 * STEPS // CI)
            turn(o_1, FC, FC, [(slice(k * FC, (k + 1) * FC), b) for b in range(B) for k in range(KC)], None)
            wait_turned()
            for ci in range(NC_):
                for k in range(KC):
                    last = mm(score_bank[ci // 2][0:P, (ci % 2) * C:(ci % 2 + 1) * C],
                              x_t[:, k, ci * P:(ci + 1) * P], w1s[:, k, C:2 * C], start=(k == 0), stop=(k == KC - 1))
                last.then_inc(y_mm, 1)

            turn_xn(2 * NC_)
            for ci in range(NC_):
                for k in range(KC):
                    last = mm(o_bank[0:P, ci * E:(ci + 1) * E], x_t[:, k, ci * P:(ci + 1) * P],
                              w1s[:, k, 2 * C:2 * C + E], start=(k == 0), stop=(k == KC - 1))
            last.then_inc(gate_mm, 1)
            pe.wait_ge(oh_ready, 1)
            ohf = oh[:].rearrange("p k c e -> p (k c e)")
            mm(score_bank[0][0:P, 0:2 * NC_ * E], before_bf[:], ohf, start=True, stop=True)
            mm(score_bank[1][0:P, 0:2 * NC_ * E], ones_bf[:], ohf, start=True, stop=True).then_inc(rank_mm, 1)

            def expert_hidden(e):
                p = e % 2
                pe.wait_ge(ld_slot[p], 16 * (e // 2 + 1))
                for k in range(KC):
                    for s in range(2):
                        last = nc.tensor.transpose(
                            pt_bank[p][0:FC, k * CAP + s * SH:k * CAP + (s + 1) * SH],
                            x_slot[:, p, s, k * FC:(k + 1) * FC], ident[0:SH, 0:SH])
                last.then_inc(slot_turn, 1)
                pe.wait_ge(slot_t_ready, e + 1)
                pe.wait_ge(ld_fc[p], 16 * (e // 2 + 1))
                for f in range(FK):
                    n = FK * e + f
                    if n >= 3:
                        pe.wait_ge(hid_ready, n - 2)
                    for k in range(KC):
                        last = mm(score_bank[n % 3][:, 0:CAP], fc_w[:, p, k, f * 128:(f + 1) * 128],
                                  x_slot_t[:, p, k], start=(k == 0), stop=(k == KC - 1))
                    last.then_inc(hid_mm, 1)

            def expert_out(e):
                p = e % 2
                pe.wait_ge(ld_pj[p], 16 * (e // 2 + 1))
                pe.wait_ge(hid_ready, FK * (e + 1))
                for s in range(2):
                    if e >= 1:
                        pe.wait_ge(ys_ready, 2 * e - 1 + s)
                    for f in range(FK):
                        last = mm(proj_bank[s][0:SH, 0:C], hid[:, p, f, s * SH:(s + 1) * SH], pj_w[:, p, f],
                                  start=(f == 0), stop=(f == FK - 1))
                    last.then_inc(out_mm, 1)

            for e in range(E):
                expert_hidden(e)
                if e:
                    expert_out(e - 1)
            expert_out(E - 1)

            turn_xn(3 * NC_)
            pe.wait_ge(ld_wv2, 16)
            v_banks(x_t, lambda k: wv2[:, k], C)

            def proj2(h, p, piece):
                m = 5 * h + piece
                count = 2 * HEADS + m
                dst = proj_bank[(p * 5 + piece) % 2]
                if not (isinstance(h, int) and m < 2):
                    pe.wait_ge(proj_act, count - 1)
                if piece == 0:
                    pe.wait_ge(ld_head2[p], head_loads2(h, p))
                    for d in range(KC):
                        for k in range(KC):
                            last = mm(dst[0:FC, d * C:(d + 1) * C], wqk2[:, p, 0, k, d * FC:(d + 1) * FC],
                                      wqk2[:, p, 1, k], start=(k == 0), stop=(k == KC - 1))
                else:
                    if piece == 1:
                        pe.wait_ge(proj_act, count)
                    b, d = divmod(piece - 1, 2)
                    for k in range(KC):
                        last = mm(dst[0:FC, 0:T], qk_2[:, k, d * FC:(d + 1) * FC], x_t[:, k, b * T:(b + 1) * T],
                                  start=(k == 0), stop=(k == KC - 1))
                last.then_inc(proj_mm, 1)

            def scores2(h, n, p, s):
                b, i = divmod(s, CI)
                if i == 0:
                    pe.wait_ge(proj_act, 2 * HEADS + 5 * h + 3 + 2 * b)
                for k in range(KC):
                    last = mm(score_bank[s % 3][0:P, 0:T], z_t[:, p, k, tok(b, i)], x_t[:, k, b * T:(b + 1) * T],
                              start=(k == 0), stop=(k == KC - 1))
                last.then_inc(scores_mm, 1)

            for piece in range(5):
                proj2(0, 0, piece)
            pe.wait_ge(v_dve, NC_ + 6)
            for s in range(2):
                scores2(0, 2 * STEPS + s, 0, s)

            def body2(pair, final):
                for p in range(2):
                    h = pair * 2 + p
                    for s in range(SPH):
                        n = h * SPH + (2 * STEPS + s)
                        transposes(n, s, False, n)
                        more = not (final and p == 1)
                        if more and s < 5:
                            proj2(h + 1, 1 - p, s)
                        if s + 2 < SPH:
                            scores2(h, n + 2, p, s + 2)
                        elif more:
                            scores2(h + 1, n + 2, 1 - p, s + 2 - SPH)
                        av(n, h * B + (2 * STEPS // CI + s // CI), s, False, v_1, head_cols(h, D1), D1)

            with nc.tensor.Fori(0, PAIRS - 1) as pair:
                body2(pair, False)
            body2(PAIRS - 1, True)

            pe.wait_ge(ld_wf, 48)
            turn_xn(4 * NC_)
            for b in range(B):
                for k in range(KC):
                    last = mm(turn_bank[b][:, 0:T], fw1[:, k], x_t[:, k, b * T:(b + 1) * T],
                              start=(k == 0), stop=(k == KC - 1))
                last.then_inc(fh_mm, 1)
            for b in range(B):
                pe.wait_ge(fh_ready, b + 1)
                for k in range(KC):
                    if b == 1:
                        pe.wait_ge(fp_ready, k + 1)
                    mm(turn_bank[2 + k][0:FC, 0:T], fw2[:, k * FC:(k + 1) * FC], f_h[:, b * T:(b + 1) * T],
                       start=True, stop=True).then_inc(fp_mm, 1)
            pe.wait_ge(fp_ready, 2 * B)
            for ci in range(NC_):
                for k in range(KC):
                    last = mm(score_bank[ci // 2][0:P, (ci % 2) * C:(ci % 2 + 1) * C],
                              f_p[:, k, ci * P:(ci + 1) * P], fwo[:, k], start=(k == 0), stop=(k == KC - 1))
                last.then_inc(y_mm, 1)

        @block.scalar
        def _(act):
            turned = [0]
            norms = [0]

            def root():
                norms[0] += 1
                act.wait_ge(var_ready, norms[0])
                nc.scalar.activation(std[:], mv[:, :, 1], ACT.Sqrt, bias=cst["eps"][0:P], scale=1.0).then_inc(std_ready, 1)

            def take_turned(dst, count, w=None, bvec=None):
                for g in range(0, count, 2):
                    n = turned[0]
                    act.wait_ge(turn_mm, n + 1)
                    d = dst(g)
                    src = turn_bank[n % 4][0:d.shape[0], 0:T]
                    if w is None:
                        nc.scalar.copy(d, src).then_inc(turn_act, 1)
                    else:
                        k = g % KC
                        nc.scalar.activation(d, src, ACT.Identity, bias=bvec[0:FC, k:k + 1],
                                             scale=w[0:FC, k:k + 1]).then_inc(turn_act, 1)
                    turned[0] += 2

            def x_t_part(g):
                b, k = divmod(g, KC)
                return x_t[:, k, b * T:(b + 1) * T]

            def o_t_part(g):
                b, k = divmod(g, FK)
                return o_0t[:, k, b * T:(b + 1) * T]

            def exps(n, s, causal, n_first=3):
                w = width(causal, s % CI)
                act.wait_ge(max_ready, n + 1)
                if n_first >= 3:
                    act.wait_ge(probs_turn, n - 2)
                nc.scalar.activation(probs[:, s % 3, 0:w], score_bank[s % 3][0:P, 0:w], ACT.Exp,
                                     bias=nmax[:, s:s + 1], scale=1.0,
                                     accum_out=rsum[:, s:s + 1]).then_inc(probs_ready, 1)

            def copy_pt(n, s, causal):
                w = width(causal, s % CI)
                act.wait_ge(probs_turn, n + 1)
                nc.scalar.copy(flat(probs_t[:, s % 2])[:, 0:w], pt_bank[s % 2][0:P, 0:w]).then_inc(pt_ready, 1)

            act.wait_ge(ld_const, 16)
            root()
            take_turned(x_t_part, 4)
            root()
            act.wait_ge(ld_cols, 16)
            for b in range(B):
                act.wait_ge(lat_turn, b + 1)
                nc.scalar.activation(c_t[:, b * T:(b + 1) * T], pt_bank[b][0:D0, 0:T], ACT.Identity,
                                     bias=col["lnb"][0:D0], scale=col["lng"][0:D0]).then_inc(ct_ready, 1)
            for m in range(1, 2 * NC_, 2):
                act.wait_ge(v_mm, m + 1)
                nc.scalar.copy(v_0[:, m // 2, 384:768], score_bank[m % 3][0:P, 0:384]).then_inc(v_act, 1)

            def doubled(h, p, b):
                act.wait_ge(proj_mm, 6 * h + (4 if b == 0 else 6))
                nc.scalar.copy(k_t[:, p, b * T:(b + 1) * T], proj_bank[1][:, 0:T]).then_inc(proj_act, 1)

            doubled(0, 0, 0)
            doubled(0, 0, 1)
            exps(0, 0, True, 0)
            exps(1, 1, True, 0)

            def body0(pair, final):
                for p in range(2):
                    h = pair * 2 + p
                    for s in range(SPH):
                        n = h * SPH + s
                        copy_pt(n, s, True)
                        more = not (final and p == 1)
                        if more and s in (1, 3):
                            doubled(h + 1, 1 - p, s // 2)
                        if s + 2 < SPH or more:
                            exps(n + 2, (s + 2) % SPH, True, 0)

            with nc.scalar.Fori(0, PAIRS - 1) as pair:
                body0(pair, False)
            body0(PAIRS - 1, True)
            take_turned(o_t_part, 2 * FK)
            root()
            root()
            take_turned(x_t_part, 4, col["ln1w"], col["ln1b"])
            for m in range(2 * GROUPS):
                g, b = divmod(m, 2)
                act.wait_ge(qk1_mm, 2 * GROUPS + m + 1)
                nc.scalar.activation(k_1t[:, g, b * T:(b + 1) * T], turn_bank[(2 * GROUPS + m) % 4][:, 0:T],
                                     ACT.Identity, bias=col["qkb"][:, GROUPS + g:GROUPS + g + 1],
                                     scale=1.0).then_inc(k1_ready, 1)
            exps(STEPS, 0, True)
            exps(STEPS + 1, 1, True)
            with nc.scalar.Fori(0, HEADS - 1) as h:
                for s in range(SPH):
                    exps(h * SPH + (STEPS + s + 2), (s + 2) % SPH, True)
            for s in range(SPH - 2):
                exps(2 * STEPS - SPH + s + 2, s + 2, True)
            take_turned(x_t_part, 4)
            root()
            take_turned(x_t_part, 4)
            act.wait_ge(diff_ready, 1)
            nc.scalar.activation(eexp[:], ediff[:], ACT.Exp).then_inc(exp_ready, 1)
            for e in range(E):
                p = e % 2
                act.wait_ge(slot_turn, e + 1)
                nc.scalar.copy(flat(x_slot_t[:, p]), pt_bank[p][0:FC, 0:KC * CAP]).then_inc(slot_t_ready, 1)
                for f in range(FK):
                    n = FK * e + f
                    act.wait_ge(hid_mm, n + 1)
                    if e >= 2:
                        act.wait_ge(out_mm, 2 * (e - 1))
                    nc.scalar.activation(hid[:, p, f], score_bank[n % 3][:, 0:CAP], ACT.Gelu,
                                         bias=col["fcb"][:, n:n + 1], scale=1.0).then_inc(hid_ready, 1)
            root()
            take_turned(x_t_part, 4)

            def take2(h, p, piece):
                act.wait_ge(proj_mm, 6 * HEADS + 1 + (5 * h + piece))
                src = proj_bank[(p * 5 + piece) % 2]
                if piece == 0:
                    nc.scalar.copy(flat(qk_2[:]), src[0:FC, 0:KC * C]).then_inc(proj_act, 1)
                else:
                    b, d = divmod(piece - 1, 2)
                    nc.scalar.copy(z_t[:, p, d, b * T:(b + 1) * T], src[0:FC, 0:T]).then_inc(proj_act, 1)

            for piece in range(5):
                take2(0, 0, piece)
            exps(2 * STEPS, 0, False)
            exps(2 * STEPS + 1, 1, False)

            def body2(pair, final):
                for p in range(2):
                    h = pair * 2 + p
                    for s in range(SPH):
                        more = not (final and p == 1)
                        if more and s < 5:
                            take2(h + 1, 1 - p, s)
                        if s + 2 < SPH or more:
                            exps(h * SPH + (2 * STEPS + s + 2), (s + 2) % SPH, False)

            with nc.scalar.Fori(0, PAIRS - 1) as pair:
                body2(pair, False)
            body2(PAIRS - 1, True)
            root()
            take_turned(x_t_part, 4)
            for b in range(B):
                act.wait_ge(fh_mm, b + 1)
                nc.scalar.activation(f_h[:, b * T:(b + 1) * T], turn_bank[b][:, 0:T], ACT.Relu,
                                     bias=col["fb1"], scale=1.0).then_inc(fh_ready, 1)
            for m in range(2 * B):
                b, k = divmod(m, KC)
                act.wait_ge(fp_mm, m + 1)
                nc.scalar.activation(f_p[:, k, b * T:(b + 1) * T], turn_bank[2 + k][0:FC, 0:T], ACT.Identity,
                                     bias=col["fb2"][0:FC, k:k + 1], scale=1.0).then_inc(fp_ready, 1)
            root()

        @block.vector
        def _(dve):
            own = [0]
            norms = [0]
            turned = [0]

            def step(ins):
                own[0] += 1
                ins.then_inc(dve_step, 1)
                dve.wait_ge(dve_step, own[0])

            def moments(src):
                for ci in range(NC_):
                    last = nc.vector.bn_stats(bn[:, ci], src[:, ci])
                step(last)
                for ci in range(NC_):
                    last = nc.vector.bn_aggr(mv[:, ci], bn[:, ci])
                last.then_inc(var_ready, 1)
                norms[0] += 1
                dve.wait_ge(std_ready, norms[0])
                step(nc.vector.reciprocal(rstd[:], std[:]))

            def normalise(dst, src, signal):
                for ci in range(NC_):
                    last = nc.vector.tensor_scalar(dst[:, ci], src[:, ci], mv[:, ci, 0:1], rstd[:, ci:ci + 1],
                                                   ALU.subtract, ALU.mult)
                    if signal is not None:
                        last.then_inc(signal, 1)
                return last

            def take_turned(dst, count, w=None, bvec=None):
                for g in range(1, count, 2):
                    n = turned[0] + 1
                    dve.wait_ge(turn_mm, n + 1)
                    d = dst(g)
                    src = turn_bank[n % 4][0:d.shape[0], 0:T]
                    if w is None:
                        nc.vector.tensor_copy(d, src).then_inc(turn_dve, 1)
                    else:
                        k = g % KC
                        nc.vector.tensor_scalar(d, src, w[0:FC, k:k + 1], bvec[0:FC, k:k + 1],
                                                ALU.mult, ALU.add).then_inc(turn_dve, 1)
                    turned[0] += 2

            def x_t_part(g):
                b, k = divmod(g, KC)
                return x_t[:, k, b * T:(b + 1) * T]

            def o_t_part(g):
                b, k = divmod(g, FK)
                return o_0t[:, k, b * T:(b + 1) * T]

            def maxima(n, s, causal):
                dve.wait_ge(scores_mm, n + 1)
                nc.vector.tensor_reduce(nmax[:, s:s + 1], score_bank[s % 3][0:P, 0:width(causal, s % CI)],
                                        AX.X, ALU.max, negate=True).then_inc(max_ready, 1)

            def copy_pt(n, s, causal):
                w = width(causal, s % CI)
                dve.wait_ge(probs_turn, n + 1)
                nc.vector.tensor_copy(flat(probs_t[:, s % 2])[:, 0:w], pt_bank[s % 2][0:P, 0:w]).then_inc(pt_ready, 1)

            def divide(n, u, s, o, hd, d):
                b = s // CI
                dve.wait_ge(probs_ready, n + 1)
                nc.vector.reciprocal(rinv[:, b], rsum[:, b * CI:(b + 1) * CI]).then_inc(rinv_ready, 1)
                dve.wait_ge(rinv_ready, u + 1)
                dve.wait_ge(av_mm, n + 1)
                nc.vector.tensor_tensor(
                    o[:, b * CI:(b + 1) * CI, hd],
                    o_bank[0:P, 0:CI * d].rearrange("p (i d) -> p i d", i=CI),
                    rinv[:, b].unsqueeze(2).to_broadcast([P, CI, d]), ALU.mult).then_inc(o_ready, 1)

            def add_banks(dst, other, mm_sem, first, ready, each):
                for k in range(3):
                    dve.wait_ge(mm_sem, first + (2 * (k + 1) if each else k + 1))
                    last = nc.vector.tensor_tensor(
                        dst[:, 2 * k:2 * k + 2],
                        score_bank[k][0:P, 0:2 * C].rearrange("p (a c) -> p a c", a=2), other(k), ALU.add)
                    last.then_inc(ready, 1)

            dve.wait_ge(ld_base, 16)
            add_banks(h_a, lambda k: base[:, 2 * k:2 * k + 2], tok_mm, 0, h_ready, True)
            dve.wait_ge(h_ready, 3)
            moments(h_a)
            normalise(xn, h_a, norm_ready)
            take_turned(x_t_part, 4)
            nc.vector.tensor_copy(ident_bf[:], cst["ident"][0:P, 0:P])
            nc.vector.tensor_copy(causal_bf[:], cst["causal"][0:P])
            nc.vector.tensor_copy(before_bf[:], cst["before"][0:P]).then_inc(o_ready, 1)
            nc.vector.tensor_copy(ones_bf[:], cst["ones"][0:P]).then_inc(cast_done, 1)
            dve.wait_ge(lat_mm, 1)
            lat = o_bank[0:P, 0:NC_ * D0].rearrange("p (c d) -> p c d", c=NC_)
            moments(lat)
            normalise(c_n, lat, lat_ready)
            for m in range(0, 2 * NC_, 2):
                dve.wait_ge(v_mm, m + 1)
                nc.vector.tensor_copy(v_0[:, m // 2, 0:384], score_bank[m % 3][0:P, 0:384]).then_inc(v_dve, 1)

            def rope(h, p, piece):
                b = {0: 0, 1: 0, 2: 1, 4: 1}[piece]
                dve.wait_ge(proj_mm, 6 * h + (piece + 1))
                src = proj_bank[piece % 2][:, 0:T]
                if piece in (0, 2):
                    nc.vector.tensor_tensor(q_t[:, p, b * T:(b + 1) * T], src, cst["cos_sin_q"], ALU.mult).then_inc(proj_dve, 1)
                else:
                    nc.vector.tensor_tensor(k_cs[:, b], src, cst["cos_sin_k"], ALU.mult).then_inc(proj_dve, 1)

            for piece in (0, 1, 2, 4):
                rope(0, 0, piece)
            maxima(0, 0, True)
            maxima(1, 1, True)
            pieces = {0: (0, 1), 1: (2,), 2: (4,)}

            def body0(pair, final):
                for p in range(2):
                    h = pair * 2 + p
                    for s in range(SPH):
                        n = h * SPH + s
                        more = not (final and p == 1)
                        if more:
                            for piece in pieces.get(s, ()):
                                rope(h + 1, 1 - p, piece)
                        if s + 2 < SPH or more:
                            maxima(n + 2, (s + 2) % SPH, True)
                        if s % CI == CI - 1:
                            divide(n, h * B + s // CI, s, o_0, head_cols(h, D0), D0)

            with nc.vector.Fori(0, PAIRS - 1) as pair:
                body0(pair, False)
            body0(PAIRS - 1, True)
            take_turned(o_t_part, 2 * FK)
            dve.wait_ge(hb_ready, 1)
            add_banks(h_a, lambda k: h_b[:, 2 * k:2 * k + 2], y_mm, 0, h_ready, True)
            dve.wait_ge(h_ready, 6)
            moments(h_a)
            step(normalise(g_a, h_a, None))
            moments(g_a)
            normalise(xn, g_a, norm_ready)
            take_turned(x_t_part, 4, col["ln1w"], col["ln1b"])
            for m in range(2 * GROUPS):
                g, b = divmod(m, 2)
                dve.wait_ge(qk1_mm, m + 1)
                nc.vector.tensor_scalar(q_1t[:, g, b * T:(b + 1) * T], turn_bank[m % 4][:, 0:T],
                                        col["qkb"][:, g:g + 1], D1 ** -0.5, ALU.add, ALU.mult).then_inc(q1_ready, 1)
            add_banks(v_1, lambda k: row["vb"].unsqueeze(1).to_broadcast([P, 2, C]), v_mm, 2 * NC_, v_dve, False)
            maxima(STEPS, 0, True)
            maxima(STEPS + 1, 1, True)
            with nc.vector.Fori(0, HEADS - 1) as h:
                for s in range(SPH):
                    n = h * SPH + (STEPS + s)
                    copy_pt(n, s, True)
                    maxima(n + 2, (s + 2) % SPH, True)
                    if s % CI == CI - 1:
                        divide(n, h * B + (STEPS // CI + s // CI), s, o_1, head_cols(h, D1), D1)
            for s in range(SPH):
                n = 2 * STEPS - SPH + s
                copy_pt(n, s, True)
                if s + 2 < SPH:
                    maxima(n + 2, s + 2, True)
                if s % CI == CI - 1:
                    divide(n, n // CI, s, o_1, head_cols(HEADS - 1, D1), D1)
            take_turned(x_t_part, 4)
            dve.wait_ge(hb_ready, 2)
            add_banks(g_a, lambda k: h_b[:, 2 * k:2 * k + 2], y_mm, NC_, h_ready, True)
            dve.wait_ge(h_ready, 9)
            moments(g_a)
            for ci in range(NC_):
                last = nc.vector.scalar_tensor_tensor(xn[:, ci], g_a[:, ci], mv[:, ci, 0:1], row["ln2w"],
                                                      ALU.subtract, ALU.mult)
            step(last)
            for ci in range(NC_):
                nc.vector.scalar_tensor_tensor(xn[:, ci], xn[:, ci], rstd[:, ci:ci + 1], row["ln2b"],
                                               ALU.mult, ALU.add).then_inc(norm_ready, 1)
            take_turned(x_t_part, 4)

            dve.wait_ge(gate_mm, 1)
            step(nc.vector.tensor_copy(flat(lg[:]), o_bank[0:P, 0:NC_ * E]))
            for ci in range(NC_):
                last = nc.vector.max(m8[:, ci], lg[:, ci])
            step(last)
            nc.vector.tensor_tensor(ediff[:], m8[:, :, 1], m8[:, :, 0], ALU.subtract).then_inc(diff_ready, 1)
            for ci in range(NC_):
                last = nc.vector.max_index(i8[:, ci], m8[:, ci], lg[:, ci])
            step(last)
            step(nc.vector.tensor_copy(i8f[:], i8[:, :, 0:2].rearrange("p c k -> p k c")))
            ex = cst["expert"][0:P].unsqueeze(1).to_broadcast([P, 2 * NC_, E])
            oh12 = oh[:].rearrange("p k c e -> p (k c) e")
            i8f12 = flat(i8f[:])
            nc.vector.tensor_tensor(oh12, ex, i8f12.unsqueeze(2).to_broadcast([P, 2 * NC_, E]),
                                    ALU.is_equal).then_inc(oh_ready, 1)
            dve.wait_ge(rank_mm, 1)
            step(nc.vector.tensor_copy(tot[:], score_bank[1][0:P, 0:96].rearrange("p (b e) -> p e b", e=E)))
            step(nc.vector.tensor_tensor_scan(flat(run[:]), cst["restart"][0:P], flat(tot[:]), 0.0, ALU.mult, ALU.add))
            step(nc.vector.tensor_tensor(run[:], run[:], tot[:], ALU.subtract))
            step(nc.vector.tensor_tensor(rk[:], score_bank[0][0:P, 0:96].rearrange("p (b e) -> p b e", e=E),
                                         run[:].rearrange("p e b -> p b e"), ALU.add))
            step(nc.vector.tensor_tensor(rk[:], rk[:], oh12, ALU.mult))
            step(nc.vector.tensor_reduce(small["rank"][:], rk[:], AX.X, ALU.add))
            nc.vector.tensor_scalar(small["keep"][:], small["rank"][:], float(CAP), None, ALU.is_lt)
            step(nc.vector.scalar_tensor_tensor(small["slot"][:], i8f12, float(CAP), small["rank"][:],
                                                ALU.mult, ALU.add))
            step(nc.vector.tensor_tensor(small["off"][:], small["slot"][:], cst["dump"][0:P], ALU.subtract))
            step(nc.vector.tensor_tensor(small["off"][:], small["off"][:], small["keep"][:], ALU.mult))
            nc.vector.tensor_tensor(scat[:], small["off"][:], cst["dump"][0:P], ALU.add).then_inc(place_ready, 1)
            nc.vector.tensor_tensor(gath[:], small["slot"][:], small["keep"][:], ALU.mult).then_inc(place_ready, 1)
            dve.wait_ge(exp_ready, 1)
            step(nc.vector.tensor_scalar(eden[:], eexp[:], 1.0, None, ALU.add))
            step(nc.vector.reciprocal(small["w"][:, 0:NC_], eden[:]))
            step(nc.vector.tensor_tensor(small["w"][:, NC_:2 * NC_], small["w"][:, 0:NC_], eexp[:], ALU.mult))
            step(nc.vector.tensor_tensor(small["w"][:], small["w"][:], small["keep"][:], ALU.mult))
            for e in range(E):
                for s in range(2):
                    dve.wait_ge(out_mm, 2 * e + s + 1)
                    if e >= 2:
                        dve.wait_ge(st_slot[e % 2], 16 * (e // 2))
                    nc.vector.tensor_tensor(y_slot[:, e % 2, s], proj_bank[s][0:SH, 0:C],
                                            row["pjb"][0:SH, e * C:(e + 1) * C], ALU.add).then_inc(ys_ready, 1)
            dve.wait_ge(hb_ready, 3)
            dve.wait_ge(gathered, 16 * 2 * NC_)
            for ci in range(NC_):
                last = nc.vector.scalar_tensor_tensor(h_b[:, ci], y_tok[:, ci], small["w"][:, ci:ci + 1],
                                                      h_b[:, ci], ALU.mult, ALU.add)
            step(last)
            for ci in range(NC_):
                last = nc.vector.scalar_tensor_tensor(h_a[:, ci], y_tok[:, NC_ + ci], small["w"][:, NC_ + ci:NC_ + ci + 1],
                                                      h_b[:, ci], ALU.mult, ALU.add)
            step(last)

            moments(h_a)
            normalise(xn, h_a, norm_ready)
            take_turned(x_t_part, 4)
            for k in range(3):
                dve.wait_ge(v_mm, 2 * NC_ + 3 + k + 1)
                nc.vector.tensor_copy(v_1[:, 2 * k:2 * k + 2],
                                      score_bank[k][0:P, 0:2 * C].rearrange("p (a c) -> p a c", a=2)).then_inc(v_dve, 1)
            maxima(2 * STEPS, 0, False)
            maxima(2 * STEPS + 1, 1, False)
            with nc.vector.Fori(0, HEADS - 1) as h:
                for s in range(SPH):
                    n = h * SPH + (2 * STEPS + s)
                    copy_pt(n, s, False)
                    maxima(n + 2, (s + 2) % SPH, False)
                    if s % CI == CI - 1:
                        divide(n, h * B + (2 * STEPS // CI + s // CI), s, o_1, head_cols(h, D1), D1)
            for s in range(SPH):
                n = 3 * STEPS - SPH + s
                copy_pt(n, s, False)
                if s + 2 < SPH:
                    maxima(n + 2, s + 2, False)
                if s % CI == CI - 1:
                    divide(n, n // CI, s, o_1, head_cols(HEADS - 1, D1), D1)
            dve.wait_ge(o_ready, 1 + 3 * STEPS // CI)
            step(nc.vector.tensor_tensor(h_a[:], h_a[:], o_1[:], ALU.add))
            moments(h_a)
            normalise(xn, h_a, norm_ready)
            take_turned(x_t_part, 4)
            add_banks(g_a, lambda k: row["bo1"].unsqueeze(1).to_broadcast([P, 2, C]), y_mm, 2 * NC_, h_ready, True)
            dve.wait_ge(h_ready, 12)
            nc.vector.tensor_tensor(h_b[:], h_a[:], row["beta"].unsqueeze(1).to_broadcast([P, NC_, C]), ALU.add)
            moments(g_a)
            for ci in range(NC_):
                last = nc.vector.scalar_tensor_tensor(g_a[:, ci], g_a[:, ci], mv[:, ci, 0:1], row["gamma"],
                                                      ALU.subtract, ALU.mult)
            step(last)
            for ci in range(NC_):
                nc.vector.scalar_tensor_tensor(h_b[:, ci], g_a[:, ci], rstd[:, ci:ci + 1], h_b[:, ci],
                                               ALU.mult, ALU.add).then_inc(h_ready, 1)

        @block.gpsimd
        def _(pool):
            nc.gpsimd.memset(zero[:], 0.0).then_inc(zero_ready, 1)
            pool.wait_ge(ld_rows, 16)
            pool.wait_ge(h_ready, 3)
            nc.gpsimd.tensor_tensor(h_b[:], h_a[:], row["bo0"].unsqueeze(1).to_broadcast([P, NC_, C]),
                                    ALU.add).then_inc(hb_ready, 1)
            pool.wait_ge(norm_ready, 2 * NC_)
            nc.gpsimd.tensor_tensor(h_b[:], g_a[:], row["projb"].unsqueeze(1).to_broadcast([P, NC_, C]),
                                    ALU.add).then_inc(hb_ready, 1)
            pool.wait_ge(h_ready, 9)
            pool.wait_ge(zeroed, 16)
            pool.wait_ge(place_ready, 2)
            for k in range(2):
                for ci in range(NC_):
                    m = k * NC_ + ci
                    nc.gpsimd.indirect_dma_start(
                        x_dram, bass.IndirectOffsetOnAxis(ap=scat[:, m:m + 1].bitcast(U32), axis=0), xn[:, ci], None
                    ).then_inc(scattered, 16)
            nc.gpsimd.tensor_tensor(h_b[:], h_a[:], g_a[:], ALU.add).then_inc(hb_ready, 1)
            for p in range(2):
                pool.wait_ge(st_slot[p], 16 * (E // 2))
            for m in range(2 * NC_):
                nc.gpsimd.indirect_dma_start(
                    y_tok[:, m], None, y_dram, bass.IndirectOffsetOnAxis(ap=gath[:, m:m + 1].bitcast(U32), axis=0)
                ).then_inc(gathered, 16)


HR_OUT = 12


def head_cols(h, d):
    return bass.ds(h * d, d)


def head_loads(h, p):
    return 32 * (h // 2 + 1) if isinstance(h, int) else (h - p) * 16 + 32


def head_loads2(h, p):
    return 16 * (h // 2 + 1) if isinstance(h, int) else (h - p) * 8 + 16


def rope_tables():
    import numpy as np
    inv = (np.float32(1.0) / np.float32(10000.0) ** (np.arange(0, D0, 2, dtype=np.float32) / np.float32(D0))).astype(np.float32)
    ang = (np.arange(T, dtype=np.float32)[:, None] * inv[None, :]).astype(np.float32)
    cos, sin = np.cos(ang).T, np.sin(ang).T
    return np.concatenate([cos, cos, -sin, sin], axis=0).astype(np.float32)


def constants():
    import numpy as np
    c = np.zeros((128, CONST_N), np.float32)

    def put(name, v):
        lo, hi = CONST_AT[name]
        c[:v.shape[0], lo:hi] = v

    put("ident", np.eye(128))
    put("dup", np.tile(np.eye(D0), (2, 2)))
    table = rope_tables()
    put("cos_sin_q", table * np.float32(D0 ** -0.5))
    put("cos_sin_k", table)
    t = np.arange(P)
    put("before", (t[:, None] < t[None, :]).astype(np.float32))
    put("ones", np.ones((P, P)))
    put("causal", np.where(t[None, :] > t[:, None], -1e30, 0.0))
    put("expert", np.tile(np.arange(E), (P, 1)))
    put("dump", SLOTS + np.arange(2 * NC_)[None, :] * P + t[:, None])
    put("restart", np.tile((np.arange(E * 2 * NC_) % (2 * NC_) != 0).astype(np.float32), (P, 1)))
    put("eps", np.full((128, 1), EPS))
    return c


def lay_out(i):
    import numpy as np
    i = {k: np.asarray(v) for k, v in i.items()}
    z = np.zeros

    def chunked(w):
        return w.reshape(KC, FC, -1).transpose(1, 0, 2)

    def token_major(x):
        return x.reshape(B, CI, P, -1).transpose(2, 0, 1, 3).reshape(P, NC_, -1)

    def columns(v):
        return v.reshape(KC, FC).T

    f32 = np.float32
    x = i["x"].reshape(B, 3, 16, 4, 16, 4).transpose(0, 1, 2, 4, 3, 5).reshape(B, 256, PATCH)
    tok_x = z((PATCH + 1, B, T), f32)
    tok_x[:PATCH, :, :256] = x.transpose(2, 0, 1)
    tok_x[PATCH, :, :256] = 1.0
    base = z((B, T, C), f32)
    base[:, :256] = i["L0_tok_pos"][None]
    base[:, 256:] = i["txt"]
    rot = np.concatenate([np.arange(32, 64), np.arange(0, 32)])
    wq = i["L0_attn_Wq"].reshape(C, HEADS, D0)
    wq = np.concatenate([wq, wq[:, :, rot]], axis=2).reshape(KC, FC, HEADS, 128).transpose(2, 1, 0, 3)
    wk = i["L0_attn_Wup"][:, :FF].reshape(D0, HEADS, D0)
    wk = np.concatenate([wk, wk[:, :, rot]], axis=2).transpose(1, 0, 2)
    qkv = i["L0_ffn_attn_qkv_w"]
    qkvb = i["L0_ffn_attn_qkv_b"]
    wqk1 = z((C, 2, GROUPS, 4, 32), f32)
    wqk1[..., :D1] = qkv[:, :2 * C].reshape(C, 2, GROUPS, 4, D1)
    qkb = z((2, GROUPS, 4, 32), f32)
    qkb[..., :D1] = qkvb[:2 * C].reshape(2, GROUPS, 4, D1)
    cols = z((128, COLS_N), f32)

    def put(name, v):
        lo, hi = COLS_AT[name]
        cols[:v.shape[0], lo:hi] = v

    put("lng", i["L0_attn_ln_g"][:, None])
    put("lnb", i["L0_attn_ln_b"][:, None])
    put("ln1w", columns(i["L0_ffn_ln1_w"]))
    put("ln1b", columns(i["L0_ffn_ln1_b"]))
    put("qkb", qkb.reshape(2 * GROUPS, 128).T)
    put("fb1", i["L1_ffn_b1"][:, None])
    put("fb2", columns(i["L1_ffn_b2"]))
    put("fcb", i["L0_ffn_exp_fc_b"].reshape(E, FK, 128).transpose(2, 0, 1).reshape(128, E * FK))
    rows = np.concatenate([i[k].reshape(-1) for k in (
        "L0_attn_bo", "L0_ffn_attn_proj_b")] + [qkvb[2 * C:]] + [i[k].reshape(-1) for k in (
            "L0_ffn_ln2_w", "L0_ffn_ln2_b", "L1_ffn_bo", "L1_ffn_gamma", "L1_ffn_beta", "L0_ffn_exp_proj_b")])
    a = dict(
        tok_x=tok_x.reshape(PATCH + 1, N),
        tok_w=np.concatenate([i["L0_tok_W"].T, i["L0_tok_b"][None]], axis=0),
        base=token_major(base),
        const=constants(),
        cols=cols,
        rows=rows,
        wdown=chunked(i["L0_attn_Wdown"]),
        wup_v=i["L0_attn_Wup"][:, FF:],
        wq_h=wq, wk_h=wk,
        wo0=i["L0_attn_Wo"].reshape(FK, 128, C).transpose(1, 0, 2),
        wqk1=chunked(wqk1.reshape(C, -1)).reshape(FC, KC, 2 * GROUPS, 128),
        w1s=np.concatenate([chunked(qkv[:, 2 * C:]), chunked(i["L0_ffn_attn_proj_w"]), chunked(i["L0_ffn_w_g"])], axis=2),
        fc_w=i["L0_ffn_exp_fc_w"].reshape(E, KC, FC, FF).transpose(0, 2, 1, 3),
        pj_w=i["L0_ffn_exp_proj_w"].reshape(E, FK, 128, C).transpose(0, 2, 1, 3),
        wqk2=np.stack([i["L1_attn_q"], i["L1_attn_k"]], axis=1).reshape(HEADS, 2, KC, FC, C).transpose(0, 3, 1, 2, 4),
        wv2=chunked(i["L1_attn_v"].reshape(C, C).T),
        fw1=chunked(i["L1_ffn_W1"].T),
        fw2=i["L1_ffn_W2"].T,
        fwo=chunked(i["L1_ffn_Wo"].T),
    )
    return {k: np.ascontiguousarray(v) for k, v in a.items()}


def kernel(**inputs):
    import concourse.bacc as _bacc
    from concourse import mybir as _mybir
    from concourse.bass_utils import run_bass_kernel_spmd as _run

    arrays = lay_out(inputs)
    nc = _bacc.Bacc("TRN2", target_bir_lowering=False, num_devices=1)
    aps = {k: nc.dram_tensor("in_" + k, v.shape, _mybir.dt.from_np(v.dtype), kind="ExternalInput").ap() for k, v in arrays.items()}
    out = nc.dram_tensor("out", (B, T, C), F32, kind="ExternalOutput").ap()
    build(nc, aps, out)
    r = _run(nc, [{"in_" + k: v for k, v in arrays.items()}], core_ids=[0])
    return r.results[0]["out"]
```

```python
from contextlib import ExitStack

import concourse.bass as bass
from concourse import mybir

F32 = mybir.dt.float32
BF16 = mybir.dt.bfloat16
I32 = mybir.dt.int32
U32 = mybir.dt.uint32
ALU = mybir.AluOpType
ACT = mybir.ActivationFunctionType
AX = mybir.AxisListType

B, T, C = 2, 333, 192
N = B * T
P = 111
CI = T // P
NC_ = B * CI
FC = 96
KC = C // FC
HEADS = 12
PAIRS = HEADS // 2
SPH = B * CI
STEPS = HEADS * SPH
AHEAD = CI
QUADS = HEADS // 4
BLOCK0, BLOCK = 2 * CI, 4 * CI
BODY0, BODY = B * BLOCK0, B * BLOCK
D0 = 64
D1 = 16
GROUPS = HEADS // 4
PATCH = 48
E, CAP = 8, 208
FF = 768
FK = FF // 128
SH = CAP // 2
SLOTS = E * CAP
INNER = 128
EPS = 1e-5

CONST_W = dict(ident=128, dup=128, cos_sin_q=T, cos_sin_k=T, before=P, ones=P, mask=T, expert=E,
               dump=2 * NC_, restart=E * 2 * NC_, eps=1)
COLS_W = dict(lng=1, lnb=1, ln1w=KC, ln1b=KC, qkb=2 * GROUPS, fb1=1, fb2=KC, fcb=E * FK)
ROWS_W = dict(bo0=C, projb=C, vb=C, ln2w=C, ln2b=C, bo1=C, gamma=C, beta=C, pjb=E * C)


def offsets(widths):
    at, out = 0, {}
    for name, w in widths.items():
        out[name] = (at, at + w)
        at += w
    return out, at


CONST_AT, CONST_N = offsets(CONST_W)
COLS_AT, COLS_N = offsets(COLS_W)
ROWS_AT, ROWS_N = offsets(ROWS_W)


def build(nc, a, out):
    ctx = ExitStack()
    with ctx:
        def sb(name, shape, dt=F32):
            return ctx.enter_context(nc.sbuf_tensor(name, shape, dt))

        def sem(name):
            return ctx.enter_context(nc.semaphore(name))

        bank = [ctx.enter_context(nc.psum_tensor(f"bank{i}", [128, 512], F32)) for i in range(8)]
        score_bank, pt_bank, o_bank, proj_bank = bank[0:3], bank[3:5], bank[5], bank[6:8]
        turn_bank = [pt_bank[0], pt_bank[1], proj_bank[0], proj_bank[1]]

        const = sb("consts", [128, CONST_N])
        cols = sb("cols", [128, COLS_N])
        rows = sb("rows", [P, ROWS_N])
        cst = {k: const[:, lo:hi] for k, (lo, hi) in CONST_AT.items()}
        col = {k: cols[:, lo:hi] for k, (lo, hi) in COLS_AT.items()}
        row = {k: rows[:, lo:hi] for k, (lo, hi) in ROWS_AT.items()}
        before_bf = sb("before_bf", [P, P], BF16)
        ones_bf = sb("ones_bf", [P, P], BF16)
        tok_x = sb("tok_x", [PATCH + 1, N])
        tok_w = sb("tok_w", [PATCH + 1, C])
        base = sb("base", [P, NC_, C])
        h_a = sb("h_a", [P, NC_, C])
        h_b = sb("h_b", [P, NC_, C])
        g_a = sb("g_a", [P, NC_, C])
        xn = sb("xn", [P, NC_, C])
        x_t = sb("x_t", [FC, KC, N])
        bn = sb("bn", [P, NC_, 6])
        mv = sb("mv", [P, NC_, 2])
        std = sb("std", [P, NC_])
        rstd = sb("rstd", [P, NC_])
        wdown = sb("wdown", [FC, KC, D0])
        wup_v = sb("wup_v", [D0, HEADS * D0])
        c_n = sb("c_n", [P, NC_, D0])
        c_t = sb("c_t", [D0, N])
        wq_h = sb("wq_h", [FC, 2, KC, 128])
        wk_h = sb("wk_h", [D0, 2, 128])
        qk_space = sb("qk_space", [128, 4 * N])
        q_t = qk_space[:, 0:2 * N].rearrange("p (s n) -> p s n", s=2)
        k_t = qk_space[:, 2 * N:4 * N].rearrange("p (s n) -> p s n", s=2)
        q_m = qk_space[:].rearrange("p (s n) -> p s n", s=4)
        k_cs = sb("k_cs", [128, 2, T])
        wo0 = sb("wo0", [128, FK, C])
        wide_a = sb("wide_a", [128, FK * N])
        o_0t = wide_a[:, 0:FK * N].rearrange("p (k n) -> p k n", k=FK)
        q_1t = wide_a[:, 0:GROUPS * N].rearrange("p (g n) -> p g n", g=GROUPS)
        k_1t = wide_a[:, GROUPS * N:2 * GROUPS * N].rearrange("p (g n) -> p g n", g=GROUPS)
        z_t = wide_a[0:FC, 0:2 * KC * T].rearrange("p (s k n) -> p s k n", s=2, k=KC)
        qk_2 = wide_a[0:FC, 2 * N:2 * N + 4 * KC * C].rearrange("p (s k n) -> p s k n", s=4, k=KC)
        f_h = wide_a[0:INNER, 0:N]
        v_p = sb("v_p", [P, NC_, 2 * D0])
        v_q = sb("v_q", [P, NC_, 4, 32])
        pt_ring = sb("pt_ring", [P, 8 * CI * T])
        probs_t = pt_ring[:].rearrange("p (u j l) -> p u j l", u=8, j=CI)
        o_t = sb("o_t", [128, T])
        masked = sb("masked", [P, CI, T])
        v_1 = sb("v_1", [P, NC_, C])
        o_1 = sb("o_1", [P, NC_, C])
        probs = sb("probs", [P, 3, T])
        nmax = sb("nmax", [P, CI])
        rsum = sb("rsum", [P, CI])
        rinv0 = sb("rinv0", [P, CI])
        spare = sb("spare", [1, 1])
        rinv = sb("rinv", [P, CI, 4])
        wqk1 = sb("wqk1", [FC, KC, 2 * GROUPS, 128])
        w1s = sb("w1s", [FC, KC, 2 * C + E])
        fc_w = sb("fc_w", [FC, 2, KC, FF])
        pj_w = sb("pj_w", [128, 2, FK, C])
        lg = sb("lg", [P, NC_, E])
        m8 = sb("m8", [P, NC_, 8])
        i8 = sb("i8", [P, NC_, 8], U32)
        i8f = sb("i8f", [P, 2, NC_])
        oh = sb("oh", [P, 2, NC_, E], BF16)
        tot = sb("tot", [P, E, 2 * NC_])
        run = sb("run", [P, E, 2 * NC_])
        rk = sb("rk", [P, 2 * NC_, E])
        small = {k: sb("r_" + k, [P, 2 * NC_]) for k in ("rank", "keep", "slot", "off", "w")}
        scat = sb("scat", [P, 2 * NC_], I32)
        gath = sb("gath", [P, 2 * NC_], I32)
        ediff = sb("ediff", [P, NC_])
        eexp = sb("eexp", [P, NC_])
        eden = sb("eden", [P, NC_])
        moe_space = sb("moe_hid", [128, 2 * FK * CAP])
        hid = moe_space[:].rearrange("p (s f c) -> p s f c", s=2, f=FK)
        x_slot = pt_ring[0:SH, 0:4 * C].rearrange("p (s h c) -> p s h c", s=2, h=2)
        y_slot = pt_ring[0:SH, 4 * C:8 * C].rearrange("p (s h c) -> p s h c", s=2, h=2)
        x_slot_t = pt_ring[0:FC, 8 * C:8 * C + 4 * CAP].rearrange("p (s k c) -> p s k c", s=2, k=KC)
        y_tok = pt_ring[:, 8 * C + 4 * CAP:8 * C + 4 * CAP + 12 * C].rearrange("p (m c) -> p m c", m=2 * NC_)
        zero = sb("zero", [SH, C])
        wqk2 = sb("wqk2", [FC, 2, 2, KC, C])
        wv2 = sb("wv2", [FC, KC, C])
        fw1 = sb("fw1", [FC, KC, INNER])
        fw2 = sb("fw2", [INNER, C])
        fwo = sb("fwo", [FC, KC, C])
        f_p = x_t

        x_dram = nc.dram_tensor("slot_rows", [SLOTS + 2 * N, C], F32, kind="Internal").ap()
        y_dram = nc.dram_tensor("expert_rows", [SLOTS, C], F32, kind="Internal").ap()

        ld_tok, ld_base, ld_const, ld_cols, ld_rows = (sem(s) for s in (
            "ld_tok", "ld_base", "ld_const", "ld_cols", "ld_rows"))
        ld_w0, ld_wo0, ld_w1, ld_wv2, ld_wf = (sem(s) for s in (
            "ld_w0", "ld_wo0", "ld_w1", "ld_wv2", "ld_wf"))
        ld_head = [sem(f"ld_head{p}") for p in range(2)]
        ld_head2 = [sem(f"ld_head2{p}") for p in range(2)]
        ld_fc = [sem(f"ld_fc{p}") for p in range(2)]
        ld_pj = [sem(f"ld_pj{p}") for p in range(2)]
        tok_mm = sem("tok_mm")
        h_ready = sem("h_ready")
        hb_ready = sem("hb_ready")
        var_ready = sem("var_ready")
        std_ready = sem("std_ready")
        norm_ready = sem("norm_ready")
        turn_mm = sem("turn_mm")
        turn_act = sem("turn_act")
        turn_dve = sem("turn_dve")
        lat_mm = sem("lat_mm")
        lat_ready = sem("lat_ready")
        lat_turn = sem("lat_turn")
        ct_ready = sem("ct_ready")
        v_mm = sem("v_mm")
        v_act = sem("v_act")
        v_dve = sem("v_dve")
        proj_mm = sem("proj_mm")
        proj_dve = sem("proj_dve")
        proj_act = sem("proj_act")
        scores_mm = sem("scores_mm")
        max_ready = sem("max_ready")
        probs_ready = sem("probs_ready")
        probs_turn = sem("probs_turn")
        pt_ready = sem("pt_ready")
        scaled = sem("scaled")
        block_mm = sem("block_mm")
        ot_ready = sem("ot_ready")
        ot_turn = sem("ot_turn")
        small_dve = sem("small_dve")
        rsum_inv = sem("rsum_inv")
        o_ready = sem("o_ready")
        vq_ready = sem("vq_ready")
        vq_set = sem("vq_set")
        qm_zero = sem("qm_zero")
        qm_ready = sem("qm_ready")
        qk1_mm = sem("qk1_mm")
        q1_ready = sem("q1_ready")
        k1_ready = sem("k1_ready")
        y_mm = sem("y_mm")
        gate_mm = sem("gate_mm")
        oh_ready = sem("oh_ready")
        rank_mm = sem("rank_mm")
        diff_ready = sem("diff_ready")
        exp_ready = sem("exp_ready")
        place_ready = sem("place_ready")
        zero_ready = sem("zero_ready")
        zeroed = sem("zeroed")
        scattered = sem("scattered")
        ld_slot = [sem(f"ld_slot{p}") for p in range(2)]
        slot_turn = sem("slot_turn")
        slot_t_ready = sem("slot_t_ready")
        hid_mm = sem("hid_mm")
        hid_ready = sem("hid_ready")
        out_mm = sem("out_mm")
        ys_ready = sem("ys_ready")
        st_slot = [sem(f"st_slot{p}") for p in range(2)]
        gathered = sem("gathered")
        qk2_done = sem("qk2_done")
        fh_mm = sem("fh_mm")
        fh_ready = sem("fh_ready")
        fp_mm = sem("fp_mm")
        fp_ready = sem("fp_ready")
        dve_step = sem("dve_step")
        stored = sem("stored")

        block = ctx.enter_context(nc.Block())

        def flat(x):
            return x.rearrange("p a b -> p (a b)")

        pieces0 = [("v", 0, 0), ("v", 1, 0), ("q", 0, 0), ("k", 0, 0), ("q", 0, 1), ("d", 0, 0), ("k", 0, 1),
                   ("d", 0, 1), ("q", 1, 0), ("k", 1, 0), ("q", 1, 1), ("d", 1, 0), ("k", 1, 1), ("d", 1, 1)]
        at0 = {0: (0,), 1: (1,), 3: (2, 3), 4: (4, 5), 5: (6,), 6: (7,), 9: (8, 9), 10: (10, 11), 11: (12, 13)}
        n0 = len(pieces0)
        dve0 = [m for m in range(n0) if pieces0[m][0] in "qk"]
        act0 = [m for m in range(n0) if pieces0[m][0] in "vd"]
        PRE_MM, PRE_DVE, PRE_ACT = n0 - 2, len(dve0), len(act0) - 2
        MM0 = PRE_MM + n0 * (PAIRS - 1) + 2
        ACT0 = PRE_ACT + len(act0) * (PAIRS - 1) + 2

        def count0(pair, m, of):
            per, pre = {"mm": (list(range(n0)), PRE_MM), "dve": (dve0, PRE_DVE), "act": (act0, PRE_ACT)}[of]
            return pair * len(per) + (pre + per.index(m) + 1)

        pieces2 = []
        at2 = {}
        for u in range(2 * 4):
            todo = ([("a", u + 2, 0)] if (u + 2) % 8 < 4 else []) + [("z", u + 2, 0), ("z", u + 2, 1)]
            for t, piece in enumerate(todo):
                at2[u * CI + t] = len(pieces2)
                pieces2.append(piece)
        n2 = len(pieces2)
        PRE2 = [p for p in pieces2 if p[1] >= 8]

        def count2(quad, m):
            return quad * n2 + (len(PRE2) + m + 1)

        def count_a(h):
            quad, j = divmod(h, 4)
            if j < 2:
                return count2(quad - 1, pieces2.index(("a", 8 + j, 0)))
            return count2(quad, pieces2.index(("a", j, 0)))

        def width(causal, i):
            return P * (i + 1) if causal else T

        def tok(b, i):
            return slice(b * T + i * P, b * T + (i + 1) * P)

        @block.sync
        def _(sp):
            sp.dma_start(tok_x[:], a["tok_x"]).then_inc(ld_tok, 16)
            sp.dma_start(tok_w[:], a["tok_w"]).then_inc(ld_tok, 16)
            sp.dma_start(base[:], a["base"]).then_inc(ld_base, 16)
            sp.dma_start(const[:], a["const"]).then_inc(ld_const, 16)
            sp.dma_start(wdown[:], a["wdown"]).then_inc(ld_w0, 16)
            sp.dma_start(cols[:], a["cols"]).then_inc(ld_cols, 16)
            sp.dma_start(wup_v[:], a["wup_v"]).then_inc(ld_w0, 16)
            for p in range(2):
                sp.dma_start(wq_h[:, p], a["wq_h"][p]).then_inc(ld_head[p], 16)
                sp.dma_start(wk_h[:, p], a["wk_h"][p]).then_inc(ld_head[p], 16)
            sp.dma_start(rows[:], a["rows"].partition_broadcast(P)).then_inc(ld_rows, 16)
            sp.wait_ge(proj_mm, count0(-1, 12, "mm"))
            for p in range(2):
                sp.dma_start(wq_h[:, p], a["wq_h"][2 + p]).then_inc(ld_head[p], 16)
                sp.dma_start(wk_h[:, p], a["wk_h"][2 + p]).then_inc(ld_head[p], 16)
            sp.dma_start(wo0[:], a["wo0"]).then_inc(ld_wo0, 16)
            sp.dma_start(wqk1[:], a["wqk1"]).then_inc(ld_w1, 16)
            sp.dma_start(w1s[:], a["w1s"]).then_inc(ld_w1, 16)
            for p in range(2):
                sp.dma_start(fc_w[:, p], a["fc_w"][p]).then_inc(ld_fc[p], 16)
                sp.dma_start(pj_w[:, p], a["pj_w"][p]).then_inc(ld_pj[p], 16)
                sp.dma_start(wqk2[:, p], a["wqk2"][p]).then_inc(ld_head2[p], 16)
            sp.dma_start(wv2[:], a["wv2"]).then_inc(ld_wv2, 16)
            sp.dma_start(fw1[:], a["fw1"]).then_inc(ld_wf, 16)
            sp.dma_start(fw2[:], a["fw2"]).then_inc(ld_wf, 16)
            sp.dma_start(fwo[:], a["fwo"]).then_inc(ld_wf, 16)
            sp.wait_ge(zero_ready, 1)
            sp.dma_start(x_dram[0:SLOTS, :].rearrange("(s p) c -> p s c", p=SH),
                         zero[:].unsqueeze(1).to_broadcast([SH, 2 * E, C])).then_inc(zeroed, 16)
            with nc.sync.Fori(0, PAIRS - 2) as pair:
                sp.wait_ge(proj_mm, count0(pair, 12, "mm"))
                for p in range(2):
                    h = pair * 2 + (4 + p)
                    sp.dma_start(wq_h[:, p], a["wq_h"][bass.ds(h, 1)].rearrange("o p k n -> (o p) k n")).then_inc(ld_head[p], 16)
                    sp.dma_start(wk_h[:, p], a["wk_h"][bass.ds(h, 1)].rearrange("o p n -> (o p) n")).then_inc(ld_head[p], 16)
            sp.wait_ge(scattered, 16 * 2 * NC_)
            x_rows = x_dram[0:SLOTS, :].rearrange("(e s p) c -> e p s c", e=E, s=2)
            y_rows = y_dram.rearrange("(e s p) c -> e p s c", e=E, s=2)
            for e in range(2):
                sp.dma_start(x_slot[:, e], x_rows[e]).then_inc(ld_slot[e], 16)
            for e in range(E):
                p = e % 2
                if e + 2 < E:
                    sp.wait_ge(hid_mm, FK * (e + 1))
                    sp.dma_start(x_slot[:, p], x_rows[e + 2]).then_inc(ld_slot[p], 16)
                    sp.dma_start(fc_w[:, p], a["fc_w"][e + 2]).then_inc(ld_fc[p], 16)
                    sp.wait_ge(out_mm, 2 * (e + 1))
                    sp.dma_start(pj_w[:, p], a["pj_w"][e + 2]).then_inc(ld_pj[p], 16)
                sp.wait_ge(ys_ready, 2 * (e + 1))
                sp.dma_start(y_rows[e], y_slot[:, p]).then_inc(st_slot[p], 16)
            for h in range(2, HEADS):
                sp.wait_ge(proj_mm, MM0 + count_a(h - 2))
                sp.dma_start(wqk2[:, h % 2], a["wqk2"][h]).then_inc(ld_head2[h % 2], 16)
            out_v = out.rearrange("b (i p) c -> p (b i) c", p=P)
            for ci in range(NC_):
                sp.wait_ge(h_ready, HR_OUT + ci + 1)
                sp.dma_start(out_v[:, ci], h_b[:, ci]).then_inc(stored, 16)
            sp.wait_ge(stored, 16 * NC_)

        @block.tensor
        def _(pe):
            mm = nc.tensor.matmul
            ident = cst["ident"]
            turned = [0]

            def turn(src, width_, dst_parts, groups, ready):
                for g, (fs, b) in enumerate(groups):
                    if ready is not None:
                        pe.wait_ge(norm_ready, ready + CI * (b + 1))
                    n = turned[0]
                    if g >= 4:
                        pe.wait_ge(turn_dve if n % 2 else turn_act, (n - 4) // 2 + 1)
                    for i in range(CI):
                        last = nc.tensor.transpose(turn_bank[n % 4][0:dst_parts, i * P:(i + 1) * P],
                                                   src[:, b * CI + i, fs], ident[0:P, 0:P])
                    last.then_inc(turn_mm, 1)
                    turned[0] += 1

            def wait_turned():
                pe.wait_ge(turn_act, turned[0] // 2)
                pe.wait_ge(turn_dve, turned[0] // 2)

            def turn_xn(ready):
                turn(xn, FC, FC, [(slice(k * FC, (k + 1) * FC), b) for b in range(B) for k in range(KC)], ready)
                wait_turned()

            def v_banks(w):
                for ci in range(NC_):
                    for k in range(KC):
                        last = mm(score_bank[ci // 2][0:P, (ci % 2) * C:(ci % 2 + 1) * C],
                                  x_t[:, k, ci * P:(ci + 1) * P], w(k), start=(k == 0), stop=(k == KC - 1))
                    if ci % 2:
                        last.then_inc(v_mm, 1)

            def transposes(n, t, causal, ready):
                i = t % CI
                pe.wait_ge(ready, n + 1)
                pe.wait_ge(pt_ready, n + 1)
                for j in range(width(causal, i) // P):
                    last = nc.tensor.transpose(pt_bank[t % 2][0:P, j * P:(j + 1) * P],
                                               probs[:, i, j * P:(j + 1) * P], ident[0:P, 0:P])
                last.then_inc(probs_turn, 1)

            def block_product(n, unit0, heads, v, d, causal):
                pe.wait_ge(pt_ready, n + 3)
                for jj in range(CI):
                    lo = jj * P if causal else 0
                    for j in range(heads):
                        last = mm(o_bank[d * j:d * (j + 1), lo:T], v(jj, j), probs_t[:, unit0 + j, jj, lo:T],
                                  start=(jj == 0), stop=(jj == CI - 1))
                last.then_inc(block_mm, 1)

            def turn_block(beta):
                pe.wait_ge(ot_ready, B * PAIRS + 1 + beta)
                for i in range(CI):
                    last = nc.tensor.transpose(o_bank[0:P, i * 128:(i + 1) * 128], o_t[:, i * P:(i + 1) * P], ident)
                last.then_inc(ot_turn, 1)

            pe.wait_ge(ld_tok, 32)
            for ci in range(NC_):
                mm(score_bank[ci // 2][0:P, (ci % 2) * C:(ci % 2 + 1) * C], tok_x[:, ci * P:(ci + 1) * P],
                   tok_w[:], start=True, stop=True).then_inc(tok_mm, 1)

            pe.wait_ge(ld_const, 16)
            pe.wait_ge(ld_w0, 32)
            turn_xn(0)
            for ci in range(NC_):
                for k in range(KC):
                    last = mm(o_bank[0:P, ci * D0:(ci + 1) * D0], x_t[:, k, ci * P:(ci + 1) * P], wdown[:, k],
                              start=(k == 0), stop=(k == KC - 1))
            last.then_inc(lat_mm, 1)

            def bank_free0(pair, m):
                if m in dve0:
                    pe.wait_ge(proj_dve, count0(pair, m, "dve"))
                else:
                    pe.wait_ge(proj_act, count0(pair, m, "act"))

            def proj0(pair, m):
                kind, b, p = pieces0[m]
                dst = proj_bank[m % 2]
                if m >= 2 and not (isinstance(pair, int) and pair < 0 and m < 4):
                    bank_free0(pair, m - 2)
                xs = slice(b * T, (b + 1) * T)
                if kind == "q":
                    pe.wait_ge(ld_head[p], 32 * pair + 64)
                    for k in range(KC):
                        last = mm(dst[:, 0:T], wq_h[:, p, k], x_t[:, k, xs], start=(k == 0), stop=(k == KC - 1))
                elif kind == "k":
                    last = mm(dst[:, 0:T], wk_h[:, p], c_t[:, xs], start=True, stop=True)
                elif kind == "d":
                    pe.wait_ge(proj_dve, count0(pair, pieces0.index(("k", b, p)), "dve"))
                    last = mm(dst[:, 0:T], cst["dup"], k_cs[:, p], start=True, stop=True)
                else:
                    for i in range(CI):
                        last = mm(dst[0:P, i * 128:(i + 1) * 128], c_t[:, tok(b, i)],
                                  wup_v[:, bass.ds(pair * 128, 128)], start=True, stop=True)
                last.then_inc(proj_mm, 1)

            def scores0(pair, t):
                b, p, i = t // BLOCK0, t % BLOCK0 // CI, t % CI
                if i == 0:
                    pe.wait_ge(proj_dve, count0(pair - 1, pieces0.index(("q", b, p)), "dve"))
                    pe.wait_ge(proj_act, count0(pair - 1, pieces0.index(("d", b, p)), "act"))
                w = P * (i + 1)
                mm(score_bank[i][0:P, 0:w], q_t[:, p, tok(b, i)], k_t[:, p, b * T:b * T + w],
                   start=True, stop=True).then_inc(scores_mm, 1)

            for b in range(B):
                pe.wait_ge(lat_ready, CI * (b + 1))
                for i in range(CI):
                    last = nc.tensor.transpose(pt_bank[b][0:D0, i * P:(i + 1) * P], c_n[:, b * CI + i, :], ident[0:P, 0:P])
                last.then_inc(lat_turn, 1)
            pe.wait_ge(ct_ready, B)
            for m in range(2, n0):
                proj0(-1, m)
            for t in range(AHEAD):
                scores0(0, t)

            def body0(pair, final):
                for t in range(BODY0):
                    n = pair * BODY0 + t
                    if t < 2:
                        bank_free0(pair - 1, n0 - 2 + t)
                    transposes(n, t, True, scaled)
                    todo = [m for m in at0.get(t, ()) if not final or pieces0[m][0] == "v"]
                    late = todo[1:] if t == BODY0 - 1 else []
                    for m in todo:
                        if m not in late:
                            proj0(pair, m)
                    if t + AHEAD < BODY0:
                        scores0(pair, t + AHEAD)
                    elif not final:
                        scores0(pair + 1, t + AHEAD - BODY0)
                    if t % BLOCK0 == BLOCK0 - 1:
                        b = t // BLOCK0
                        pe.wait_ge(proj_act, count0(pair, b, "act"))
                        block_product(n, 2 * b, 2, lambda jj, j: v_p[:, b * CI + jj, D0 * j:D0 * (j + 1)], D0, True)
                    for m in late:
                        proj0(pair, m)

            with nc.tensor.Fori(0, PAIRS - 1) as pair:
                body0(pair, False)
            body0(PAIRS - 1, True)

            pe.wait_ge(ot_ready, B * PAIRS)
            pe.wait_ge(ld_wo0, 16)
            for ci in range(NC_):
                for k in range(FK):
                    last = mm(score_bank[ci // 2][0:P, (ci % 2) * C:(ci % 2 + 1) * C],
                              o_0t[:, k, ci * P:(ci + 1) * P], wo0[:, k], start=(k == 0), stop=(k == FK - 1))
                last.then_inc(y_mm, 1)

            pe.wait_ge(ld_w1, 32)
            turn_xn(NC_)
            for m in range(2 * 2 * GROUPS):
                blk, b = divmod(m, 2)
                if m >= 4:
                    if m - 4 < 2 * GROUPS:
                        pe.wait_ge(q1_ready, m - 3)
                    else:
                        pe.wait_ge(k1_ready, m - 3 - 2 * GROUPS)
                for k in range(KC):
                    last = mm(turn_bank[m % 4][:, 0:T], wqk1[:, k, blk], x_t[:, k, b * T:(b + 1) * T],
                              start=(k == 0), stop=(k == KC - 1))
                last.then_inc(qk1_mm, 1)
            v_banks(lambda k: w1s[:, k, 0:C])

            def v_quad(b):
                return lambda jj, j: v_q[:, b * CI + jj, j, :]

            def end_block(n, beta, b, causal):
                pe.wait_ge(vq_ready, beta + 1)
                pe.wait_ge(o_ready, beta + 1)
                block_product(n, 4 * b, 4, v_quad(b), 32, causal)

            def scores1(quad, t):
                b, j, i = t // BLOCK, t % BLOCK // CI, t % CI
                if i == 0:
                    pe.wait_ge(qm_ready, quad * 8 + (4 * b + j + 1))
                w = P * (i + 1)
                mm(score_bank[i][0:P, 0:w], q_m[:, j, tok(b, i)],
                   k_1t[:, bass.ds(quad, 1), b * T:b * T + w].rearrange("p o n -> p (o n)"),
                   start=True, stop=True).then_inc(scores_mm, 1)

            pe.wait_ge(k1_ready, 2 * GROUPS)
            pe.wait_ge(v_dve, 3)
            for t in range(AHEAD):
                scores1(0, t)

            def body1(quad, final):
                for t in range(BODY):
                    n = quad * BODY + (STEPS + t)
                    beta = quad * B
                    transposes(n, t, True, probs_ready)
                    if t + AHEAD < BODY:
                        scores1(quad, t + AHEAD)
                    elif not final:
                        scores1(quad + 1, t + AHEAD - BODY)
                    if t == BLOCK - 1:
                        end_block(n, beta, 0, True)
                    if t == BLOCK + 1:
                        turn_block(beta)
                    if t == BODY - 1:
                        end_block(n, beta + 1, 1, True)
                        turn_block(beta + 1)

            with nc.tensor.Fori(0, QUADS - 1) as quad:
                body1(quad, False)
            body1(QUADS - 1, True)
            pe.wait_ge(o_ready, 1 + B * QUADS)
            turn(o_1, FC, FC, [(slice(k * FC, (k + 1) * FC), b) for b in range(B) for k in range(KC)], None)
            wait_turned()
            for ci in range(NC_):
                for k in range(KC):
                    last = mm(score_bank[ci // 2][0:P, (ci % 2) * C:(ci % 2 + 1) * C],
                              x_t[:, k, ci * P:(ci + 1) * P], w1s[:, k, C:2 * C], start=(k == 0), stop=(k == KC - 1))
                last.then_inc(y_mm, 1)

            turn_xn(2 * NC_)
            for ci in range(NC_):
                for k in range(KC):
                    last = mm(o_bank[0:P, ci * E:(ci + 1) * E], x_t[:, k, ci * P:(ci + 1) * P],
                              w1s[:, k, 2 * C:2 * C + E], start=(k == 0), stop=(k == KC - 1))
            last.then_inc(gate_mm, 1)
            pe.wait_ge(oh_ready, 1)
            ohf = oh[:].rearrange("p k c e -> p (k c e)")
            mm(score_bank[0][0:P, 0:2 * NC_ * E], before_bf[:], ohf, start=True, stop=True)
            mm(score_bank[1][0:P, 0:2 * NC_ * E], ones_bf[:], ohf, start=True, stop=True).then_inc(rank_mm, 1)

            def expert_hidden(e):
                p = e % 2
                pe.wait_ge(ld_slot[p], 16 * (e // 2 + 1))
                for k in range(KC):
                    for s in range(2):
                        last = nc.tensor.transpose(
                            pt_bank[p][0:FC, k * CAP + s * SH:k * CAP + (s + 1) * SH],
                            x_slot[:, p, s, k * FC:(k + 1) * FC], ident[0:SH, 0:SH])
                last.then_inc(slot_turn, 1)
                pe.wait_ge(slot_t_ready, e + 1)
                pe.wait_ge(ld_fc[p], 16 * (e // 2 + 1))
                for f in range(FK):
                    n = FK * e + f
                    if n >= 3:
                        pe.wait_ge(hid_ready, n - 2)
                    for k in range(KC):
                        last = mm(score_bank[n % 3][:, 0:CAP], fc_w[:, p, k, f * 128:(f + 1) * 128],
                                  x_slot_t[:, p, k], start=(k == 0), stop=(k == KC - 1))
                    last.then_inc(hid_mm, 1)

            def expert_out(e):
                p = e % 2
                pe.wait_ge(ld_pj[p], 16 * (e // 2 + 1))
                pe.wait_ge(hid_ready, FK * (e + 1))
                for s in range(2):
                    if e >= 1:
                        pe.wait_ge(ys_ready, 2 * e - 1 + s)
                    for f in range(FK):
                        last = mm(proj_bank[s][0:SH, 0:C], hid[:, p, f, s * SH:(s + 1) * SH], pj_w[:, p, f],
                                  start=(f == 0), stop=(f == FK - 1))
                    last.then_inc(out_mm, 1)

            for e in range(E):
                expert_hidden(e)
                if e:
                    expert_out(e - 1)
            expert_out(E - 1)

            turn_xn(3 * NC_)
            pe.wait_ge(ld_wv2, 16)
            v_banks(lambda k: wv2[:, k])

            def proj2(quad, m, count):
                kind, u, half = pieces2[m]
                j = u % 4
                dst = proj_bank[m % 2]
                if not (isinstance(count, int) and count < 3):
                    pe.wait_ge(proj_act, ACT0 - 2 + count)
                if kind == "a":
                    pe.wait_ge(ld_head2[j % 2], quad * 32 + 16 * (((4 if u >= 8 else 0) + j) // 2 + 1))
                    for d in range(KC):
                        for k in range(KC):
                            last = mm(dst[0:FC, d * C:(d + 1) * C], wqk2[:, j % 2, 0, k, d * FC:(d + 1) * FC],
                                      wqk2[:, j % 2, 1, k], start=(k == 0), stop=(k == KC - 1))
                else:
                    b = u % 8 // 4
                    if b == 0 and half == 0:
                        pe.wait_ge(proj_act, ACT0 - 1 + count)
                    for k in range(KC):
                        last = mm(dst[0:FC, 0:T], qk_2[:, j, k, half * FC:(half + 1) * FC],
                                  x_t[:, k, b * T:(b + 1) * T], start=(k == 0), stop=(k == KC - 1))
                last.then_inc(proj_mm, 1)

            def scores2(quad, t):
                b, u, i = t // BLOCK, t // CI, t % CI
                if i == 0:
                    z = ("z", u, 1) if u >= 2 else ("z", 8 + u, 1)
                    pe.wait_ge(proj_act, count2(quad if u >= 2 else quad - 1, pieces2.index(z)) + ACT0)
                for k in range(KC):
                    last = mm(score_bank[i][0:P, 0:T], z_t[:, u % 2, k, i * P:(i + 1) * P],
                              x_t[:, k, b * T:(b + 1) * T], start=(k == 0), stop=(k == KC - 1))
                last.then_inc(scores_mm, 1)

            for c, m in enumerate(m for m in range(n2) if pieces2[m][1] >= 8):
                proj2(-1, m, c + 1)
            pe.wait_ge(v_dve, 6)
            for t in range(AHEAD):
                scores2(0, t)

            def body2(quad, final):
                for t in range(BODY):
                    n = quad * BODY + (2 * STEPS + t)
                    beta = quad * B + B * QUADS
                    m = at2.get(t)
                    if m is not None and final and pieces2[m][1] >= 8:
                        m = None
                    late = t % BLOCK == BLOCK - 1
                    transposes(n, t, False, probs_ready)
                    if m is not None and not late:
                        proj2(quad, m, count2(quad, m))
                    if t + AHEAD < BODY:
                        scores2(quad, t + AHEAD)
                    elif not final:
                        scores2(quad + 1, t + AHEAD - BODY)
                    if late:
                        end_block(n, beta + t // BLOCK, t // BLOCK, False)
                    if m is not None and late:
                        proj2(quad, m, count2(quad, m))
                    if t == BLOCK + 1:
                        turn_block(beta)
                    if t == BODY - 1:
                        turn_block(beta + 1)

            with nc.tensor.Fori(0, QUADS - 1) as quad:
                body2(quad, False)
            body2(QUADS - 1, True)

            pe.wait_ge(ld_wf, 48)
            turn_xn(4 * NC_)
            for b in range(B):
                for k in range(KC):
                    last = mm(turn_bank[b][:, 0:T], fw1[:, k], x_t[:, k, b * T:(b + 1) * T],
                              start=(k == 0), stop=(k == KC - 1))
                last.then_inc(fh_mm, 1)
            for b in range(B):
                pe.wait_ge(fh_ready, b + 1)
                for k in range(KC):
                    if b == 1:
                        pe.wait_ge(fp_ready, k + 1)
                    mm(turn_bank[2 + k][0:FC, 0:T], fw2[:, k * FC:(k + 1) * FC], f_h[:, b * T:(b + 1) * T],
                       start=True, stop=True).then_inc(fp_mm, 1)
            pe.wait_ge(fp_ready, 2 * B)
            for ci in range(NC_):
                for k in range(KC):
                    last = mm(score_bank[ci // 2][0:P, (ci % 2) * C:(ci % 2 + 1) * C],
                              f_p[:, k, ci * P:(ci + 1) * P], fwo[:, k], start=(k == 0), stop=(k == KC - 1))
                last.then_inc(y_mm, 1)

        @block.scalar
        def _(act):
            turned = [0]
            norms = [0]

            def root():
                norms[0] += 1
                act.wait_ge(var_ready, norms[0])
                nc.scalar.activation(std[:], mv[:, :, 1], ACT.Sqrt, bias=cst["eps"][0:P], scale=1.0).then_inc(std_ready, 1)

            def take_turned(dst, count, w=None, bvec=None):
                for g in range(0, count, 2):
                    n = turned[0]
                    act.wait_ge(turn_mm, n + 1)
                    d = dst(g)
                    src = turn_bank[n % 4][0:d.shape[0], 0:T]
                    if w is None:
                        nc.scalar.copy(d, src).then_inc(turn_act, 1)
                    else:
                        k = g % KC
                        nc.scalar.activation(d, src, ACT.Identity, bias=bvec[0:FC, k:k + 1],
                                             scale=w[0:FC, k:k + 1]).then_inc(turn_act, 1)
                    turned[0] += 2

            def x_t_part(g):
                b, k = divmod(g, KC)
                return x_t[:, k, b * T:(b + 1) * T]

            def exps(n, i, causal, sums=False):
                w = width(causal, i)
                act.wait_ge(max_ready, n + 1)
                src, sign = (masked[:, i, 0:w], -1.0) if causal else (score_bank[i][0:P, 0:w], 1.0)
                if sums:
                    nc.scalar.activation(probs[:, i, 0:w], src, ACT.Exp, bias=nmax[:, i:i + 1], scale=sign,
                                         accum_out=rsum[:, i:i + 1]).then_inc(probs_ready, 1)
                else:
                    nc.scalar.activation(probs[:, i, 0:w], src, ACT.Exp, bias=nmax[:, i:i + 1],
                                         scale=sign).then_inc(probs_ready, 1)

            def copy_pt(n, t):
                i = t % CI
                act.wait_ge(probs_turn, n + 1)
                nc.scalar.copy(probs_t[:, t // CI, 0:i + 1, i * P:(i + 1) * P],
                               pt_bank[t % 2][0:P, 0:(i + 1) * P].rearrange("p (j l) -> p j l", l=P)).then_inc(pt_ready, 1)

            act.wait_ge(ld_const, 16)
            root()
            take_turned(x_t_part, 4)
            root()
            act.wait_ge(ld_cols, 16)
            for b in range(B):
                act.wait_ge(lat_turn, b + 1)
                nc.scalar.activation(c_t[:, b * T:(b + 1) * T], pt_bank[b][0:D0, 0:T], ACT.Identity,
                                     bias=col["lnb"][0:D0], scale=col["lng"][0:D0]).then_inc(ct_ready, 1)

            def take0(pair, m):
                kind, b, p = pieces0[m]
                act.wait_ge(proj_mm, count0(pair, m, "mm"))
                if kind == "d":
                    nc.scalar.copy(k_t[:, p, b * T:(b + 1) * T], proj_bank[m % 2][:, 0:T]).then_inc(proj_act, 1)
                else:
                    nc.scalar.copy(v_p[:, b * CI:(b + 1) * CI],
                                   proj_bank[m % 2][0:P, 0:CI * 128].rearrange("p (i d) -> p i d", i=CI)).then_inc(proj_act, 1)

            for m in act0[2:]:
                take0(-1, m)
            for t in range(AHEAD):
                exps(t, t, True, True)

            def body0(pair, final):
                for t in range(BODY0):
                    n = pair * BODY0 + t
                    copy_pt(n, t)
                    todo = [m for m in at0.get(t, ()) if m in act0 and (not final or pieces0[m][0] == "v")]
                    for m in todo:
                        if t < BODY0 - 1:
                            take0(pair, m)
                    if t + AHEAD < BODY0 or not final:
                        exps(n + AHEAD, t % CI, True, True)
                    if t % BLOCK0 == BLOCK0 - 1:
                        b = t // BLOCK0
                        act.wait_ge(block_mm, pair * B + (b + 1))
                        nc.scalar.copy(o_0t[:, bass.ds(pair, 1), b * T:(b + 1) * T].rearrange("p o n -> p (o n)"),
                                       o_bank[:, 0:T]).then_inc(ot_ready, 1)
                    for m in todo:
                        if t == BODY0 - 1:
                            take0(pair, m)

            with nc.scalar.Fori(0, PAIRS - 1) as pair:
                body0(pair, False)
            body0(PAIRS - 1, True)
            root()
            root()
            take_turned(x_t_part, 4, col["ln1w"], col["ln1b"])
            for m in range(2 * GROUPS):
                g, b = divmod(m, 2)
                act.wait_ge(qk1_mm, 2 * GROUPS + m + 1)
                nc.scalar.activation(k_1t[:, g, b * T:(b + 1) * T], turn_bank[(2 * GROUPS + m) % 4][:, 0:T],
                                     ACT.Identity, bias=col["qkb"][:, GROUPS + g:GROUPS + g + 1],
                                     scale=1.0).then_inc(k1_ready, 1)

            def take_block(beta):
                act.wait_ge(block_mm, B * PAIRS + 1 + beta)
                nc.scalar.copy(o_t[:], o_bank[:, 0:T]).then_inc(ot_ready, 1)

            for t in range(AHEAD):
                exps(STEPS + t, t, True)

            def body1(quad, final):
                for t in range(BODY):
                    n = quad * BODY + (STEPS + t)
                    if t + AHEAD < BODY or not final:
                        act.wait_ge(probs_turn, n + 1)
                        exps(n + AHEAD, t % CI, True)
                    if t % BLOCK == BLOCK - 1:
                        take_block(quad * B + t // BLOCK)

            with nc.scalar.Fori(0, QUADS - 1) as quad:
                body1(quad, False)
            body1(QUADS - 1, True)
            take_turned(x_t_part, 4)
            root()
            take_turned(x_t_part, 4)
            act.wait_ge(diff_ready, 1)
            nc.scalar.activation(eexp[:], ediff[:], ACT.Exp).then_inc(exp_ready, 1)
            for e in range(E):
                p = e % 2
                act.wait_ge(slot_turn, e + 1)
                nc.scalar.copy(flat(x_slot_t[:, p]), pt_bank[p][0:FC, 0:KC * CAP]).then_inc(slot_t_ready, 1)
                for f in range(FK):
                    n = FK * e + f
                    act.wait_ge(hid_mm, n + 1)
                    if e >= 2:
                        act.wait_ge(out_mm, 2 * (e - 1))
                    nc.scalar.activation(hid[:, p, f], score_bank[n % 3][:, 0:CAP], ACT.Gelu,
                                         bias=col["fcb"][:, n:n + 1], scale=1.0).then_inc(hid_ready, 1)
            root()
            take_turned(x_t_part, 4)

            def take2(m, count):
                kind, u, half = pieces2[m]
                act.wait_ge(proj_mm, count + MM0)
                src = proj_bank[m % 2]
                if kind == "a":
                    nc.scalar.copy(flat(qk_2[:, u % 4]), src[0:FC, 0:KC * C]).then_inc(proj_act, 1)
                else:
                    nc.scalar.copy(z_t[:, u % 2, half, :], src[0:FC, 0:T]).then_inc(proj_act, 1)

            for c, m in enumerate(m for m in range(n2) if pieces2[m][1] >= 8):
                take2(m, c + 1)
            for t in range(AHEAD):
                exps(2 * STEPS + t, t, False)

            def body2(quad, final):
                for t in range(BODY):
                    n = quad * BODY + (2 * STEPS + t)
                    m = at2.get(t)
                    if m is not None and final and pieces2[m][1] >= 8:
                        m = None
                    late = t % BLOCK == BLOCK - 1
                    if m is not None and not late:
                        take2(m, count2(quad, m))
                    if t + AHEAD < BODY or not final:
                        act.wait_ge(probs_turn, n + 1)
                        exps(n + AHEAD, t % CI, False)
                    if late:
                        take_block(quad * B + (B * QUADS + t // BLOCK))
                    if m is not None and late:
                        take2(m, count2(quad, m))

            with nc.scalar.Fori(0, QUADS - 1) as quad:
                body2(quad, False)
            body2(QUADS - 1, True)
            root()
            take_turned(x_t_part, 4)
            for b in range(B):
                act.wait_ge(fh_mm, b + 1)
                nc.scalar.activation(f_h[:, b * T:(b + 1) * T], turn_bank[b][:, 0:T], ACT.Relu,
                                     bias=col["fb1"], scale=1.0).then_inc(fh_ready, 1)
            for m in range(2 * B):
                b, k = divmod(m, KC)
                act.wait_ge(fp_mm, m + 1)
                nc.scalar.activation(f_p[:, k, b * T:(b + 1) * T], turn_bank[2 + k][0:FC, 0:T], ACT.Identity,
                                     bias=col["fb2"][0:FC, k:k + 1], scale=1.0).then_inc(fp_ready, 1)
            root()

        @block.vector
        def _(dve):
            own = [0]
            norms = [0]
            turned = [0]

            def step(ins):
                own[0] += 1
                ins.then_inc(dve_step, 1)
                dve.wait_ge(dve_step, own[0])

            def moments(src):
                for ci in range(NC_):
                    last = nc.vector.bn_stats(bn[:, ci], src[:, ci])
                step(last)
                for ci in range(NC_):
                    last = nc.vector.bn_aggr(mv[:, ci], bn[:, ci])
                last.then_inc(var_ready, 1)
                norms[0] += 1
                dve.wait_ge(std_ready, norms[0])
                step(nc.vector.reciprocal(rstd[:], std[:]))

            def normalise(dst, src, signal):
                for ci in range(NC_):
                    last = nc.vector.tensor_scalar(dst[:, ci], src[:, ci], mv[:, ci, 0:1], rstd[:, ci:ci + 1],
                                                   ALU.subtract, ALU.mult)
                    if signal is not None:
                        last.then_inc(signal, 1)
                return last

            def take_turned(dst, count, w=None, bvec=None):
                for g in range(1, count, 2):
                    n = turned[0] + 1
                    dve.wait_ge(turn_mm, n + 1)
                    d = dst(g)
                    src = turn_bank[n % 4][0:d.shape[0], 0:T]
                    if w is None:
                        nc.vector.tensor_copy(d, src).then_inc(turn_dve, 1)
                    else:
                        k = g % KC
                        nc.vector.tensor_scalar(d, src, w[0:FC, k:k + 1], bvec[0:FC, k:k + 1],
                                                ALU.mult, ALU.add).then_inc(turn_dve, 1)
                    turned[0] += 2

            def x_t_part(g):
                b, k = divmod(g, KC)
                return x_t[:, k, b * T:(b + 1) * T]

            def maxima(n, i):
                dve.wait_ge(scores_mm, n + 1)
                nc.vector.tensor_reduce(nmax[:, i:i + 1], score_bank[i][0:P, 0:T], AX.X, ALU.max,
                                        negate=True).then_inc(max_ready, 1)

            def masked_maxima(n, i, carrier=False):
                w = P * (i + 1)
                if carrier:
                    dve.wait_ge(scores_mm, n + 1)
                    nc.vector.memset(spare[:], 0.0).then_inc(small_dve, 1)
                nc.vector.tensor_tensor_reduce(masked[:, i, 0:w], score_bank[i][0:P, 0:w], cst["mask"][0:P, T - w:T],
                                               -1.0, 3e38, ALU.add, ALU.min, nmax[:, i:i + 1]).then_inc(max_ready, 1)

            def scale(n, i):
                dve.wait_ge(probs_ready, n + 1)
                nc.vector.reciprocal(rinv0[:, i:i + 1], rsum[:, i:i + 1]).then_inc(small_dve, 1)
                first, last = isinstance(n, int) and n == 0, isinstance(n, int) and n == STEPS - 1
                dve.wait_ge(small_dve, 1 if first else 2 * n - 1 if last else 2 * n)
                w = P * (i + 1)
                nc.vector.tensor_scalar(probs[:, i, 0:w], probs[:, i, 0:w], rinv0[:, i:i + 1], None,
                                        ALU.mult).then_inc(scaled, 1)

            def copy_pt(n, t, causal):
                i = t % CI
                k = i + 1 if causal else CI
                dve.wait_ge(probs_turn, n + 1)
                nc.vector.tensor_copy(probs_t[:, t // CI, 0:k, i * P:(i + 1) * P],
                                      pt_bank[t % 2][0:P, 0:k * P].rearrange("p (j l) -> p j l", l=P)).then_inc(pt_ready, 1)

            def divide(beta, quad, b):
                sums = o_bank[0:P, 0:CI * 128].rearrange("p (i j d) -> p i j d", i=CI, j=4)
                dve.wait_ge(ot_turn, beta + 1)
                nc.vector.reciprocal(rinv[:], sums[:, :, :, D1]).then_inc(rsum_inv, 1)
                dve.wait_ge(rsum_inv, beta + 1)
                nc.vector.tensor_tensor(
                    o_1[:, b * CI:(b + 1) * CI, bass.ds(quad * 64, 64)].rearrange("p i (j d) -> p i j d", j=4),
                    sums[:, :, :, 0:D1], rinv[:].unsqueeze(3).to_broadcast([P, CI, 4, D1]), ALU.mult).then_inc(o_ready, 1)

            def add_banks(dst, other, mm_sem, first, ready, each):
                for k in range(3):
                    dve.wait_ge(mm_sem, first + (2 * (k + 1) if each else k + 1))
                    last = nc.vector.tensor_tensor(
                        dst[:, 2 * k:2 * k + 2],
                        score_bank[k][0:P, 0:2 * C].rearrange("p (a c) -> p a c", a=2), other(k), ALU.add)
                    last.then_inc(ready, 1)

            dve.wait_ge(ld_base, 16)
            add_banks(h_a, lambda k: base[:, 2 * k:2 * k + 2], tok_mm, 0, h_ready, True)
            dve.wait_ge(h_ready, 3)
            moments(h_a)
            normalise(xn, h_a, norm_ready)
            take_turned(x_t_part, 4)
            nc.vector.tensor_copy(before_bf[:], cst["before"][0:P]).then_inc(o_ready, 1)
            nc.vector.tensor_copy(ones_bf[:], cst["ones"][0:P]).then_inc(pt_ready, 2)
            dve.wait_ge(lat_mm, 1)
            lat = o_bank[0:P, 0:NC_ * D0].rearrange("p (c d) -> p c d", c=NC_)
            moments(lat)
            normalise(c_n, lat, lat_ready)

            def rope(pair, m):
                kind, b, p = pieces0[m]
                dve.wait_ge(proj_mm, count0(pair, m, "mm"))
                src = proj_bank[m % 2][:, 0:T]
                if kind == "q":
                    nc.vector.tensor_tensor(q_t[:, p, b * T:(b + 1) * T], src, cst["cos_sin_q"], ALU.mult).then_inc(proj_dve, 1)
                else:
                    nc.vector.tensor_tensor(k_cs[:, p], src, cst["cos_sin_k"], ALU.mult).then_inc(proj_dve, 1)

            for m in dve0:
                rope(-1, m)
            dve.wait_ge(scores_mm, AHEAD)
            for t in range(AHEAD):
                masked_maxima(t, t)
            scale(0, 0)

            def body0(pair, final):
                for t in range(BODY0):
                    n = pair * BODY0 + t
                    if not (final and t == BODY0 - 1):
                        scale(n + 1, (t + 1) % CI)
                    if not final:
                        for m in at0.get(t, ()):
                            if m in dve0:
                                rope(pair, m)
                    if t + AHEAD < BODY0 or not final:
                        masked_maxima(n + AHEAD, t % CI, True)

            with nc.vector.Fori(0, PAIRS - 1) as pair:
                body0(pair, False)
            body0(PAIRS - 1, True)
            dve.wait_ge(hb_ready, 1)
            add_banks(h_a, lambda k: h_b[:, 2 * k:2 * k + 2], y_mm, 0, h_ready, True)
            dve.wait_ge(h_ready, 6)
            moments(h_a)
            step(normalise(g_a, h_a, None))
            moments(g_a)
            normalise(xn, g_a, norm_ready)
            take_turned(x_t_part, 4, col["ln1w"], col["ln1b"])
            for m in range(2 * GROUPS):
                g, b = divmod(m, 2)
                dve.wait_ge(qk1_mm, m + 1)
                nc.vector.tensor_scalar(q_1t[:, g, b * T:(b + 1) * T], turn_bank[m % 4][:, 0:T],
                                        col["qkb"][:, g:g + 1], D1 ** -0.5, ALU.add, ALU.mult).then_inc(q1_ready, 1)
            add_banks(v_1, lambda k: row["vb"].unsqueeze(1).to_broadcast([P, 2, C]), v_mm, 0, v_dve, False)
            dve.wait_ge(scores_mm, STEPS + AHEAD)
            for t in range(AHEAD):
                masked_maxima(STEPS + t, t)

            def body1(quad, final):
                for t in range(BODY):
                    n = quad * BODY + (STEPS + t)
                    more = t + AHEAD < BODY or not final
                    if more:
                        dve.wait_ge(scores_mm, n + (AHEAD + 1))
                    copy_pt(n, t, True)
                    if more:
                        masked_maxima(n + AHEAD, t % CI)
                    if t == BLOCK + 1:
                        divide(quad * B, quad, 0)
                    if t == BODY - 1:
                        divide(quad * B + 1, quad, 1)

            with nc.vector.Fori(0, QUADS - 1) as quad:
                body1(quad, False)
            body1(QUADS - 1, True)
            take_turned(x_t_part, 4)
            dve.wait_ge(hb_ready, 2)
            add_banks(g_a, lambda k: h_b[:, 2 * k:2 * k + 2], y_mm, NC_, h_ready, True)
            dve.wait_ge(h_ready, 9)
            moments(g_a)
            for ci in range(NC_):
                last = nc.vector.scalar_tensor_tensor(xn[:, ci], g_a[:, ci], mv[:, ci, 0:1], row["ln2w"],
                                                      ALU.subtract, ALU.mult)
            step(last)
            for ci in range(NC_):
                nc.vector.scalar_tensor_tensor(xn[:, ci], xn[:, ci], rstd[:, ci:ci + 1], row["ln2b"],
                                               ALU.mult, ALU.add).then_inc(norm_ready, 1)
            take_turned(x_t_part, 4)

            dve.wait_ge(gate_mm, 1)
            step(nc.vector.tensor_copy(flat(lg[:]), o_bank[0:P, 0:NC_ * E]))
            for ci in range(NC_):
                last = nc.vector.max(m8[:, ci], lg[:, ci])
            step(last)
            nc.vector.tensor_tensor(ediff[:], m8[:, :, 1], m8[:, :, 0], ALU.subtract).then_inc(diff_ready, 1)
            for ci in range(NC_):
                last = nc.vector.max_index(i8[:, ci], m8[:, ci], lg[:, ci])
            step(last)
            step(nc.vector.tensor_copy(i8f[:], i8[:, :, 0:2].rearrange("p c k -> p k c")))
            ex = cst["expert"][0:P].unsqueeze(1).to_broadcast([P, 2 * NC_, E])
            oh12 = oh[:].rearrange("p k c e -> p (k c) e")
            i8f12 = flat(i8f[:])
            nc.vector.tensor_tensor(oh12, ex, i8f12.unsqueeze(2).to_broadcast([P, 2 * NC_, E]),
                                    ALU.is_equal).then_inc(oh_ready, 1)
            dve.wait_ge(rank_mm, 1)
            step(nc.vector.tensor_copy(tot[:], score_bank[1][0:P, 0:96].rearrange("p (b e) -> p e b", e=E)))
            step(nc.vector.tensor_tensor_scan(flat(run[:]), cst["restart"][0:P], flat(tot[:]), 0.0, ALU.mult, ALU.add))
            step(nc.vector.tensor_tensor(run[:], run[:], tot[:], ALU.subtract))
            step(nc.vector.tensor_tensor(rk[:], score_bank[0][0:P, 0:96].rearrange("p (b e) -> p b e", e=E),
                                         run[:].rearrange("p e b -> p b e"), ALU.add))
            step(nc.vector.tensor_tensor(rk[:], rk[:], oh12, ALU.mult))
            step(nc.vector.tensor_reduce(small["rank"][:], rk[:], AX.X, ALU.add))
            nc.vector.tensor_scalar(small["keep"][:], small["rank"][:], float(CAP), None, ALU.is_lt)
            step(nc.vector.scalar_tensor_tensor(small["slot"][:], i8f12, float(CAP), small["rank"][:],
                                                ALU.mult, ALU.add))
            step(nc.vector.tensor_tensor(small["off"][:], small["slot"][:], cst["dump"][0:P], ALU.subtract))
            step(nc.vector.tensor_tensor(small["off"][:], small["off"][:], small["keep"][:], ALU.mult))
            nc.vector.tensor_tensor(scat[:], small["off"][:], cst["dump"][0:P], ALU.add).then_inc(place_ready, 1)
            nc.vector.tensor_tensor(gath[:], small["slot"][:], small["keep"][:], ALU.mult).then_inc(place_ready, 1)
            dve.wait_ge(exp_ready, 1)
            step(nc.vector.tensor_scalar(eden[:], eexp[:], 1.0, None, ALU.add))
            step(nc.vector.reciprocal(small["w"][:, 0:NC_], eden[:]))
            step(nc.vector.tensor_tensor(small["w"][:, NC_:2 * NC_], small["w"][:, 0:NC_], eexp[:], ALU.mult))
            step(nc.vector.tensor_tensor(small["w"][:], small["w"][:], small["keep"][:], ALU.mult))
            for e in range(E):
                for s in range(2):
                    dve.wait_ge(out_mm, 2 * e + s + 1)
                    if e >= 2:
                        dve.wait_ge(st_slot[e % 2], 16 * (e // 2))
                    nc.vector.tensor_tensor(y_slot[:, e % 2, s], proj_bank[s][0:SH, 0:C],
                                            row["pjb"][0:SH, e * C:(e + 1) * C], ALU.add).then_inc(ys_ready, 1)
            dve.wait_ge(hb_ready, 3)
            dve.wait_ge(gathered, 16 * 2 * NC_)
            for ci in range(NC_):
                last = nc.vector.scalar_tensor_tensor(h_b[:, ci], y_tok[:, ci], small["w"][:, ci:ci + 1],
                                                      h_b[:, ci], ALU.mult, ALU.add)
            step(last)
            for ci in range(NC_):
                last = nc.vector.scalar_tensor_tensor(h_a[:, ci], y_tok[:, NC_ + ci], small["w"][:, NC_ + ci:NC_ + ci + 1],
                                                      h_b[:, ci], ALU.mult, ALU.add)
            step(last)

            moments(h_a)
            normalise(xn, h_a, norm_ready)
            take_turned(x_t_part, 4)
            for k in range(3):
                dve.wait_ge(v_mm, 3 + k + 1)
                nc.vector.tensor_copy(v_1[:, 2 * k:2 * k + 2],
                                      score_bank[k][0:P, 0:2 * C].rearrange("p (a c) -> p a c", a=2)).then_inc(v_dve, 1)
            for t in range(AHEAD):
                maxima(2 * STEPS + t, t)

            def body2(quad, final):
                for t in range(BODY):
                    n = quad * BODY + (2 * STEPS + t)
                    copy_pt(n, t, False)
                    if t + AHEAD < BODY or not final:
                        maxima(n + AHEAD, t % CI)
                    if t == BLOCK + 1:
                        divide(quad * B + B * QUADS, quad, 0)
                    if t == BODY - 1:
                        divide(quad * B + (B * QUADS + 1), quad, 1)

            with nc.vector.Fori(0, QUADS - 1) as quad:
                body2(quad, False)
            body2(QUADS - 1, True)
            dve.wait_ge(o_ready, 1 + 2 * B * QUADS)
            step(nc.vector.tensor_tensor(h_a[:], h_a[:], o_1[:], ALU.add))
            moments(h_a)
            normalise(xn, h_a, norm_ready)
            take_turned(x_t_part, 4)
            add_banks(g_a, lambda k: row["bo1"].unsqueeze(1).to_broadcast([P, 2, C]), y_mm, 2 * NC_, h_ready, True)
            dve.wait_ge(h_ready, 12)
            nc.vector.tensor_tensor(h_b[:], h_a[:], row["beta"].unsqueeze(1).to_broadcast([P, NC_, C]), ALU.add)
            moments(g_a)
            for ci in range(NC_):
                last = nc.vector.scalar_tensor_tensor(g_a[:, ci], g_a[:, ci], mv[:, ci, 0:1], row["gamma"],
                                                      ALU.subtract, ALU.mult)
            step(last)
            for ci in range(NC_):
                nc.vector.scalar_tensor_tensor(h_b[:, ci], g_a[:, ci], rstd[:, ci:ci + 1], h_b[:, ci],
                                               ALU.mult, ALU.add).then_inc(h_ready, 1)

        @block.gpsimd
        def _(pool):
            nc.gpsimd.memset(zero[:], 0.0).then_inc(zero_ready, 1)
            nc.gpsimd.memset(v_q[:], 0.0).then_inc(vq_set, 1)
            pool.wait_ge(vq_set, 1)
            nc.gpsimd.memset(v_q[:, :, :, D1:D1 + 1], 1.0).then_inc(vq_set, 1)
            pool.wait_ge(ld_rows, 16)
            pool.wait_ge(h_ready, 3)
            nc.gpsimd.tensor_tensor(h_b[:], h_a[:], row["bo0"].unsqueeze(1).to_broadcast([P, NC_, C]),
                                    ALU.add).then_inc(hb_ready, 1)
            pool.wait_ge(block_mm, B * PAIRS)
            nc.gpsimd.memset(qk_space[:], 0.0).then_inc(qm_zero, 1)
            pool.wait_ge(norm_ready, 2 * NC_)
            nc.gpsimd.tensor_tensor(h_b[:], g_a[:], row["projb"].unsqueeze(1).to_broadcast([P, NC_, C]),
                                    ALU.add).then_inc(hb_ready, 1)

            def fill_vq(beta, quad, b):
                if beta >= B:
                    pool.wait_ge(block_mm, B * PAIRS + beta - B + 1)
                nc.gpsimd.tensor_copy(
                    v_q[:, b * CI:(b + 1) * CI, :, 0:D1],
                    v_1[:, b * CI:(b + 1) * CI, quad * 64:(quad + 1) * 64].rearrange("p i (j d) -> p i j d", j=4)
                ).then_inc(vq_ready, 1)

            pool.wait_ge(qm_zero, 1)
            pool.wait_ge(vq_set, 2)
            for quad in range(QUADS):
                for b in range(B):
                    pool.wait_ge(q1_ready, 2 * quad + b + 1)
                    for j in range(4):
                        if quad:
                            pool.wait_ge(scores_mm, STEPS + (quad - 1) * BODY + b * BLOCK + (j + 1) * CI)
                        if j:
                            pool.wait_ge(qm_ready, (quad * B + b) * 4 + j)
                        elif quad or b:
                            pool.wait_ge(vq_ready, quad * B + b)
                        else:
                            pool.wait_ge(hb_ready, 2)
                        rows_j = slice(32 * j, 32 * j + 32)
                        nc.gpsimd.tensor_copy(q_m[rows_j, j, b * T:(b + 1) * T],
                                              q_1t[rows_j, quad, b * T:(b + 1) * T]).then_inc(qm_ready, 1)
                    if quad == 0:
                        pool.wait_ge(v_dve, 3)
                    pool.wait_ge(qm_ready, (quad * B + b + 1) * 4)
                    fill_vq(quad * B + b, quad, b)
            pool.wait_ge(h_ready, 9)
            pool.wait_ge(zeroed, 16)
            pool.wait_ge(place_ready, 2)
            for k in range(2):
                for ci in range(NC_):
                    m = k * NC_ + ci
                    nc.gpsimd.indirect_dma_start(
                        x_dram, bass.IndirectOffsetOnAxis(ap=scat[:, m:m + 1].bitcast(U32), axis=0), xn[:, ci], None
                    ).then_inc(scattered, 16)
            nc.gpsimd.tensor_tensor(h_b[:], h_a[:], g_a[:], ALU.add).then_inc(hb_ready, 1)
            for p in range(2):
                pool.wait_ge(st_slot[p], 16 * (E // 2))
            for m in range(2 * NC_):
                nc.gpsimd.indirect_dma_start(
                    y_tok[:, m], None, y_dram, bass.IndirectOffsetOnAxis(ap=gath[:, m:m + 1].bitcast(U32), axis=0)
                ).then_inc(gathered, 16)
            pool.wait_ge(v_dve, 6)
            for quad in range(QUADS):
                for b in range(B):
                    fill_vq((QUADS + quad) * B + b, quad, b)



HR_OUT = 12


def rope_tables():
    import numpy as np
    inv = (np.float32(1.0) / np.float32(10000.0) ** (np.arange(0, D0, 2, dtype=np.float32) / np.float32(D0))).astype(np.float32)
    ang = (np.arange(T, dtype=np.float32)[:, None] * inv[None, :]).astype(np.float32)
    cos, sin = np.cos(ang).T, np.sin(ang).T
    return np.concatenate([cos, cos, -sin, sin], axis=0).astype(np.float32)


def constants():
    import numpy as np
    c = np.zeros((128, CONST_N), np.float32)

    def put(name, v):
        lo, hi = CONST_AT[name]
        c[:v.shape[0], lo:hi] = v

    put("ident", np.eye(128))
    put("dup", np.tile(np.eye(D0), (2, 2)))
    table = rope_tables()
    put("cos_sin_q", table * np.float32(D0 ** -0.5))
    put("cos_sin_k", table)
    t = np.arange(P)
    put("before", (t[:, None] < t[None, :]).astype(np.float32))
    put("ones", np.ones((P, P)))
    mask = np.zeros((P, T), np.float32)
    mask[:, T - P:] = np.where(t[None, :] > t[:, None], -1e30, 0.0)
    put("mask", mask)
    put("expert", np.tile(np.arange(E), (P, 1)))
    put("dump", SLOTS + np.arange(2 * NC_)[None, :] * P + t[:, None])
    put("restart", np.tile((np.arange(E * 2 * NC_) % (2 * NC_) != 0).astype(np.float32), (P, 1)))
    put("eps", np.full((128, 1), EPS))
    return c


def lay_out(i):
    import numpy as np
    i = {k: np.asarray(v) for k, v in i.items()}
    z = np.zeros

    def chunked(w):
        return w.reshape(KC, FC, -1).transpose(1, 0, 2)

    def token_major(x):
        return x.reshape(B, CI, P, -1).transpose(2, 0, 1, 3).reshape(P, NC_, -1)

    def columns(v):
        return v.reshape(KC, FC).T

    f32 = np.float32
    x = i["x"].reshape(B, 3, 16, 4, 16, 4).transpose(0, 1, 2, 4, 3, 5).reshape(B, 256, PATCH)
    tok_x = z((PATCH + 1, B, T), f32)
    tok_x[:PATCH, :, :256] = x.transpose(2, 0, 1)
    tok_x[PATCH, :, :256] = 1.0
    base = z((B, T, C), f32)
    base[:, :256] = i["L0_tok_pos"][None]
    base[:, 256:] = i["txt"]
    rot = np.concatenate([np.arange(32, 64), np.arange(0, 32)])
    wq = i["L0_attn_Wq"].reshape(C, HEADS, D0)
    wq = np.concatenate([wq, wq[:, :, rot]], axis=2).reshape(KC, FC, HEADS, 128).transpose(2, 1, 0, 3)
    wk = i["L0_attn_Wup"][:, :FF].reshape(D0, HEADS, D0)
    wk = np.concatenate([wk, wk[:, :, rot]], axis=2).transpose(1, 0, 2)
    qkv = i["L0_ffn_attn_qkv_w"]
    qkvb = i["L0_ffn_attn_qkv_b"]
    wqk1 = z((C, 2, GROUPS, 4, 32), f32)
    wqk1[..., :D1] = qkv[:, :2 * C].reshape(C, 2, GROUPS, 4, D1)
    qkb = z((2, GROUPS, 4, 32), f32)
    qkb[..., :D1] = qkvb[:2 * C].reshape(2, GROUPS, 4, D1)
    cols = z((128, COLS_N), f32)

    def put(name, v):
        lo, hi = COLS_AT[name]
        cols[:v.shape[0], lo:hi] = v

    put("lng", i["L0_attn_ln_g"][:, None])
    put("lnb", i["L0_attn_ln_b"][:, None])
    put("ln1w", columns(i["L0_ffn_ln1_w"]))
    put("ln1b", columns(i["L0_ffn_ln1_b"]))
    put("qkb", qkb.reshape(2 * GROUPS, 128).T)
    put("fb1", i["L1_ffn_b1"][:, None])
    put("fb2", columns(i["L1_ffn_b2"]))
    put("fcb", i["L0_ffn_exp_fc_b"].reshape(E, FK, 128).transpose(2, 0, 1).reshape(128, E * FK))
    rows = np.concatenate([i[k].reshape(-1) for k in (
        "L0_attn_bo", "L0_ffn_attn_proj_b")] + [qkvb[2 * C:]] + [i[k].reshape(-1) for k in (
            "L0_ffn_ln2_w", "L0_ffn_ln2_b", "L1_ffn_bo", "L1_ffn_gamma", "L1_ffn_beta", "L0_ffn_exp_proj_b")])
    a = dict(
        tok_x=tok_x.reshape(PATCH + 1, N),
        tok_w=np.concatenate([i["L0_tok_W"].T, i["L0_tok_b"][None]], axis=0),
        base=token_major(base),
        const=constants(),
        cols=cols,
        rows=rows,
        wdown=chunked(i["L0_attn_Wdown"]),
        wup_v=i["L0_attn_Wup"][:, FF:],
        wq_h=wq, wk_h=wk,
        wo0=i["L0_attn_Wo"].reshape(FK, 128, C).transpose(1, 0, 2),
        wqk1=chunked(wqk1.reshape(C, -1)).reshape(FC, KC, 2 * GROUPS, 128),
        w1s=np.concatenate([chunked(qkv[:, 2 * C:]), chunked(i["L0_ffn_attn_proj_w"]), chunked(i["L0_ffn_w_g"])], axis=2),
        fc_w=i["L0_ffn_exp_fc_w"].reshape(E, KC, FC, FF).transpose(0, 2, 1, 3),
        pj_w=i["L0_ffn_exp_proj_w"].reshape(E, FK, 128, C).transpose(0, 2, 1, 3),
        wqk2=np.stack([i["L1_attn_q"], i["L1_attn_k"]], axis=1).reshape(HEADS, 2, KC, FC, C).transpose(0, 3, 1, 2, 4),
        wv2=chunked(i["L1_attn_v"].reshape(C, C).T),
        fw1=chunked(i["L1_ffn_W1"].T),
        fw2=i["L1_ffn_W2"].T,
        fwo=chunked(i["L1_ffn_Wo"].T),
    )
    return {k: np.ascontiguousarray(v) for k, v in a.items()}


def kernel(**inputs):
    import concourse.bacc as _bacc
    from concourse import mybir as _mybir
    from concourse.bass_utils import run_bass_kernel_spmd as _run

    arrays = lay_out(inputs)
    nc = _bacc.Bacc("TRN2", target_bir_lowering=False, num_devices=1)
    aps = {k: nc.dram_tensor("in_" + k, v.shape, _mybir.dt.from_np(v.dtype), kind="ExternalInput").ap() for k, v in arrays.items()}
    out = nc.dram_tensor("out", (B, T, C), F32, kind="ExternalOutput").ap()
    build(nc, aps, out)
    r = _run(nc, [{"in_" + k: v for k, v in arrays.items()}], core_ids=[0])
    return r.results[0]["out"]
```

```python
from contextlib import ExitStack

import concourse.bass as bass
from concourse import mybir

F32 = mybir.dt.float32
BF16 = mybir.dt.bfloat16
I32 = mybir.dt.int32
U32 = mybir.dt.uint32
ALU = mybir.AluOpType
ACT = mybir.ActivationFunctionType
AX = mybir.AxisListType

B, T, C = 2, 333, 192
N = B * T
P = 111
CI = T // P
NC_ = B * CI
FC = 96
KC = C // FC
HEADS = 12
PAIRS = HEADS // 2
SPH = B * CI
STEPS = HEADS * SPH
AHEAD = CI
QUADS = HEADS // 4
BLOCK0, BLOCK = 2 * CI, 4 * CI
BODY0, BODY = B * BLOCK0, B * BLOCK
D0 = 64
D1 = 16
LAG = 2
PEEL = LAG + 2
PATCH = 48
E, CAP = 8, 208
FF = 768
FK = FF // 128
SH = CAP // 2
SLOTS = E * CAP
ROW = C + 1
INNER = 128
QK_AHEAD = 4
EPS = 1e-5

CONST_W = dict(ident=128, cos_sin_q=2 * T, cos_sin_k=2 * T, before=P, ones=P, rows16=8, mask=T, expert=E,
               dump=2 * NC_, home=2 * NC_, restart=E * 2 * NC_)
COLS_W = dict(lng=1, lnb=1, ln1w=KC, ln1b=KC, ln2w=KC, ln2b=KC, qkb=4, fb1=1, fb2=KC, fcb=E * FK)
ROWS_W = dict(bo0=C, projb=C, vb=C, ln2w=C, ln2b=C, bo1=C, gamma=C, beta=C, pjb=E * C)


def offsets(widths):
    at, out = 0, {}
    for name, w in widths.items():
        out[name] = (at, at + w)
        at += w
    return out, at


CONST_AT, CONST_N = offsets(CONST_W)
COLS_AT, COLS_N = offsets(COLS_W)
ROWS_AT, ROWS_N = offsets(ROWS_W)


def build(nc, a, out):
    ctx = ExitStack()
    with ctx:
        def sb(name, shape, dt=F32):
            return ctx.enter_context(nc.sbuf_tensor(name, shape, dt))

        def sem(name):
            return ctx.enter_context(nc.semaphore(name))

        bank = [ctx.enter_context(nc.psum_tensor(f"bank{i}", [128, 512], F32)) for i in range(8)]
        score_bank, pt_bank, o_bank, proj_bank = bank[0:3], bank[3:5], bank[5], bank[6:8]
        turn_bank = [pt_bank[0], pt_bank[1], proj_bank[0], proj_bank[1]]

        const = sb("consts", [128, CONST_N])
        cols = sb("cols", [128, COLS_N])
        rows = sb("rows", [P, ROWS_N])
        cst = {k: const[:, lo:hi] for k, (lo, hi) in CONST_AT.items()}
        col = {k: cols[:, lo:hi] for k, (lo, hi) in COLS_AT.items()}
        row = {k: rows[:, lo:hi] for k, (lo, hi) in ROWS_AT.items()}
        before_bf = sb("before_bf", [P, P], BF16)
        ones_bf = sb("ones_bf", [P, P], BF16)
        tok_x = sb("tok_x", [PATCH + 1, N])
        tok_w = sb("tok_w", [PATCH + 1, C])
        h_a = sb("h_a", [P, NC_, C])
        h_b = sb("h_b", [P, NC_, C])
        g_a = sb("g_a", [P, NC_, C])
        xn = sb("xn", [P, NC_, C])
        x_t = sb("x_t", [FC, KC, N])
        bn = sb("bn", [P, NC_, 6])
        mv = sb("mv", [P, NC_, 2])
        std = sb("std", [P, NC_])
        rstd = sb("rstd", [P, NC_])
        var_2 = sb("var_2", [P, NC_])
        rstd_2 = sb("rstd_2", [P, NC_])
        eps = sb("eps", [P, 1])
        wdown = sb("wdown", [FC, KC, D0])
        up_space = sb("up_space", [128, HEADS * D0])
        wup_v = up_space[0:D0, :]
        fw_out, bias_out = up_space[:, 0:C], up_space[0:P, C:2 * C]
        c_n = sb("c_n", [P, NC_, D0])
        c_t = sb("c_t", [D0, N])
        wq_h = sb("wq_h", [FC, 2, KC, 128])
        wk_h = sb("wk_h", [D0, 2, 128])
        wide = sb("wide", [128, (FK + 4) * N])
        wide_a, wide_b = wide[:, 0:FK * N], wide[:, FK * N:(FK + 4) * N]
        q_t = wide_b[:, 0:2 * N].rearrange("p (s n) -> p s n", s=2)
        k_t = wide_b[:, 2 * N:3 * N]
        rope_q = wide_b[:, 3 * N:4 * N].rearrange("p (s n) -> p s n", s=2)
        q_m = wide_b.rearrange("p (s n) -> p s n", s=4)
        rope_k = sb("rope_k", [128, 2, T])
        wo0 = sb("wo0", [128, FK, C])
        o_0t = wide_a.rearrange("p (k n) -> p k n", k=FK)
        q_1t = wide_a[:, 0:2 * N].rearrange("p (g n) -> p g n", g=2)
        k_1t = wide_a[:, 2 * N:(2 + QUADS) * N].rearrange("p (g n) -> p g n", g=QUADS)
        qk_all = wide[0:FC, 0:HEADS * KC * C].rearrange("p (s n) -> p s n", s=HEADS)
        qk_2 = wide[0:FC, HEADS * KC * C:(HEADS + 4) * KC * C].rearrange("p (s k n) -> p s k n", s=2, k=KC)
        f_h = wide_a[0:INNER, 0:N]
        v_p = sb("v_p", [P, NC_, 2 * D0])
        v_q = sb("v_q", [P, NC_, 4, 32])
        pt_ring = sb("pt_ring", [P, 8 * CI * T])
        probs_t = pt_ring[:].rearrange("p (u j l) -> p u j l", u=8, j=CI)
        base = pt_ring[:, 0:NC_ * C].rearrange("p (c n) -> p c n", c=NC_)
        o_t = sb("o_t", [128, T])
        masked = sb("masked", [P, CI, T])
        v_1 = sb("v_1", [P, NC_, C])
        o_1 = sb("o_1", [P, NC_, C])
        probs = sb("probs", [P, 3, T])
        nmax = sb("nmax", [P, CI])
        rsum = sb("rsum", [P, CI])
        rinv0 = sb("rinv0", [P, CI])
        spare = sb("spare", [1, CI])
        rinv = sb("rinv", [P, CI, 4])
        wqk1 = sb("wqk1", [FC, KC, 3, 128])
        w1s = sb("w1s", [FC, KC, 2 * C + E])
        fc_space = sb("fc_space", [128, 2 * KC * FF])
        fc_w = fc_space[0:FC, :].rearrange("p (s k f) -> p s k f", s=2, k=KC)
        pj_w = sb("pj_w", [128, 2, FK, C])
        x_w = fc_space[:, 0:4 * N].rearrange("p (s n) -> p s n", s=4)
        lg = sb("lg", [P, NC_, E])
        m8 = sb("m8", [P, NC_, 8])
        i8 = sb("i8", [P, NC_, 8], U32)
        i8f = sb("i8f", [P, 2, NC_])
        oh = sb("oh", [P, 2, NC_, E], BF16)
        tot = sb("tot", [P, E, 2 * NC_])
        run = sb("run", [P, E, 2 * NC_])
        rk = sb("rk", [P, 2 * NC_, E])
        small = {k: sb("r_" + k, [P, 2 * NC_]) for k in ("rank", "keep", "slot", "off", "w")}
        scat = sb("scat", [P, 2 * NC_], I32)
        home = sb("home", [SH, 2, 2], I32)
        ediff = sb("ediff", [P, NC_])
        eexp = sb("eexp", [P, NC_])
        eden = sb("eden", [P, NC_])
        moe_space = sb("moe_hid", [128, 2 * FK * CAP])
        hid = moe_space[:].rearrange("p (s f c) -> p s f c", s=2, f=FK)
        z_t = moe_space[:, 0:2 * 3 * T].rearrange("p (s k n) -> p s k n", s=2, k=3)
        moe_at, moe_n = offsets(dict(x_slot=4 * ROW, y_slot=4 * C, x_slot_t=4 * CAP, y_tok=2 * NC_ * C,
                                     x_home=2 * NC_ * ROW))
        assert moe_n <= 8 * CI * T
        moe = {k: pt_ring[:, lo:hi] for k, (lo, hi) in moe_at.items()}
        x_slot = moe["x_slot"][0:SH].rearrange("p (s h c) -> p s h c", s=2, h=2)
        y_slot = moe["y_slot"][0:SH].rearrange("p (s h c) -> p s h c", s=2, h=2)
        x_slot_t = moe["x_slot_t"][0:FC].rearrange("p (s k c) -> p s k c", s=2, k=KC)
        y_tok = moe["y_tok"].rearrange("p (m c) -> p m c", m=2 * NC_)
        x_home = moe["x_home"].rearrange("p (m c) -> p m c", m=2 * NC_)
        zero = sb("zero", [P, C])
        wqk2 = sb("wqk2", [FC, QK_AHEAD, 2, KC, C])
        wv2 = sb("wv2", [FC, KC, C])
        fw1 = sb("fw1", [FC, KC, INNER])
        fw2 = sb("fw2", [FC, KC, INNER])
        fwo = sb("fwo", [FC, KC, C])

        x_dram = nc.dram_tensor("slot_rows", [SLOTS + 2 * N, ROW], F32, kind="Internal").ap()
        y_dram = nc.dram_tensor("result_rows", [2 * N + SLOTS, C], F32, kind="Internal").ap()

        ld_tok, ld_base, ld_const, ld_cols, ld_rows = (sem(s) for s in (
            "ld_tok", "ld_base", "ld_const", "ld_cols", "ld_rows"))
        ld_w0, ld_wo0, ld_w1, ld_wv2, ld_wf = (sem(s) for s in (
            "ld_w0", "ld_wo0", "ld_w1", "ld_wv2", "ld_wf"))
        ld_head = [sem(f"ld_head{p}") for p in range(2)]
        ld_head2 = [sem(f"ld_head2{p}") for p in range(QK_AHEAD)]
        ld_fc = [sem(f"ld_fc{p}") for p in range(2)]
        ld_pj = [sem(f"ld_pj{p}") for p in range(2)]
        tok_mm = sem("tok_mm")
        h_ready = sem("h_ready")
        hb_ready = sem("hb_ready")
        var_ready = sem("var_ready")
        eps_set = sem("eps_set")
        g_ready = sem("g_ready")
        std_ready = sem("std_ready")
        norm_ready = sem("norm_ready")
        turn_mm = sem("turn_mm")
        turn_act = sem("turn_act")
        turn_dve = sem("turn_dve")
        lat_mm = sem("lat_mm")
        lat_ready = sem("lat_ready")
        lat_turn = sem("lat_turn")
        ct_ready = sem("ct_ready")
        v_mm = sem("v_mm")
        v_act = sem("v_act")
        v_dve = sem("v_dve")
        proj_mm = sem("proj_mm")
        proj_dve = sem("proj_dve")
        proj_act = sem("proj_act")
        qt_zero = sem("qt_zero")
        q_sum = sem("q_sum")
        k_sum = sem("k_sum")
        scores_mm = sem("scores_mm")
        max_ready = sem("max_ready")
        probs_ready = sem("probs_ready")
        probs_turn = sem("probs_turn")
        pt_ready = sem("pt_ready")
        pt_1 = [sem(f"pt_1{p}") for p in range(2)]
        scaled = sem("scaled")
        block_mm = sem("block_mm")
        ot_ready = sem("ot_ready")
        ot_turn = sem("ot_turn")
        inverted = sem("inverted")
        rsum_inv = sem("rsum_inv")
        o_ready = sem("o_ready")
        vq_ready = sem("vq_ready")
        vq_set = sem("vq_set")
        qm_ready = sem("qm_ready")
        qk1_mm = sem("qk1_mm")
        q1_ready = sem("q1_ready")
        k1_ready = sem("k1_ready")
        y_mm = sem("y_mm")
        gate_mm = sem("gate_mm")
        oh_ready = sem("oh_ready")
        rank_mm = sem("rank_mm")
        diff_ready = sem("diff_ready")
        exp_ready = sem("exp_ready")
        place_ready = sem("place_ready")
        zero_ready = sem("zero_ready")
        zeroed = sem("zeroed")
        home_set = sem("home_set")
        x_home_act = sem("x_home_act")
        x_home_pool = sem("x_home_pool")
        home_ready = sem("home_ready")
        scattered = sem("scattered")
        ld_slot = [sem(f"ld_slot{p}") for p in range(2)]
        slot_turn = sem("slot_turn")
        slot_t_ready = sem("slot_t_ready")
        hid_mm = sem("hid_mm")
        hid_ready = sem("hid_ready")
        out_mm = sem("out_mm")
        ys_ready = sem("ys_ready")
        st_slot = [sem(f"st_slot{p}") for p in range(2)]
        ld_y = [sem(f"ld_y{b}") for b in range(B)]
        xw_zero = sem("xw_zero")
        qk_mm = sem("qk_mm")
        qk_act = sem("qk_act")
        qk_ready = sem("qk_ready")
        fh_mm = sem("fh_mm")
        fh_ready = sem("fh_ready")
        fold_mm = sem("fold_mm")
        folded = sem("folded")
        dve_step = sem("dve_step")
        hb_beta = sem("hb_beta")
        out_ready = sem("out_ready")
        stored = sem("stored")

        block = ctx.enter_context(nc.Block())

        THIRDS, HALVES, WHOLE = [(0, 2), (2, 4), (4, 6)], [(0, CI), (CI, NC_)], [(0, NC_)]

        def flat(x):
            return x.rearrange("p a b -> p (a b)")

        pieces0 = [("v", 0, 0), ("v", 1, 0)] + [(kind, b, part) for b in range(B) for kind in "qk" for part in range(2)]
        at0 = {0: (0,), 2: (1,), 4: (2, 3), 5: (4,), 6: (5,), 8: (6,), 9: (7,), 10: (8,), 11: (9,)}
        assert min(t for t in at0 if at0[t][0] >= 2) >= PEEL
        n0 = len(pieces0)
        dve0 = [m for m in range(n0) if pieces0[m][0] in "qk"]
        act0 = [m for m in range(n0) if pieces0[m][0] == "v"]
        PRE_MM, PRE_DVE, PRE_ACT = n0 - 2, len(dve0), 0
        MM0 = PRE_MM + n0 * (PAIRS - 1) + 2
        ACT0 = len(act0) * PAIRS

        def count0(pair, m, of):
            per, pre = {"mm": (list(range(n0)), PRE_MM), "dve": (dve0, PRE_DVE), "act": (act0, PRE_ACT)}[of]
            return pair * len(per) + (pre + per.index(m) + 1)

        def summed(pair, b, kind):
            return (pair * B + (b + 1)) * (2 if kind == "q" else 1)

        pieces2 = [(1, 1), (1, 2)] + [(u, part) for u in (2, 3, 4) for part in range(3)] + [(5, 0)]
        at2 = {2 * m: m for m in range(len(pieces2))}
        n2 = len(pieces2)
        FIRST2 = [m for m in range(n2) if pieces2[m][0] >= 4]

        def count2(quad, m):
            return quad * n2 + (len(FIRST2) + m + 1)

        def width(causal, i):
            return P * (i + 1) if causal else T

        def tok(b, i):
            return slice(b * T + i * P, b * T + (i + 1) * P)

        def steps_of(engine, step, bodies, steps):
            for t in range(PEEL):
                step(0, t, True, False)
            with engine.Fori(0, bodies - 1) as i:
                for t in range(PEEL, steps + PEEL):
                    step(i + t // steps, t % steps, False, False)
            for t in range(PEEL, steps):
                step(bodies - 1, t, False, True)

        def ended(body, t, block):
            b = (t // block - 1) % B
            return body * B + (t // block - 1), body - (t < block), b

        def copied1(quad, t):
            if t % CI == CI - 1:
                return pt_1[1], quad * (BODY // CI) + (t // CI + 1)
            return pt_1[0], quad * (BODY // CI * 2) + (t // CI * 2 + t % CI + 1)

        @block.sync
        def _(sp):
            sp.dma_start(tok_x[:], a["tok_x"]).then_inc(ld_tok, 16)
            sp.dma_start(tok_w[:], a["tok_w"]).then_inc(ld_tok, 16)
            sp.dma_start(base[:], a["base"]).then_inc(ld_base, 16)
            sp.dma_start(const[:], a["const"]).then_inc(ld_const, 16)
            sp.dma_start(wdown[:], a["wdown"]).then_inc(ld_w0, 16)
            sp.dma_start(cols[:], a["cols"]).then_inc(ld_cols, 16)
            sp.dma_start(wup_v, a["wup_v"]).then_inc(ld_w0, 16)
            for p in range(2):
                sp.dma_start(wq_h[:, p], a["wq_h"][p]).then_inc(ld_head[p], 16)
                sp.dma_start(wk_h[:, p], a["wk_h"][p]).then_inc(ld_head[p], 16)
            sp.dma_start(rows[:], a["rows"].partition_broadcast(P)).then_inc(ld_rows, 16)
            sp.wait_ge(proj_mm, count0(-1, n0 - 1, "mm"))
            for p in range(2):
                sp.dma_start(wq_h[:, p], a["wq_h"][2 + p]).then_inc(ld_head[p], 16)
                sp.dma_start(wk_h[:, p], a["wk_h"][2 + p]).then_inc(ld_head[p], 16)
            sp.dma_start(wo0[:], a["wo0"]).then_inc(ld_wo0, 16)
            sp.dma_start(wqk1[:], a["wqk1"]).then_inc(ld_w1, 16)
            sp.dma_start(w1s[:], a["w1s"]).then_inc(ld_w1, 16)
            for p in range(2):
                sp.dma_start(fc_w[:, p], a["fc_w"][p]).then_inc(ld_fc[p], 16)
                sp.dma_start(pj_w[:, p], a["pj_w"][p]).then_inc(ld_pj[p], 16)
            for h in range(QK_AHEAD):
                sp.dma_start(wqk2[:, h], a["wqk2"][h]).then_inc(ld_head2[h], 16)
            sp.dma_start(wv2[:], a["wv2"]).then_inc(ld_wv2, 16)
            sp.dma_start(fw1[:], a["fw1"]).then_inc(ld_wf, 16)
            sp.dma_start(fw2[:], a["fw2"]).then_inc(ld_wf, 16)
            sp.dma_start(fwo[:], a["fwo"]).then_inc(ld_wf, 16)
            sp.wait_ge(zero_ready, 1)
            sp.dma_start(x_dram[0:SLOTS, :], a["empty_rows"]).then_inc(zeroed, 16)
            sp.dma_start(y_dram[0:2 * N, :].rearrange("(m p) c -> p m c", p=P),
                         zero[:].unsqueeze(1).to_broadcast([P, 2 * NC_, C])).then_inc(zeroed, 16)
            with nc.sync.Fori(0, PAIRS - 2) as pair:
                sp.wait_ge(proj_mm, count0(pair, n0 - 1, "mm"))
                for p in range(2):
                    h = pair * 2 + (4 + p)
                    sp.dma_start(wq_h[:, p], a["wq_h"][bass.ds(h, 1)].rearrange("o p k n -> (o p) k n")).then_inc(ld_head[p], 16)
                    sp.dma_start(wk_h[:, p], a["wk_h"][bass.ds(h, 1)].rearrange("o p n -> (o p) n")).then_inc(ld_head[p], 16)
            for h in range(QK_AHEAD, HEADS):
                sp.wait_ge(qk_mm, h - QK_AHEAD + 1)
                sp.dma_start(wqk2[:, h % QK_AHEAD], a["wqk2"][h]).then_inc(ld_head2[h % QK_AHEAD], 16)
            sp.wait_ge(scattered, 16 * 2 * NC_)
            x_rows = x_dram[0:SLOTS, :].rearrange("(e s p) c -> e p s c", e=E, s=2)
            for e in range(2):
                sp.dma_start(x_slot[:, e], x_rows[e]).then_inc(ld_slot[e], 16)
            for e in range(E):
                p = e % 2
                if e + 2 < E:
                    sp.wait_ge(hid_mm, FK * (e + 1))
                    sp.wait_ge(home_ready, e + 1)
                    sp.dma_start(x_slot[:, p], x_rows[e + 2]).then_inc(ld_slot[p], 16)
                    sp.dma_start(fc_w[:, p], a["fc_w"][e + 2]).then_inc(ld_fc[p], 16)
                    sp.wait_ge(out_mm, 2 * (e + 1))
                    sp.dma_start(pj_w[:, p], a["pj_w"][e + 2]).then_inc(ld_pj[p], 16)
            for p in range(2):
                sp.wait_ge(st_slot[p], 16 * E)
            y_rows = y_dram[0:2 * N, :].rearrange("(k m p) c -> p k m c", k=2, p=P)
            for b in range(B):
                for k in range(2):
                    sp.dma_start(y_tok[:, k * NC_ + b * CI:k * NC_ + (b + 1) * CI],
                                 y_rows[:, k, b * CI:(b + 1) * CI]).then_inc(ld_y[b], 16)
            out_v = out.rearrange("b (i p) c -> p (b i) c", p=P)
            for ci in range(NC_):
                sp.wait_ge(out_ready, ci + 1)
                sp.dma_start(out_v[:, ci], h_b[:, ci]).then_inc(stored, 16)
            sp.wait_ge(stored, 16 * NC_)

        @block.tensor
        def _(pe):
            mm = nc.tensor.matmul
            ident = cst["ident"]
            turned = [0]

            def turn(src, width_, dst_parts, groups, ready):
                for g, (fs, b) in enumerate(groups):
                    if ready is not None:
                        pe.wait_ge(norm_ready, ready + CI * (b + 1))
                    n = turned[0]
                    if g >= 4:
                        pe.wait_ge(turn_dve if n % 2 else turn_act, (n - 4) // 2 + 1)
                    for i in range(CI):
                        last = nc.tensor.transpose(turn_bank[n % 4][0:dst_parts, i * P:(i + 1) * P],
                                                   src[:, b * CI + i, fs], ident[0:P, 0:P])
                    last.then_inc(turn_mm, 1)
                    turned[0] += 1

            def wait_turned():
                pe.wait_ge(turn_act, turned[0] // 2)
                pe.wait_ge(turn_dve, turned[0] // 2)

            def turn_xn(ready, src=xn):
                turn(src, FC, FC, [(slice(k * FC, (k + 1) * FC), b) for b in range(B) for k in range(KC)], ready)
                wait_turned()

            def v_banks(w):
                for ci in range(NC_):
                    for k in range(KC):
                        last = mm(score_bank[ci // 2][0:P, (ci % 2) * C:(ci % 2 + 1) * C],
                                  x_t[:, k, ci * P:(ci + 1) * P], w(k), start=(k == 0), stop=(k == KC - 1))
                    if ci % 2:
                        last.then_inc(v_mm, 1)

            def transposes(n, t, causal, ready, bank_free):
                i = t % CI
                pe.wait_ge(ready, n + 1)
                if bank_free is not None:
                    pe.wait_ge(*bank_free)
                for j in range(width(causal, i) // P):
                    last = nc.tensor.transpose(pt_bank[t % 2][0:P, j * P:(j + 1) * P],
                                               probs[:, i, j * P:(j + 1) * P], ident[0:P, 0:P])
                last.then_inc(probs_turn, 1)

            def block_product(copies, unit0, heads, v, d, causal):
                for copied in copies:
                    pe.wait_ge(*copied)
                for jj in range(CI):
                    lo = jj * P if causal else 0
                    for j in range(heads):
                        last = mm(o_bank[d * j:d * (j + 1), lo:T], v(jj, j), probs_t[:, unit0 + j, jj, lo:T],
                                  start=(jj == 0), stop=(jj == CI - 1))
                last.then_inc(block_mm, 1)

            def turn_block(beta):
                pe.wait_ge(ot_ready, B * PAIRS + 1 + beta)
                for i in range(CI):
                    last = nc.tensor.transpose(o_bank[0:P, i * 128:(i + 1) * 128], o_t[:, i * P:(i + 1) * P], ident)
                last.then_inc(ot_turn, 1)

            pe.wait_ge(ld_tok, 32)
            for ci in range(NC_):
                mm(score_bank[ci // 2][0:P, (ci % 2) * C:(ci % 2 + 1) * C], tok_x[:, ci * P:(ci + 1) * P],
                   tok_w[:], start=True, stop=True).then_inc(tok_mm, 1)

            pe.wait_ge(ld_const, 16)
            pe.wait_ge(ld_w0, 32)
            turn_xn(0)
            for ci in range(NC_):
                for k in range(KC):
                    last = mm(o_bank[0:P, ci * D0:(ci + 1) * D0], x_t[:, k, ci * P:(ci + 1) * P], wdown[:, k],
                              start=(k == 0), stop=(k == KC - 1))
            last.then_inc(lat_mm, 1)

            def bank_free0(pair, m):
                if m in dve0:
                    pe.wait_ge(proj_dve, count0(pair, m, "dve"))
                else:
                    pe.wait_ge(proj_act, count0(pair, m, "act"))

            def proj0(pair, m):
                kind, b, p = pieces0[m]
                dst = proj_bank[m % 2]
                if m >= 2 and not (isinstance(pair, int) and pair < 0 and m < 4):
                    bank_free0(pair, m - 2)
                xs = slice(b * T, (b + 1) * T)
                if kind == "q":
                    pe.wait_ge(ld_head[p], 32 * pair + 64)
                    for k in range(KC):
                        last = mm(dst[:, 0:T], wq_h[:, p, k], x_t[:, k, xs], start=(k == 0), stop=(k == KC - 1))
                elif kind == "k":
                    last = mm(dst[:, 0:T], wk_h[:, p], c_t[:, xs], start=True, stop=True)
                else:
                    for i in range(CI):
                        last = mm(dst[0:P, i * 128:(i + 1) * 128], c_t[:, tok(b, i)],
                                  wup_v[:, bass.ds(pair * 128, 128)], start=True, stop=True)
                last.then_inc(proj_mm, 1)

            def scores0(pair, t, behind=None):
                b, p, i = t // BLOCK0, t % BLOCK0 // CI, t % CI
                if t % BLOCK0 == 0:
                    pe.wait_ge(q_sum, summed(pair, b, "q"))
                    pe.wait_ge(k_sum, summed(pair, b, "k"))
                if behind is not None:
                    pe.wait_ge(max_ready, behind + 1)
                w = P * (i + 1)
                mm(score_bank[i][0:P, 0:w], q_t[:, p, tok(b, i)], k_t[:, b * T:b * T + w],
                   start=True, stop=True).then_inc(scores_mm, 1)

            for m in (2, 3):
                proj0(-1, m)
            for b in range(B):
                pe.wait_ge(lat_ready, CI * (b + 1))
                for i in range(CI):
                    last = nc.tensor.transpose(pt_bank[b][0:D0, i * P:(i + 1) * P], c_n[:, b * CI + i, :], ident[0:P, 0:P])
                last.then_inc(lat_turn, 1)
            pe.wait_ge(ct_ready, B)
            for m in range(4, n0):
                proj0(-1, m)
            for t in range(AHEAD):
                scores0(0, t)

            def end0(block, pair, b):
                pe.wait_ge(proj_act, count0(pair, b, "act"))
                block_product([(pt_ready, (block + 1) * BLOCK0 + 2)], 2 * b, 2,
                              lambda jj, j: v_p[:, b * CI + jj, D0 * j:D0 * (j + 1)], D0, True)

            def step0(pair, t, first, final):
                n = pair * BODY0 + t
                if t + AHEAD < BODY0:
                    scores0(pair, t + AHEAD, n)
                elif not final:
                    scores0(pair + 1, t + AHEAD - BODY0, n)
                for m in at0.get(t, ()):
                    if m < 2:
                        bank_free0(pair - 1, n0 - 2 + m)
                transposes(n, t, True, scaled, (pt_ready, n + 1))
                if t % BLOCK0 == LAG - 1 and not (first and t < BLOCK0):
                    end0(*ended(pair, t, BLOCK0))
                for m in at0.get(t, ()):
                    if not final or pieces0[m][0] == "v":
                        proj0(pair, m)

            steps_of(nc.tensor, step0, PAIRS, BODY0)
            end0(*ended(PAIRS, 0, BLOCK0))

            pe.wait_ge(ot_ready, B * PAIRS)
            pe.wait_ge(ld_wo0, 16)
            for ci in range(NC_):
                for k in range(FK):
                    last = mm(score_bank[ci // 2][0:P, (ci % 2) * C:(ci % 2 + 1) * C],
                              o_0t[:, k, ci * P:(ci + 1) * P], wo0[:, k], start=(k == 0), stop=(k == FK - 1))
                last.then_inc(y_mm, 1)

            pe.wait_ge(ld_w1, 32)
            turn_xn(NC_)
            for m in range(3 * B):
                blk, b = divmod(m, B)
                if m >= 4:
                    pe.wait_ge(q1_ready, m - 3)
                for k in range(KC):
                    last = mm(turn_bank[m % 4][:, 0:T], wqk1[:, k, blk], x_t[:, k, b * T:(b + 1) * T],
                              start=(k == 0), stop=(k == KC - 1))
                last.then_inc(qk1_mm, 1)
            v_banks(lambda k: w1s[:, k, 0:C])

            def v_quad(b):
                return lambda jj, j: v_q[:, b * CI + jj, j, :]

            def end_block(copies, beta, b, causal):
                pe.wait_ge(vq_ready, beta + 1)
                pe.wait_ge(o_ready, beta + 1)
                block_product(copies, 4 * b, 4, v_quad(b), 32, causal)

            def scores1(quad, t, behind=None):
                b, j, i = t // BLOCK, t % BLOCK // CI, t % CI
                if behind is not None:
                    pe.wait_ge(max_ready, behind + 1)
                if i == 0:
                    pe.wait_ge(qm_ready, quad * 8 + (4 * b + j + 1))
                w = P * (i + 1)
                mm(score_bank[i][0:P, 0:w], q_m[:, j, tok(b, i)],
                   k_1t[:, bass.ds(quad, 1), b * T:b * T + w].rearrange("p o n -> p (o n)"),
                   start=True, stop=True).then_inc(scores_mm, 1)

            pe.wait_ge(k1_ready, 2 * B)
            pe.wait_ge(q1_ready, 2 * B)
            pe.wait_ge(v_dve, 3)
            for t in range(AHEAD):
                scores1(0, t)

            def end1(beta, quad, b):
                end = (b + 1) * BLOCK
                end_block([copied1(quad, end - 2), copied1(quad, end - 1)], beta, b, True)

            def step1(quad, t, first, final):
                n = quad * BODY + (STEPS + t)
                if t + AHEAD < BODY:
                    scores1(quad, t + AHEAD, n)
                elif not final:
                    scores1(quad + 1, t + AHEAD - BODY, n)
                transposes(n, t, True, probs_ready,
                           None if first and t < 2 else copied1(quad - int(t < 2), (t - 2) % BODY))
                if not (first and t < BLOCK):
                    if t % BLOCK == LAG - 1:
                        end1(*ended(quad, t, BLOCK))
                    if t % BLOCK == PEEL - 1:
                        turn_block(ended(quad, t, BLOCK)[0])

            steps_of(nc.tensor, step1, QUADS, BODY)
            end1(*ended(QUADS, 0, BLOCK))
            turn_block(B * QUADS - 1)
            pe.wait_ge(o_ready, 1 + B * QUADS)
            turn(o_1, FC, FC, [(slice(k * FC, (k + 1) * FC), b) for b in range(B) for k in range(KC)], None)
            wait_turned()
            for ci in range(NC_):
                for k in range(KC):
                    last = mm(score_bank[ci // 2][0:P, (ci % 2) * C:(ci % 2 + 1) * C],
                              x_t[:, k, ci * P:(ci + 1) * P], w1s[:, k, C:2 * C], start=(k == 0), stop=(k == KC - 1))
                last.then_inc(y_mm, 1)

            def qk_product(h):
                pe.wait_ge(ld_head2[h % QK_AHEAD], 16 * (h // QK_AHEAD + 1))
                if h >= 2:
                    pe.wait_ge(qk_act, h - 1)
                for d in range(KC):
                    for k in range(KC):
                        last = mm(pt_bank[h % 2][0:FC, d * C:(d + 1) * C],
                                  wqk2[:, h % QK_AHEAD, 0, k, d * FC:(d + 1) * FC],
                                  wqk2[:, h % QK_AHEAD, 1, k], start=(k == 0), stop=(k == KC - 1))
                last.then_inc(qk_mm, 1)

            turn_xn(2 * NC_, o_1)
            for ci in range(NC_):
                for k in range(KC):
                    last = mm(o_bank[0:P, ci * E:(ci + 1) * E], x_t[:, k, ci * P:(ci + 1) * P],
                              w1s[:, k, 2 * C:2 * C + E], start=(k == 0), stop=(k == KC - 1))
            last.then_inc(gate_mm, 1)
            pe.wait_ge(oh_ready, 1)
            ohf = oh[:].rearrange("p k c e -> p (k c e)")
            mm(score_bank[0][0:P, 0:2 * NC_ * E], before_bf[:], ohf, start=True, stop=True)
            mm(score_bank[1][0:P, 0:2 * NC_ * E], ones_bf[:], ohf, start=True, stop=True).then_inc(rank_mm, 1)
            for h in range(HEADS):
                qk_product(h)
            pe.wait_ge(qk_act, HEADS)

            def expert_hidden(e):
                p = e % 2
                pe.wait_ge(ld_slot[p], 16 * (e // 2 + 1))
                for k in range(KC):
                    for s in range(2):
                        last = nc.tensor.transpose(
                            pt_bank[p][0:FC, k * CAP + s * SH:k * CAP + (s + 1) * SH],
                            x_slot[:, p, s, k * FC:(k + 1) * FC], ident[0:SH, 0:SH])
                last.then_inc(slot_turn, 1)
                pe.wait_ge(slot_t_ready, e + 1)
                pe.wait_ge(ld_fc[p], 16 * (e // 2 + 1))
                for f in range(FK):
                    n = FK * e + f
                    if n >= 3:
                        pe.wait_ge(hid_ready, n - 2)
                    for k in range(KC):
                        last = mm(score_bank[n % 3][:, 0:CAP], fc_w[:, p, k, f * 128:(f + 1) * 128],
                                  x_slot_t[:, p, k], start=(k == 0), stop=(k == KC - 1))
                    last.then_inc(hid_mm, 1)

            def expert_out(e):
                p = e % 2
                pe.wait_ge(ld_pj[p], 16 * (e // 2 + 1))
                pe.wait_ge(hid_ready, FK * (e + 1))
                for s in range(2):
                    if e >= 1:
                        pe.wait_ge(ys_ready, 2 * e - 1 + s)
                    for f in range(FK):
                        last = mm(proj_bank[s][0:SH, 0:C], hid[:, p, f, s * SH:(s + 1) * SH], pj_w[:, p, f],
                                  start=(f == 0), stop=(f == FK - 1))
                    last.then_inc(out_mm, 1)

            for e in range(E):
                expert_hidden(e)
                if e:
                    expert_out(e - 1)
            expert_out(E - 1)
            pe.wait_ge(ld_wf, 48)
            for k in range(KC):
                last = mm(o_bank[0:INNER, 0:C], fw2[:, k], fwo[:, k], start=(k == 0), stop=(k == KC - 1))
            last.then_inc(fold_mm, 1)
            pe.wait_ge(folded, 1)
            for k in range(KC):
                last = mm(o_bank[0:P, 0:C], col["fb2"][0:FC, k:k + 1].to_broadcast([FC, P]), fwo[:, k],
                          start=(k == 0), stop=(k == KC - 1))
            last.then_inc(fold_mm, 1)

            turn_xn(3 * NC_)
            turn(xn, 128, 128, [(slice(lo, lo + 128), b) for b in range(B) for lo in (0, C - 128)], None)
            pe.wait_ge(ld_wv2, 16)
            v_banks(lambda k: wv2[:, k])

            def proj2(quad, m, count):
                u, part = pieces2[m]
                b, p = u % 4 // 2, u % 2
                if not (isinstance(count, int) and count < 3):
                    pe.wait_ge(proj_act, ACT0 - 2 + count)
                if u >= 4 and part == 0:
                    pe.wait_ge(qk_ready, (quad + 1) * 4 + 2 * (u - 4) + 2)
                for k in range(KC):
                    last = mm(proj_bank[m % 2][:, 0:T], qk_2[:, p, k, part * 128:(part + 1) * 128],
                              x_t[:, k, b * T:(b + 1) * T], start=(k == 0), stop=(k == KC - 1))
                last.then_inc(proj_mm, 1)

            def scores2(quad, t):
                b, u, j, i = t // BLOCK, t // (2 * CI), t // CI % 2, t % CI
                if t % (2 * CI) == 0:
                    made, z = (quad, (u, 2)) if u else (quad - 1, (4, 2))
                    pe.wait_ge(proj_act, count2(made, pieces2.index(z)) + ACT0)
                for k in range(2):
                    last = mm(score_bank[i][0:P, 0:T], z_t[:, u % 2, j + k, i * P:(i + 1) * P],
                              x_w[:, 2 * j + k, b * T:(b + 1) * T], start=(k == 0), stop=(k == 1))
                last.then_inc(scores_mm, 1)

            wait_turned()
            for c, m in enumerate(FIRST2):
                proj2(-1, m, c + 1)
            pe.wait_ge(v_dve, 6)
            pe.wait_ge(xw_zero, 2)
            for t in range(AHEAD):
                scores2(0, t)

            def body2(quad, final):
                for t in range(BODY):
                    n = quad * BODY + (2 * STEPS + t)
                    beta = quad * B + B * QUADS
                    m = at2.get(t)
                    if m is not None and final and m in FIRST2:
                        m = None
                    late = t % BLOCK == BLOCK - 1
                    transposes(n, t, False, probs_ready, (pt_ready, n - STEPS + 1))
                    if m is not None and not late:
                        proj2(quad, m, count2(quad, m))
                    if t + AHEAD < BODY:
                        scores2(quad, t + AHEAD)
                    elif not final:
                        scores2(quad + 1, t + AHEAD - BODY)
                    if late:
                        end_block([(pt_ready, n - STEPS + 3)], beta + t // BLOCK, t // BLOCK, False)
                    if m is not None and late:
                        proj2(quad, m, count2(quad, m))
                    if t == BLOCK + 1:
                        turn_block(beta)
                    if t == BODY - 1:
                        turn_block(beta + 1)

            with nc.tensor.Fori(0, QUADS - 1) as quad:
                body2(quad, False)
            body2(QUADS - 1, True)

            turn_xn(4 * NC_)
            for b in range(B):
                for k in range(KC):
                    last = mm(turn_bank[b][:, 0:T], fw1[:, k], x_t[:, k, b * T:(b + 1) * T],
                              start=(k == 0), stop=(k == KC - 1))
                last.then_inc(fh_mm, 1)
            for ci in range(NC_):
                if ci % CI == 0:
                    pe.wait_ge(fh_ready, ci // CI + 1)
                mm(score_bank[ci // 2][0:P, (ci % 2) * C:(ci % 2 + 1) * C], f_h[:, ci * P:(ci + 1) * P], fw_out,
                   start=True, stop=True).then_inc(y_mm, 1)

        @block.scalar
        def _(act):
            turned = [0]
            norms = [0]

            def roots(parts, of=None):
                for lo, hi in parts:
                    norms[0] += 1
                    act.wait_ge(var_ready, norms[0])
                    nc.scalar.activation(std[:, lo:hi], mv[:, lo:hi, 1] if of is None else of[:, lo:hi], ACT.Sqrt,
                                         bias=eps[:], scale=1.0).then_inc(std_ready, 1)

            def take_turned(dst, count, w=None, bvec=None):
                for g in range(0, count, 2):
                    n = turned[0]
                    act.wait_ge(turn_mm, n + 1)
                    d = dst(g)
                    src = turn_bank[n % 4][0:d.shape[0], 0:T]
                    if w is None:
                        nc.scalar.copy(d, src).then_inc(turn_act, 1)
                    else:
                        k = g % KC
                        nc.scalar.activation(d, src, ACT.Identity, bias=bvec[0:FC, k:k + 1],
                                             scale=w[0:FC, k:k + 1]).then_inc(turn_act, 1)
                    turned[0] += 2

            def x_t_part(g):
                b, k = divmod(g, KC)
                return x_t[:, k, b * T:(b + 1) * T]

            def exps(n, i, causal, sums=False):
                w = width(causal, i)
                act.wait_ge(max_ready, n + 1)
                src, sign = (masked[:, i, 0:w], -1.0) if causal else (score_bank[i][0:P, 0:w], 1.0)
                if sums:
                    nc.scalar.activation(probs[:, i, 0:w], src, ACT.Exp, bias=nmax[:, i:i + 1], scale=sign,
                                         accum_out=rsum[:, i:i + 1]).then_inc(probs_ready, 1)
                else:
                    nc.scalar.activation(probs[:, i, 0:w], src, ACT.Exp, bias=nmax[:, i:i + 1],
                                         scale=sign).then_inc(probs_ready, 1)

            def copy_pt(n, t, signal):
                i = t % CI
                act.wait_ge(probs_turn, n + 1)
                nc.scalar.copy(probs_t[:, t // CI, 0:i + 1, i * P:(i + 1) * P],
                               pt_bank[t % 2][0:P, 0:(i + 1) * P].rearrange("p (j l) -> p j l", l=P)).then_inc(signal, 1)

            act.wait_ge(eps_set, 1)
            roots(THIRDS)
            take_turned(x_t_part, 4)
            roots(WHOLE)
            act.wait_ge(ld_cols, 16)
            for b in range(B):
                act.wait_ge(lat_turn, b + 1)
                nc.scalar.activation(c_t[:, b * T:(b + 1) * T], pt_bank[b][0:D0, 0:T], ACT.Identity,
                                     bias=col["lnb"][0:D0], scale=col["lng"][0:D0]).then_inc(ct_ready, 1)

            def take0(pair, m):
                b = pieces0[m][1]
                act.wait_ge(proj_mm, count0(pair, m, "mm"))
                nc.scalar.copy(v_p[:, b * CI:(b + 1) * CI],
                               proj_bank[m % 2][0:P, 0:CI * 128].rearrange("p (i d) -> p i d", i=CI)).then_inc(proj_act, 1)

            for t in range(AHEAD):
                exps(t, t, True, True)

            def take_o0(block, pair, b):
                act.wait_ge(block_mm, block + 1)
                nc.scalar.copy(o_0t[:, bass.ds(pair, 1), b * T:(b + 1) * T].rearrange("p o n -> p (o n)"),
                               o_bank[:, 0:T]).then_inc(ot_ready, 1)

            def step0(pair, t, first, final):
                n = pair * BODY0 + t
                copy_pt(n, t, pt_ready)
                if t + AHEAD < BODY0 or not final:
                    exps(n + AHEAD, t % CI, True, True)
                if t % BLOCK0 == LAG - 1 and not (first and t < BLOCK0):
                    take_o0(*ended(pair, t, BLOCK0))
                for m in at0.get(t, ()):
                    if m in act0:
                        take0(pair, m)

            steps_of(nc.scalar, step0, PAIRS, BODY0)
            take_o0(*ended(PAIRS, 0, BLOCK0))
            for part in THIRDS:
                roots([part])
                roots([part], var_2)
            take_turned(x_t_part, 4, col["ln1w"], col["ln1b"])
            for m in range(B, 3 * B):
                blk, b = divmod(m, B)
                act.wait_ge(qk1_mm, m + 1)
                for quad in (range(2) if blk == 1 else (2,)):
                    last = nc.scalar.activation(k_1t[:, quad, b * T:(b + 1) * T], turn_bank[m % 4][:, 0:T],
                                                ACT.Identity, bias=col["qkb"][:, blk:blk + 1], scale=1.0)
                last.then_inc(k1_ready, 1)

            def take_block(beta):
                act.wait_ge(block_mm, B * PAIRS + 1 + beta)
                nc.scalar.copy(o_t[:], o_bank[:, 0:T]).then_inc(ot_ready, 1)

            for t in range(AHEAD):
                exps(STEPS + t, t, True)

            def step1(quad, t, first, final):
                n = quad * BODY + (STEPS + t)
                if t % CI == CI - 1:
                    copy_pt(n, t, pt_1[1])
                if t + AHEAD < BODY or not final:
                    act.wait_ge(probs_turn, n + 1)
                    exps(n + AHEAD, t % CI, True)
                if t % BLOCK == LAG - 1 and not (first and t < BLOCK):
                    take_block(ended(quad, t, BLOCK)[0])

            steps_of(nc.scalar, step1, QUADS, BODY)
            take_block(B * QUADS - 1)
            take_turned(x_t_part, 4)

            def take_qk(h):
                act.wait_ge(qk_mm, h + 1)
                nc.scalar.copy(qk_all[:, h], pt_bank[h % 2][0:FC, 0:KC * C]).then_inc(qk_act, 1)

            roots(THIRDS)
            take_turned(x_t_part, 4, col["ln2w"], col["ln2b"])
            act.wait_ge(diff_ready, 1)
            nc.scalar.activation(eexp[:], ediff[:], ACT.Exp).then_inc(exp_ready, 1)
            act.wait_ge(x_home_pool, 2)
            nc.scalar.copy(x_home[:, 0:NC_, 0:C], x_home[:, NC_:2 * NC_, 0:C]).then_inc(x_home_act, 1)
            for h in range(HEADS):
                take_qk(h)
            for e in range(E):
                p = e % 2
                act.wait_ge(slot_turn, e + 1)
                nc.scalar.copy(flat(x_slot_t[:, p]), pt_bank[p][0:FC, 0:KC * CAP]).then_inc(slot_t_ready, 1)
                for f in range(FK):
                    n = FK * e + f
                    act.wait_ge(hid_mm, n + 1)
                    if e >= 2:
                        act.wait_ge(out_mm, 2 * (e - 1))
                    nc.scalar.activation(hid[:, p, f], score_bank[n % 3][:, 0:CAP], ACT.Gelu,
                                         bias=col["fcb"][:, n:n + 1], scale=1.0).then_inc(hid_ready, 1)
            act.wait_ge(fold_mm, 1)
            nc.scalar.copy(fw_out, o_bank[0:INNER, 0:C]).then_inc(folded, 1)
            roots(HALVES)
            take_turned(x_t_part, 4)

            for b in range(B):
                n = turned[0]
                act.wait_ge(turn_mm, n + 1)
                bs = slice(b * T, (b + 1) * T)
                nc.scalar.copy(x_w[:, 0, bs], turn_bank[n % 4][:, 0:T])
                nc.scalar.copy(x_w[64:128, 2, bs], turn_bank[n % 4][0:64, 0:T]).then_inc(turn_act, 1)
                turned[0] += 2

            def take2(m, count):
                u, part = pieces2[m]
                act.wait_ge(proj_mm, count + MM0)
                nc.scalar.copy(z_t[:, u % 2, part, :], proj_bank[m % 2][:, 0:T]).then_inc(proj_act, 1)

            for c, m in enumerate(FIRST2):
                take2(m, c + 1)
            for t in range(AHEAD):
                exps(2 * STEPS + t, t, False)

            def body2(quad, final):
                for t in range(BODY):
                    n = quad * BODY + (2 * STEPS + t)
                    m = at2.get(t)
                    if m is not None and final and m in FIRST2:
                        m = None
                    late = t % BLOCK == BLOCK - 1
                    if m is not None and not late:
                        take2(m, count2(quad, m))
                    if t + AHEAD < BODY or not final:
                        act.wait_ge(probs_turn, n + 1)
                        exps(n + AHEAD, t % CI, False)
                    if late:
                        take_block(quad * B + (B * QUADS + t // BLOCK))
                    if m is not None and late:
                        take2(m, count2(quad, m))

            with nc.scalar.Fori(0, QUADS - 1) as quad:
                body2(quad, False)
            body2(QUADS - 1, True)
            roots(HALVES)
            take_turned(x_t_part, 4)
            for b in range(B):
                act.wait_ge(fh_mm, b + 1)
                nc.scalar.activation(f_h[:, b * T:(b + 1) * T], turn_bank[b][:, 0:T], ACT.Relu,
                                     bias=col["fb1"], scale=1.0).then_inc(fh_ready, 1)
            roots(THIRDS)

        @block.vector
        def _(dve):
            own = [0]
            norms = [0]
            turned = [0]

            def step(ins):
                own[0] += 1
                ins.then_inc(dve_step, 1)
                dve.wait_ge(dve_step, own[0])

            def moments(src, lo, hi):
                for ci in range(lo, hi):
                    last = nc.vector.bn_stats(bn[:, ci], src[:, ci])
                step(last)
                for ci in range(lo, hi):
                    last = nc.vector.bn_aggr(mv[:, ci], bn[:, ci])
                last.then_inc(var_ready, 1)
                norms[0] += 1
                return norms[0]

            def inverse_std(dst, root, lo, hi):
                dve.wait_ge(std_ready, root)
                step(nc.vector.reciprocal(dst[:, lo:hi], std[:, lo:hi]))

            def normalise(dst, src, signal, lo, hi, scale=rstd):
                for ci in range(lo, hi):
                    last = nc.vector.tensor_scalar(dst[:, ci], src[:, ci], mv[:, ci, 0:1], scale[:, ci:ci + 1],
                                                   ALU.subtract, ALU.mult)
                    if signal is not None:
                        last.then_inc(signal, 1)
                return last

            def layer_norm(dst, src, signal, parts, add=None):
                roots = []
                for k, (lo, hi) in enumerate(parts + [(0, 0)]):
                    if k < len(parts):
                        if add is not None:
                            add(k)
                        roots.append(moments(src, lo, hi))
                    if k:
                        inverse_std(rstd, roots[k - 1], *parts[k - 1])
                        normalise(dst, src, signal, *parts[k - 1])

            def take_turned(dst, count, w=None, bvec=None):
                for g in range(1, count, 2):
                    n = turned[0] + 1
                    dve.wait_ge(turn_mm, n + 1)
                    d = dst(g)
                    src = turn_bank[n % 4][0:d.shape[0], 0:T]
                    if w is None:
                        nc.vector.tensor_copy(d, src).then_inc(turn_dve, 1)
                    else:
                        k = g % KC
                        nc.vector.tensor_scalar(d, src, w[0:FC, k:k + 1], bvec[0:FC, k:k + 1],
                                                ALU.mult, ALU.add).then_inc(turn_dve, 1)
                    turned[0] += 2

            def x_t_part(g):
                b, k = divmod(g, KC)
                return x_t[:, k, b * T:(b + 1) * T]

            def maxima(n, i):
                dve.wait_ge(scores_mm, n + 1)
                nc.vector.tensor_reduce(nmax[:, i:i + 1], score_bank[i][0:P, 0:T], AX.X, ALU.max,
                                        negate=True).then_inc(max_ready, 1)

            def masked_maxima(n, i, carrier=False):
                w = P * (i + 1)
                if carrier:
                    dve.wait_ge(scores_mm, n + 1)
                    nc.vector.memset(spare[:, i:i + 1], 0.0)
                nc.vector.tensor_tensor_reduce(masked[:, i, 0:w], score_bank[i][0:P, 0:w], cst["mask"][0:P, T - w:T],
                                               -1.0, 3e38, ALU.add, ALU.min, nmax[:, i:i + 1]).then_inc(max_ready, 1)

            def invert(n, i):
                dve.wait_ge(probs_ready, n + 1)
                nc.vector.reciprocal(rinv0[:, i:i + 1], rsum[:, i:i + 1]).then_inc(inverted, 1)

            def scale(n, i):
                dve.wait_ge(inverted, n + 1)
                w = P * (i + 1)
                nc.vector.tensor_scalar(probs[:, i, 0:w], probs[:, i, 0:w], rinv0[:, i:i + 1], None,
                                        ALU.mult).then_inc(scaled, 1)

            def copy_pt(n, t, causal, signal):
                i = t % CI
                k = i + 1 if causal else CI
                dve.wait_ge(probs_turn, n + 1)
                nc.vector.tensor_copy(probs_t[:, t // CI, 0:k, i * P:(i + 1) * P],
                                      pt_bank[t % 2][0:P, 0:k * P].rearrange("p (j l) -> p j l", l=P)).then_inc(signal, 1)

            def divide(beta, quad, b):
                sums = o_bank[0:P, 0:CI * 128].rearrange("p (i j d) -> p i j d", i=CI, j=4)
                dve.wait_ge(ot_turn, beta + 1)
                nc.vector.reciprocal(rinv[:], sums[:, :, :, D1]).then_inc(rsum_inv, 1)
                dve.wait_ge(rsum_inv, beta + 1)
                nc.vector.tensor_tensor(
                    o_1[:, b * CI:(b + 1) * CI, bass.ds(quad * 64, 64)].rearrange("p i (j d) -> p i j d", j=4),
                    sums[:, :, :, 0:D1], rinv[:].unsqueeze(3).to_broadcast([P, CI, 4, D1]), ALU.mult).then_inc(o_ready, 1)

            def add_bank(k, dst, other, mm_sem, count, ready, total):
                dve.wait_ge(mm_sem, count)
                nc.vector.tensor_tensor(
                    dst[:, 2 * k:2 * k + 2],
                    score_bank[k][0:P, 0:2 * C].rearrange("p (a c) -> p a c", a=2), other, ALU.add).then_inc(ready, 1)
                dve.wait_ge(ready, total)

            dve.wait_ge(ld_base, 16)
            layer_norm(xn, h_a, norm_ready, THIRDS,
                       lambda k: add_bank(k, h_a, base[:, 2 * k:2 * k + 2], tok_mm, 2 * k + 2, h_ready, k + 1))
            take_turned(x_t_part, 4)
            nc.vector.tensor_copy(before_bf[:], cst["before"][0:P]).then_inc(o_ready, 1)
            nc.vector.tensor_copy(ones_bf[:], cst["ones"][0:P]).then_inc(pt_ready, 2)
            dve.wait_ge(lat_mm, 1)
            lat = o_bank[0:P, 0:NC_ * D0].rearrange("p (c d) -> p c d", c=NC_)
            layer_norm(c_n, lat, lat_ready, WHOLE)

            def rope(pair, m):
                kind, b, part = pieces0[m]
                if kind == "q":
                    dst, table, done, want = rope_q, cst["cos_sin_q"], q_sum, summed(pair + 1, b - 1, "q")
                else:
                    dst, table, done, want = rope_k, cst["cos_sin_k"], k_sum, summed(pair + 1, b - 1, "k")
                if part == 0 and not (isinstance(pair, int) and pair < 0 and b == 0):
                    dve.wait_ge(done, want)
                dve.wait_ge(proj_mm, count0(pair, m, "mm"))
                nc.vector.tensor_tensor(dst[:, part], proj_bank[m % 2][:, 0:T], table[:, part * T:(part + 1) * T],
                                        ALU.mult).then_inc(proj_dve, 1)

            for m in dve0:
                rope(-1, m)
            dve.wait_ge(scores_mm, AHEAD)
            for t in range(AHEAD):
                masked_maxima(t, t)
            invert(0, 0)
            scale(0, 0)

            def body0(pair, final):
                for t in range(BODY0):
                    n = pair * BODY0 + t
                    more = not (final and t == BODY0 - 1)
                    if more:
                        invert(n + 1, (t + 1) % CI)
                    if t + AHEAD < BODY0 or not final:
                        masked_maxima(n + AHEAD, t % CI, True)
                    if more:
                        scale(n + 1, (t + 1) % CI)
                    if not final:
                        for m in at0.get(t, ()):
                            if m in dve0:
                                rope(pair, m)

            with nc.vector.Fori(0, PAIRS - 1) as pair:
                body0(pair, False)
            body0(PAIRS - 1, True)
            dve.wait_ge(hb_ready, 1)
            for k, (lo, hi) in enumerate(THIRDS):
                add_bank(k, h_a, h_b[:, lo:hi], y_mm, 2 * k + 2, h_ready, 3 + k + 1)
                inverse_std(rstd, moments(h_a, lo, hi), lo, hi)
                part = slice(lo, hi)
                step(nc.vector.tensor_tensor(var_2[:, part], mv[:, part, 1], rstd[:, part], ALU.mult))
                nc.vector.tensor_tensor(var_2[:, part], var_2[:, part], rstd[:, part], ALU.mult).then_inc(var_ready, 1)
                norms[0] += 1
                inverse_std(rstd_2, norms[0], lo, hi)
                step(nc.vector.tensor_tensor(rstd_2[:, part], rstd_2[:, part], rstd[:, part], ALU.mult))
                normalise(xn, h_a, norm_ready, lo, hi, rstd_2)
            take_turned(x_t_part, 4, col["ln1w"], col["ln1b"])
            normalise(g_a, h_a, None, 0, NC_).then_inc(g_ready, 1)
            for b in range(B):
                dve.wait_ge(qk1_mm, b + 1)
                nc.vector.tensor_scalar(q_1t[:, 0, b * T:(b + 1) * T], turn_bank[b][:, 0:T],
                                        col["qkb"][:, 0:1], D1 ** -0.5, ALU.add, ALU.mult).then_inc(q1_ready, 1)
            for b in range(B):
                dve.wait_ge(k1_ready, B + b + 1)
                for lo in (0, 64):
                    last = nc.vector.tensor_scalar(q_1t[lo:lo + 64, 1, b * T:(b + 1) * T],
                                                   turn_bank[(2 * B + b) % 4][0:64, 0:T], col["qkb"][0:64, 3:4],
                                                   D1 ** -0.5, ALU.add, ALU.mult)
                last.then_inc(q1_ready, 1)
            for k in range(3):
                add_bank(k, v_1, row["vb"].unsqueeze(1).to_broadcast([P, 2, C]), v_mm, k + 1, v_dve, k + 1)
            dve.wait_ge(scores_mm, STEPS + AHEAD)
            for t in range(AHEAD):
                masked_maxima(STEPS + t, t)

            def step1(quad, t, first, final):
                n = quad * BODY + (STEPS + t)
                more = t + AHEAD < BODY or not final
                if more:
                    dve.wait_ge(probs_ready, n + 1)
                if t % CI:
                    if more:
                        dve.wait_ge(scores_mm, n + (AHEAD + 1))
                    copy_pt(n - 1, t - 1, True, pt_1[0])
                if more:
                    masked_maxima(n + AHEAD, t % CI, t % CI == 0)
                if t % BLOCK == PEEL - 1 and not (first and t < BLOCK):
                    divide(*ended(quad, t, BLOCK))

            steps_of(nc.vector, step1, QUADS, BODY)
            divide(*ended(QUADS, 0, BLOCK))
            take_turned(x_t_part, 4)
            dve.wait_ge(hb_ready, 2)
            layer_norm(o_1, g_a, norm_ready, THIRDS,
                       lambda k: add_bank(k, g_a, h_b[:, 2 * k:2 * k + 2], y_mm, NC_ + 2 * k + 2, h_ready, 6 + k + 1))
            take_turned(x_t_part, 4, col["ln2w"], col["ln2b"])

            dve.wait_ge(gate_mm, 1)
            step(nc.vector.tensor_copy(flat(lg[:]), o_bank[0:P, 0:NC_ * E]))
            for ci in range(NC_):
                last = nc.vector.max(m8[:, ci], lg[:, ci])
            step(last)
            nc.vector.tensor_tensor(ediff[:], m8[:, :, 1], m8[:, :, 0], ALU.subtract).then_inc(diff_ready, 1)
            for ci in range(NC_):
                last = nc.vector.max_index(i8[:, ci], m8[:, ci], lg[:, ci])
            step(last)
            step(nc.vector.tensor_copy(i8f[:], i8[:, :, 0:2].rearrange("p c k -> p k c")))
            ex = cst["expert"][0:P].unsqueeze(1).to_broadcast([P, 2 * NC_, E])
            oh12 = oh[:].rearrange("p k c e -> p (k c) e")
            i8f12 = flat(i8f[:])
            nc.vector.tensor_tensor(oh12, ex, i8f12.unsqueeze(2).to_broadcast([P, 2 * NC_, E]),
                                    ALU.is_equal).then_inc(oh_ready, 1)
            dve.wait_ge(rank_mm, 1)
            step(nc.vector.tensor_copy(tot[:], score_bank[1][0:P, 0:96].rearrange("p (b e) -> p e b", e=E)))
            step(nc.vector.tensor_tensor_scan(flat(run[:]), cst["restart"][0:P], flat(tot[:]), 0.0, ALU.mult, ALU.add))
            step(nc.vector.tensor_tensor(run[:], run[:], tot[:], ALU.subtract))
            step(nc.vector.tensor_tensor(rk[:], score_bank[0][0:P, 0:96].rearrange("p (b e) -> p b e", e=E),
                                         run[:].rearrange("p e b -> p b e"), ALU.add))
            step(nc.vector.tensor_tensor(rk[:], rk[:], oh12, ALU.mult))
            step(nc.vector.tensor_reduce(small["rank"][:], rk[:], AX.X, ALU.add))
            nc.vector.tensor_scalar(small["keep"][:], small["rank"][:], float(CAP), None, ALU.is_lt)
            step(nc.vector.scalar_tensor_tensor(small["slot"][:], i8f12, float(CAP), small["rank"][:],
                                                ALU.mult, ALU.add))
            step(nc.vector.tensor_tensor(small["off"][:], small["slot"][:], cst["dump"][0:P], ALU.subtract))
            step(nc.vector.tensor_tensor(small["off"][:], small["off"][:], small["keep"][:], ALU.mult))
            nc.vector.tensor_tensor(scat[:], small["off"][:], cst["dump"][0:P], ALU.add).then_inc(place_ready, 1)
            dve.wait_ge(exp_ready, 1)
            step(nc.vector.tensor_scalar(eden[:], eexp[:], 1.0, None, ALU.add))
            step(nc.vector.reciprocal(small["w"][:, 0:NC_], eden[:]))
            step(nc.vector.tensor_tensor(small["w"][:, NC_:2 * NC_], small["w"][:, 0:NC_], eexp[:], ALU.mult))
            step(nc.vector.tensor_tensor(small["w"][:], small["w"][:], small["keep"][:], ALU.mult))
            for e in range(E):
                p = e % 2
                dve.wait_ge(ld_slot[p], 16 * (e // 2 + 1))
                if e >= 2:
                    dve.wait_ge(st_slot[p], 32 * (e // 2))
                nc.vector.tensor_copy(home[:, p], x_slot[:, p, :, C]).then_inc(home_ready, 1)
                for s in range(2):
                    dve.wait_ge(out_mm, 2 * e + s + 1)
                    nc.vector.tensor_tensor(y_slot[:, e % 2, s], proj_bank[s][0:SH, 0:C],
                                            row["pjb"][0:SH, e * C:(e + 1) * C], ALU.add).then_inc(ys_ready, 1)
            dve.wait_ge(hb_ready, 3)

            def add_choices(b):
                dve.wait_ge(ld_y[b], 32)
                for ci in range(b * CI, (b + 1) * CI):
                    last = nc.vector.scalar_tensor_tensor(h_b[:, ci], y_tok[:, ci], small["w"][:, ci:ci + 1],
                                                          h_b[:, ci], ALU.mult, ALU.add)
                step(last)
                for ci in range(b * CI, (b + 1) * CI):
                    last = nc.vector.scalar_tensor_tensor(h_a[:, ci], y_tok[:, NC_ + ci],
                                                          small["w"][:, NC_ + ci:NC_ + ci + 1], h_b[:, ci],
                                                          ALU.mult, ALU.add)
                step(last)

            dve.wait_ge(fold_mm, 2)
            nc.vector.tensor_tensor(bias_out, o_bank[0:P, 0:C], row["bo1"], ALU.add).then_inc(folded, 1)
            layer_norm(xn, h_a, norm_ready, HALVES, add_choices)
            take_turned(x_t_part, 4)
            for b in range(B):
                n = turned[0] + 1
                dve.wait_ge(turn_mm, n + 1)
                bs = slice(b * T, (b + 1) * T)
                nc.vector.tensor_copy(x_w[:, 3, bs], turn_bank[n % 4][:, 0:T])
                nc.vector.tensor_copy(x_w[0:64, 1, bs], turn_bank[n % 4][64:128, 0:T]).then_inc(turn_dve, 1)
                turned[0] += 2
            for k in range(3):
                dve.wait_ge(v_mm, 3 + k + 1)
                nc.vector.tensor_copy(v_1[:, 2 * k:2 * k + 2],
                                      score_bank[k][0:P, 0:2 * C].rearrange("p (a c) -> p a c", a=2)).then_inc(v_dve, 1)
            for t in range(AHEAD):
                maxima(2 * STEPS + t, t)

            def body2(quad, final):
                for t in range(BODY):
                    n = quad * BODY + (2 * STEPS + t)
                    copy_pt(n, t, False, pt_ready)
                    if t + AHEAD < BODY or not final:
                        maxima(n + AHEAD, t % CI)
                    if t == BLOCK + 1:
                        divide(quad * B + B * QUADS, quad, 0)
                    if t == BODY - 1:
                        divide(quad * B + (B * QUADS + 1), quad, 1)

            with nc.vector.Fori(0, QUADS - 1) as quad:
                body2(quad, False)
            body2(QUADS - 1, True)
            dve.wait_ge(o_ready, 1 + 2 * B * QUADS)

            def add_attention(b):
                cs = slice(b * CI, (b + 1) * CI)
                step(nc.vector.tensor_tensor(h_a[:, cs], h_a[:, cs], o_1[:, cs], ALU.add))

            layer_norm(xn, h_a, norm_ready, HALVES, add_attention)
            take_turned(x_t_part, 4)
            nc.vector.tensor_tensor(h_b[:], h_a[:], row["beta"].unsqueeze(1).to_broadcast([P, NC_, C]),
                                    ALU.add).then_inc(hb_beta, 1)
            roots = []

            def finish(lo, hi, root):
                inverse_std(rstd, root, lo, hi)
                for ci in range(lo, hi):
                    nc.vector.scalar_tensor_tensor(h_b[:, ci], g_a[:, ci], rstd[:, ci:ci + 1], h_b[:, ci],
                                                   ALU.mult, ALU.add).then_inc(out_ready, 1)

            for k, (lo, hi) in enumerate(THIRDS):
                add_bank(k, g_a, bias_out.unsqueeze(1).to_broadcast([P, 2, C]), y_mm, 2 * NC_ + 2 * k + 2,
                         h_ready, 9 + k + 1)
                roots.append(moments(g_a, lo, hi))
                if k == 0:
                    dve.wait_ge(hb_beta, 1)
                dve.wait_ge(var_ready, roots[k])
                for ci in range(lo, hi):
                    last = nc.vector.scalar_tensor_tensor(g_a[:, ci], g_a[:, ci], mv[:, ci, 0:1], row["gamma"],
                                                          ALU.subtract, ALU.mult)
                step(last)
                if k:
                    finish(*THIRDS[k - 1], roots[k - 1])
            finish(*THIRDS[2], roots[2])

        @block.gpsimd
        def _(pool):
            nc.gpsimd.memset(eps[:], EPS).then_inc(eps_set, 1)
            nc.gpsimd.memset(zero[:], 0.0).then_inc(zero_ready, 1)
            nc.gpsimd.memset(q_t, 0.0).then_inc(qt_zero, 1)
            nc.gpsimd.memset(v_q[:], 0.0).then_inc(vq_set, 1)
            pool.wait_ge(vq_set, 1)
            nc.gpsimd.memset(v_q[:, :, :, D1:D1 + 1], 1.0).then_inc(vq_set, 1)
            pool.wait_ge(ld_rows, 16)
            pool.wait_ge(h_ready, 3)
            nc.gpsimd.tensor_tensor(h_b[:], h_a[:], row["bo0"].unsqueeze(1).to_broadcast([P, NC_, C]),
                                    ALU.add).then_inc(hb_ready, 1)

            pool.wait_ge(qt_zero, 1)
            pool.wait_ge(hb_ready, 1)

            def sums(pair):
                for b in range(B):
                    bs = slice(b * T, (b + 1) * T)
                    pool.wait_ge(proj_dve, count0(pair - 1, pieces0.index(("q", b, 1)), "dve"))
                    if not (isinstance(pair, int) and pair == 0):
                        pool.wait_ge(scores_mm, (pair - 1) * BODY0 + (b + 1) * BLOCK0)
                    for p in range(2):
                        rows_p = slice(64 * p, 64 * p + 64)
                        nc.gpsimd.tensor_tensor(q_t[rows_p, p, bs], rope_q[rows_p, 0], rope_q[rows_p, 1],
                                                ALU.add).then_inc(q_sum, 1)
                        pool.wait_ge(q_sum, summed(pair, b, "q") - 1 + p)
                    pool.wait_ge(proj_dve, count0(pair - 1, pieces0.index(("k", b, 1)), "dve"))
                    nc.gpsimd.tensor_tensor(k_t[:, bs], rope_k[:, 0], rope_k[:, 1], ALU.add).then_inc(k_sum, 1)
                    pool.wait_ge(k_sum, summed(pair, b, "k"))

            sums(0)
            with nc.gpsimd.Fori(0, PAIRS - 1) as pair:
                sums(pair + 1)
            pool.wait_ge(g_ready, 1)
            nc.gpsimd.tensor_tensor(h_b[:], g_a[:], row["projb"].unsqueeze(1).to_broadcast([P, NC_, C]),
                                    ALU.add).then_inc(hb_ready, 1)

            def fill_vq(beta, quad, b):
                if beta >= B:
                    pool.wait_ge(block_mm, B * PAIRS + beta - B + 1)
                nc.gpsimd.tensor_copy(
                    v_q[:, b * CI:(b + 1) * CI, :, 0:D1],
                    v_1[:, b * CI:(b + 1) * CI, quad * 64:(quad + 1) * 64].rearrange("p i (j d) -> p i j d", j=4)
                ).then_inc(vq_ready, 1)

            pool.wait_ge(block_mm, B * PAIRS)
            pool.wait_ge(vq_set, 2)
            for quad in range(QUADS):
                for b in range(B):
                    pool.wait_ge(q1_ready, (B if quad == 2 else 0) + b + 1)
                    for j in range(4):
                        if quad:
                            pool.wait_ge(scores_mm, STEPS + (quad - 1) * BODY + b * BLOCK + (j + 1) * CI)
                        rows_of = 4 * (quad > 0) + j
                        nc.gpsimd.tensor_scalar(q_m[:, j, b * T:(b + 1) * T], q_1t[:, quad // 2, b * T:(b + 1) * T],
                                                cst["rows16"][:, rows_of:rows_of + 1], None,
                                                ALU.mult).then_inc(qm_ready, 1)
                    if quad == 0:
                        pool.wait_ge(v_dve, 3)
                    fill_vq(quad * B + b, quad, b)
            pool.wait_ge(norm_ready, 3 * NC_)
            nc.gpsimd.tensor_copy(x_home[:, :, C], cst["home"][0:P]).then_inc(home_set, 1)
            second = x_home[:, NC_:2 * NC_, 0:C]
            nc.gpsimd.tensor_tensor(second, o_1[:], row["ln2w"].unsqueeze(1).to_broadcast([P, NC_, C]),
                                    ALU.mult).then_inc(x_home_pool, 1)
            pool.wait_ge(x_home_pool, 1)
            nc.gpsimd.tensor_tensor(second, second, row["ln2b"].unsqueeze(1).to_broadcast([P, NC_, C]),
                                    ALU.add).then_inc(x_home_pool, 1)
            pool.wait_ge(home_set, 1)
            pool.wait_ge(zeroed, 32)
            pool.wait_ge(place_ready, 1)
            pool.wait_ge(x_home_pool, 2)
            pool.wait_ge(x_home_act, 1)
            for m in range(2 * NC_):
                nc.gpsimd.indirect_dma_start(
                    x_dram, bass.IndirectOffsetOnAxis(ap=scat[:, m:m + 1].bitcast(U32), axis=0), x_home[:, m], None
                ).then_inc(scattered, 16)
            nc.gpsimd.tensor_tensor(h_b[:], h_a[:], g_a[:], ALU.add).then_inc(hb_ready, 1)
            def take_head(h):
                p, j = h % 4 // 2, h % 2
                if h >= 4:
                    pool.wait_ge(proj_mm, MM0 + count2(h // 4 - 1, pieces2.index((2 + p, 2))))
                nc.gpsimd.tensor_copy(qk_2[:, p, :, j * C:(j + 1) * C],
                                      qk_all[:, h].rearrange("p (k n) -> p k n", k=KC)).then_inc(qk_ready, 1)

            pool.wait_ge(qk_act, HEADS)
            for h in range(4):
                take_head(h)
            for e in range(E):
                p = e % 2
                pool.wait_ge(home_ready, e + 1)
                for s in range(2):
                    pool.wait_ge(ys_ready, 2 * e + s + 1)
                    nc.gpsimd.indirect_dma_start(
                        y_dram, bass.IndirectOffsetOnAxis(ap=home[:, p, s:s + 1].bitcast(U32), axis=0),
                        y_slot[:, p, s], None).then_inc(st_slot[p], 16)

            pool.wait_ge(out_mm, 2 * E)
            pool.wait_ge(hb_ready, 3)
            pool.wait_ge(qk_ready, 4)
            nc.gpsimd.memset(x_w[64:128, 1], 0.0).then_inc(xw_zero, 1)
            pool.wait_ge(xw_zero, 1)
            nc.gpsimd.memset(x_w[0:64, 2], 0.0).then_inc(xw_zero, 1)
            pool.wait_ge(xw_zero, 2)
            pool.wait_ge(v_dve, 6)
            for b in range(B):
                fill_vq(QUADS * B + b, 0, b)
            for quad in range(1, QUADS):
                for b in range(B):
                    take_head(4 * quad + 2 * b)
                    take_head(4 * quad + 2 * b + 1)
                    fill_vq((QUADS + quad) * B + b, quad, b)





def rope_tables():
    import numpy as np
    inv = (np.float32(1.0) / np.float32(10000.0) ** (np.arange(0, D0, 2, dtype=np.float32) / np.float32(D0))).astype(np.float32)
    ang = (np.arange(T, dtype=np.float32)[:, None] * inv[None, :]).astype(np.float32)
    cos, sin = np.cos(ang).T, np.sin(ang).T
    cos, sin = np.tile(cos, (4, 1)), np.tile(np.concatenate([-sin, sin], axis=0), (2, 1))
    return np.concatenate([cos, sin], axis=1).astype(np.float32)


def constants():
    import numpy as np
    c = np.zeros((128, CONST_N), np.float32)

    def put(name, v):
        lo, hi = CONST_AT[name]
        c[:v.shape[0], lo:hi] = v

    put("ident", np.eye(128))
    table = rope_tables()
    put("cos_sin_q", table * np.float32(D0 ** -0.5))
    put("cos_sin_k", table)
    t = np.arange(P)
    put("before", (t[:, None] < t[None, :]).astype(np.float32))
    put("rows16", np.arange(128)[:, None] // 16 == np.arange(8)[None, :])
    put("ones", np.ones((P, P)))
    mask = np.zeros((P, T), np.float32)
    mask[:, T - P:] = np.where(t[None, :] > t[:, None], -1e30, 0.0)
    put("mask", mask)
    put("expert", np.tile(np.arange(E), (P, 1)))
    put("dump", SLOTS + np.arange(2 * NC_)[None, :] * P + t[:, None])
    put("home", np.arange(2 * NC_)[None, :] * P + t[:, None])
    put("restart", np.tile((np.arange(E * 2 * NC_) % (2 * NC_) != 0).astype(np.float32), (P, 1)))
    return c


def lay_out(i):
    import numpy as np
    i = {k: np.asarray(v) for k, v in i.items()}
    z = np.zeros

    def chunked(w):
        return w.reshape(KC, FC, -1).transpose(1, 0, 2)

    def token_major(x):
        return x.reshape(B, CI, P, -1).transpose(2, 0, 1, 3).reshape(P, NC_, -1)

    def columns(v):
        return v.reshape(KC, FC).T

    f32 = np.float32
    x = i["x"].reshape(B, 3, 16, 4, 16, 4).transpose(0, 1, 2, 4, 3, 5).reshape(B, 256, PATCH)
    tok_x = z((PATCH + 1, B, T), f32)
    tok_x[:PATCH, :, :256] = x.transpose(2, 0, 1)
    tok_x[PATCH, :, :256] = 1.0
    base = z((B, T, C), f32)
    base[:, :256] = i["L0_tok_pos"][None]
    base[:, 256:] = i["txt"]
    rot = np.concatenate([np.arange(32, 64), np.arange(0, 32)])

    def with_rotated(w):
        w = w.reshape(-1, PAIRS, 2, D0)
        w = np.stack([w, w[..., rot]], axis=2).reshape(-1, 2 * PAIRS, 128)
        return w.transpose(1, 0, 2)

    wq = with_rotated(i["L0_attn_Wq"]).reshape(2 * PAIRS, KC, FC, 128).transpose(0, 2, 1, 3)
    wk = with_rotated(i["L0_attn_Wup"][:, :FF])
    qkv = i["L0_ffn_attn_qkv_w"]
    qkvb = i["L0_ffn_attn_qkv_b"]
    split = 8 * D1
    q_k = np.concatenate([qkv[:, :2 * C], qkvb[None, :2 * C]], axis=0).reshape(C + 1, 2, C)
    wqk1 = np.concatenate([q_k[:, 0, :split], q_k[:, 1, :split], q_k[:, 0, split:], q_k[:, 1, split:]], axis=1)
    wqk1, qkb = wqk1[:C], wqk1[C].reshape(3, 128)
    qkb = np.concatenate([qkb, np.tile(qkb[2, :64], 2)[None]], axis=0)
    cols = z((128, COLS_N), f32)

    def put(name, v):
        lo, hi = COLS_AT[name]
        cols[:v.shape[0], lo:hi] = v

    put("lng", i["L0_attn_ln_g"][:, None])
    put("lnb", i["L0_attn_ln_b"][:, None])
    put("ln1w", columns(i["L0_ffn_ln1_w"]))
    put("ln1b", columns(i["L0_ffn_ln1_b"]))
    put("ln2w", columns(i["L0_ffn_ln2_w"]))
    put("ln2b", columns(i["L0_ffn_ln2_b"]))
    put("qkb", qkb.T)
    put("fb1", i["L1_ffn_b1"][:, None])
    put("fb2", columns(i["L1_ffn_b2"]))
    put("fcb", i["L0_ffn_exp_fc_b"].reshape(E, FK, 128).transpose(2, 0, 1).reshape(128, E * FK))
    rows = np.concatenate([i[k].reshape(-1) for k in (
        "L0_attn_bo", "L0_ffn_attn_proj_b")] + [qkvb[2 * C:]] + [i[k].reshape(-1) for k in (
            "L0_ffn_ln2_w", "L0_ffn_ln2_b", "L1_ffn_bo", "L1_ffn_gamma", "L1_ffn_beta", "L0_ffn_exp_proj_b")])
    empty_rows = z((SLOTS, ROW), f32)
    empty_rows[:, C] = 2 * N + np.arange(SLOTS)
    a = dict(
        empty_rows=empty_rows,
        tok_x=tok_x.reshape(PATCH + 1, N),
        tok_w=np.concatenate([i["L0_tok_W"].T, i["L0_tok_b"][None]], axis=0),
        base=token_major(base),
        const=constants(),
        cols=cols,
        rows=rows,
        wdown=chunked(i["L0_attn_Wdown"]),
        wup_v=i["L0_attn_Wup"][:, FF:],
        wq_h=wq, wk_h=wk,
        wo0=i["L0_attn_Wo"].reshape(FK, 128, C).transpose(1, 0, 2),
        wqk1=chunked(wqk1).reshape(FC, KC, 3, 128),
        w1s=np.concatenate([chunked(qkv[:, 2 * C:]), chunked(i["L0_ffn_attn_proj_w"]), chunked(i["L0_ffn_w_g"])], axis=2),
        fc_w=i["L0_ffn_exp_fc_w"].reshape(E, KC, FC, FF).transpose(0, 2, 1, 3),
        pj_w=i["L0_ffn_exp_proj_w"].reshape(E, FK, 128, C).transpose(0, 2, 1, 3),
        wqk2=np.stack([i["L1_attn_q"], i["L1_attn_k"]], axis=1).reshape(HEADS, 2, KC, FC, C).transpose(0, 3, 1, 2, 4),
        wv2=chunked(i["L1_attn_v"].reshape(C, C).T),
        fw1=chunked(i["L1_ffn_W1"].T),
        fw2=chunked(i["L1_ffn_W2"]),
        fwo=chunked(i["L1_ffn_Wo"].T),
    )
    return {k: np.ascontiguousarray(v) for k, v in a.items()}


def kernel(**inputs):
    import concourse.bacc as _bacc
    from concourse import mybir as _mybir
    from concourse.bass_utils import run_bass_kernel_spmd as _run

    arrays = lay_out(inputs)
    nc = _bacc.Bacc("TRN2", target_bir_lowering=False, num_devices=1)
    aps = {k: nc.dram_tensor("in_" + k, v.shape, _mybir.dt.from_np(v.dtype), kind="ExternalInput").ap() for k, v in arrays.items()}
    out = nc.dram_tensor("out", (B, T, C), F32, kind="ExternalOutput").ap()
    build(nc, aps, out)
    r = _run(nc, [{"in_" + k: v for k, v in arrays.items()}], core_ids=[0])
    return r.results[0]["out"]
```
